# Optimizing a Trainium2 kernel written in Bass

```python
import numpy as np
import jax
import jax.numpy as jnp

def _softmax(x, axis=-1):
    return jax.nn.softmax(x, axis=axis)

def _gelu(x):
    return jax.nn.gelu(x, approximate=True)

def _silu(x):
    return jax.nn.silu(x)

def _sigmoid(x):
    return jax.nn.sigmoid(x)

def _layernorm(x, axis=-1, eps=1e-05):
    m = jnp.mean(x, axis=axis, keepdims=True)
    v = jnp.var(x, axis=axis, keepdims=True)
    return (x - m) / jnp.sqrt(v + eps)

def _scatter_add(tgt, idx, src, axis=0):
    return tgt.at[idx].add(src)

def _segment_sum(src, seg, n):
    return jax.ops.segment_sum(src, seg, n)
kernel_name = 'mk_xattn_seq_d1_seqx_r4_8c71c4'

def setup_inputs(seed: int=0):
    np.random.seed(seed)
    _w = jnp.asarray

    def _rec_inputs():
        import jax
        import jax.numpy as jnp
        _rk = jax.random.key(seed)
        x = -0.0002928 + 1 * jax.random.normal(jax.random.fold_in(_rk, 1), (4, 512, 256), jnp.float32)
        _lenS = 512 - jax.random.randint(jax.random.fold_in(_rk, 7), (4,), 0, max(1, 512 // 4) + 1, jnp.int32)
        _lenS2 = 1024 - jax.random.randint(jax.random.fold_in(_rk, 8), (4,), 0, max(1, 1024 // 4) + 1, jnp.int32)
        _ctx_1024P = jax.random.normal(jax.random.fold_in(_rk, 11), (4, 16, 256), jnp.float32)
        _ctx_1024c = jax.random.dirichlet(jax.random.fold_in(_rk, 511), 0.3 * jnp.ones((16,), jnp.float32), (4, 1024))
        _ctx_1024t = jnp.einsum('bsk,bkd->bsd', _ctx_1024c, _ctx_1024P)
        _ctx_1024t = _ctx_1024t * jax.lax.rsqrt(jnp.mean(jnp.square(_ctx_1024t)) + 1e-12) * 0.953939
        ctx_1024 = -1.39393e-06 + 0.999914 * (_ctx_1024t + 0.3 * jax.random.normal(jax.random.fold_in(_rk, 611), (4, 1024, 256), jnp.float32))
        return (x, ctx_1024)
    x, ctx_1024 = _rec_inputs()

    def _L0_xattn_setup():
        import jax, jax.numpy as jnp
        import numpy as np
        B, S, SE, D, H, FF, E, K = (2, 512, 512, 256, 16, 1024, 8, 2)
        HD = D // H

        def _layernorm(x, g, b):
            m = x.mean(-1, keepdims=True)
            v = ((x - m) ** 2).mean(-1, keepdims=True)
            return (x - m) / jnp.sqrt(v + 1e-05) * g + b

        def _attn(q_in, k_in, v_in, wq, bq, wk, bk, wv, bv, wo, bo, causal):
            Bq, Sq, Dm = q_in.shape
            Sk = k_in.shape[1]
            Q = (q_in @ wq + bq).reshape(Bq, Sq, H, HD)
            Kp = (k_in @ wk + bk).reshape(Bq, Sk, H, HD)
            V = (v_in @ wv + bv).reshape(Bq, Sk, H, HD)
            scores = jnp.einsum('bqhd,bkhd->bhqk', Q, Kp) / jnp.sqrt(jnp.float32(HD))
            if causal:
                mask = jnp.tril(jnp.ones((Sq, Sk), bool))
                scores = jnp.where(mask, scores, -jnp.inf)
            a = jax.nn.softmax(scores, axis=-1)
            o = jnp.einsum('bhqk,bkhd->bqhd', a, V).reshape(Bq, Sq, Dm)
            return o @ wo + bo

        def _moe(x, rw, rb, w1, b1, w2, b2):
            T = x.shape[0] * x.shape[1]
            xf = x.reshape(T, D)
            router_weights = jax.nn.softmax(xf @ rw + rb, axis=-1)
            topw, topi = jax.lax.top_k(router_weights, K)
            topw = jax.nn.softmax(topw, axis=-1)
            combine = jnp.zeros((T, E), xf.dtype).at[jnp.arange(T)[:, None], topi].add(topw)
            h = jax.nn.gelu(jnp.einsum('td,edf->etf', xf, w1) + b1[:, None, :], approximate=False)
            eo = jnp.einsum('etf,efd->etd', h, w2) + b2[:, None, :]
            out = jnp.einsum('etd,te->td', eo, combine)
            return out.reshape(x.shape)
        key = jax.random.key(seed)
        ks = jax.random.split(key, 32)
        w = lambda k, shape: jax.random.normal(k, shape, jnp.float32) * 0.02
        inp = {'x': jax.random.normal(ks[0], (B, S, D), jnp.float32), 'encoder_output': jax.random.normal(ks[1], (B, SE, D), jnp.float32), 'sa_wq': w(ks[2], (D, D)), 'sa_bq': jnp.zeros((D,), jnp.float32), 'sa_wk': w(ks[3], (D, D)), 'sa_bk': jnp.zeros((D,), jnp.float32), 'sa_wv': w(ks[4], (D, D)), 'sa_bv': jnp.zeros((D,), jnp.float32), 'sa_wo': w(ks[5], (D, D)), 'sa_bo': jnp.zeros((D,), jnp.float32), 'ca_wq': w(ks[6], (D, D)), 'ca_bq': jnp.zeros((D,), jnp.float32), 'ca_wk': w(ks[7], (D, D)), 'ca_bk': jnp.zeros((D,), jnp.float32), 'ca_wv': w(ks[8], (D, D)), 'ca_bv': jnp.zeros((D,), jnp.float32), 'ca_wo': w(ks[9], (D, D)), 'ca_bo': jnp.zeros((D,), jnp.float32), 'ln1_g': jnp.ones((D,), jnp.float32), 'ln1_b': jnp.zeros((D,), jnp.float32), 'ln2_g': jnp.ones((D,), jnp.float32), 'ln2_b': jnp.zeros((D,), jnp.float32), 'ln3_g': jnp.ones((D,), jnp.float32), 'ln3_b': jnp.zeros((D,), jnp.float32), 'router_w': w(ks[10], (D, E)), 'router_b': jnp.zeros((E,), jnp.float32), 'e_w1': w(ks[11], (E, D, FF)), 'e_b1': jnp.zeros((E, FF), jnp.float32), 'e_w2': w(ks[12], (E, FF, D)), 'e_b2': jnp.zeros((E, D), jnp.float32)}
        return inp
    _L0_xattn_all = _L0_xattn_setup()
    _L0_xattn_in = {k: v for k, v in _L0_xattn_all.items() if k in ('sa_wq', 'sa_bq', 'sa_wk', 'sa_bk', 'sa_wv', 'sa_bv', 'sa_wo', 'sa_bo', 'ca_wq', 'ca_bq', 'ca_wk', 'ca_bk', 'ca_wv', 'ca_bv', 'ca_wo', 'ca_bo', 'ln1_g', 'ln1_b', 'ln2_g', 'ln2_b', 'ln3_g', 'ln3_b', 'router_w', 'router_b', 'e_w1', 'e_b1', 'e_w2', 'e_b2')}
    del _L0_xattn_all
    return {'x': x, 'ctx_1024': ctx_1024, 'L0_xattn_sa_wq': _L0_xattn_in['sa_wq'], 'L0_xattn_sa_bq': _L0_xattn_in['sa_bq'], 'L0_xattn_sa_wk': _L0_xattn_in['sa_wk'], 'L0_xattn_sa_bk': _L0_xattn_in['sa_bk'], 'L0_xattn_sa_wv': _L0_xattn_in['sa_wv'], 'L0_xattn_sa_bv': _L0_xattn_in['sa_bv'], 'L0_xattn_sa_wo': _L0_xattn_in['sa_wo'], 'L0_xattn_sa_bo': _L0_xattn_in['sa_bo'], 'L0_xattn_ca_wq': _L0_xattn_in['ca_wq'], 'L0_xattn_ca_bq': _L0_xattn_in['ca_bq'], 'L0_xattn_ca_wk': _L0_xattn_in['ca_wk'], 'L0_xattn_ca_bk': _L0_xattn_in['ca_bk'], 'L0_xattn_ca_wv': _L0_xattn_in['ca_wv'], 'L0_xattn_ca_bv': _L0_xattn_in['ca_bv'], 'L0_xattn_ca_wo': _L0_xattn_in['ca_wo'], 'L0_xattn_ca_bo': _L0_xattn_in['ca_bo'], 'L0_xattn_ln1_g': _L0_xattn_in['ln1_g'], 'L0_xattn_ln1_b': _L0_xattn_in['ln1_b'], 'L0_xattn_ln2_g': _L0_xattn_in['ln2_g'], 'L0_xattn_ln2_b': _L0_xattn_in['ln2_b'], 'L0_xattn_ln3_g': _L0_xattn_in['ln3_g'], 'L0_xattn_ln3_b': _L0_xattn_in['ln3_b'], 'L0_xattn_router_w': _L0_xattn_in['router_w'], 'L0_xattn_router_b': _L0_xattn_in['router_b'], 'L0_xattn_e_w1': _L0_xattn_in['e_w1'], 'L0_xattn_e_b1': _L0_xattn_in['e_b1'], 'L0_xattn_e_w2': _L0_xattn_in['e_w2'], 'L0_xattn_e_b2': _L0_xattn_in['e_b2']}

def reference(x, ctx_1024, L0_xattn_sa_wq, L0_xattn_sa_bq, L0_xattn_sa_wk, L0_xattn_sa_bk, L0_xattn_sa_wv, L0_xattn_sa_bv, L0_xattn_sa_wo, L0_xattn_sa_bo, L0_xattn_ca_wq, L0_xattn_ca_bq, L0_xattn_ca_wk, L0_xattn_ca_bk, L0_xattn_ca_wv, L0_xattn_ca_bv, L0_xattn_ca_wo, L0_xattn_ca_bo, L0_xattn_ln1_g, L0_xattn_ln1_b, L0_xattn_ln2_g, L0_xattn_ln2_b, L0_xattn_ln3_g, L0_xattn_ln3_b, L0_xattn_router_w, L0_xattn_router_b, L0_xattn_e_w1, L0_xattn_e_b1, L0_xattn_e_w2, L0_xattn_e_b2):
    import jax
    import jax.numpy as jnp

    def _L0_xattn_ref(x, encoder_output, sa_wq, sa_bq, sa_wk, sa_bk, sa_wv, sa_bv, sa_wo, sa_bo, ca_wq, ca_bq, ca_wk, ca_bk, ca_wv, ca_bv, ca_wo, ca_bo, ln1_g, ln1_b, ln2_g, ln2_b, ln3_g, ln3_b, router_w, router_b, e_w1, e_b1, e_w2, e_b2):
        import jax, jax.numpy as jnp
        import numpy as np
        B, S, SE, D, H, FF, E, K = (2, 512, 512, 256, 16, 1024, 8, 2)
        HD = D // H

        def _layernorm(x, g, b):
            m = x.mean(-1, keepdims=True)
            v = ((x - m) ** 2).mean(-1, keepdims=True)
            return (x - m) / jnp.sqrt(v + 1e-05) * g + b

        def _attn(q_in, k_in, v_in, wq, bq, wk, bk, wv, bv, wo, bo, causal):
            Bq, Sq, Dm = q_in.shape
            Sk = k_in.shape[1]
            Q = (q_in @ wq + bq).reshape(Bq, Sq, H, HD)
            Kp = (k_in @ wk + bk).reshape(Bq, Sk, H, HD)
            V = (v_in @ wv + bv).reshape(Bq, Sk, H, HD)
            scores = jnp.einsum('bqhd,bkhd->bhqk', Q, Kp) / jnp.sqrt(jnp.float32(HD))
            if causal:
                mask = jnp.tril(jnp.ones((Sq, Sk), bool))
                scores = jnp.where(mask, scores, -jnp.inf)
            a = jax.nn.softmax(scores, axis=-1)
            o = jnp.einsum('bhqk,bkhd->bqhd', a, V).reshape(Bq, Sq, Dm)
            return o @ wo + bo

        def _moe(x, rw, rb, w1, b1, w2, b2):
            T = x.shape[0] * x.shape[1]
            xf = x.reshape(T, D)
            router_weights = jax.nn.softmax(xf @ rw + rb, axis=-1)
            topw, topi = jax.lax.top_k(router_weights, K)
            topw = jax.nn.softmax(topw, axis=-1)
            combine = jnp.zeros((T, E), xf.dtype).at[jnp.arange(T)[:, None], topi].add(topw)
            h = jax.nn.gelu(jnp.einsum('td,edf->etf', xf, w1) + b1[:, None, :], approximate=False)
            eo = jnp.einsum('etf,efd->etd', h, w2) + b2[:, None, :]
            out = jnp.einsum('etd,te->td', eo, combine)
            return out.reshape(x.shape)
        x = _layernorm(x + _attn(x, x, x, sa_wq, sa_bq, sa_wk, sa_bk, sa_wv, sa_bv, sa_wo, sa_bo, True), ln1_g, ln1_b)
        x = _layernorm(x + _attn(x, encoder_output, encoder_output, ca_wq, ca_bq, ca_wk, ca_bk, ca_wv, ca_bv, ca_wo, ca_bo, False), ln2_g, ln2_b)
        x = _layernorm(x + _moe(x, router_w, router_b, e_w1, e_b1, e_w2, e_b2), ln3_g, ln3_b)
        return x
    x = _L0_xattn_ref(x, ctx_1024, L0_xattn_sa_wq, L0_xattn_sa_bq, L0_xattn_sa_wk, L0_xattn_sa_bk, L0_xattn_sa_wv, L0_xattn_sa_bv, L0_xattn_sa_wo, L0_xattn_sa_bo, L0_xattn_ca_wq, L0_xattn_ca_bq, L0_xattn_ca_wk, L0_xattn_ca_bk, L0_xattn_ca_wv, L0_xattn_ca_bv, L0_xattn_ca_wo, L0_xattn_ca_bo, L0_xattn_ln1_g, L0_xattn_ln1_b, L0_xattn_ln2_g, L0_xattn_ln2_b, L0_xattn_ln3_g, L0_xattn_ln3_b, L0_xattn_router_w, L0_xattn_router_b, L0_xattn_e_w1, L0_xattn_e_b1, L0_xattn_e_w2, L0_xattn_e_b2)
    return x

_drawn_inputs = setup_inputs


def setup_inputs(seed=0):
    import zlib

    import numpy as np

    out = dict(_drawn_inputs(seed))
    spreads = {'L0_xattn_sa_bq': (0.0, 0.8),
     'L0_xattn_sa_bk': (0.0, 0.8),
     'L0_xattn_sa_bv': (0.0, 0.1),
     'L0_xattn_sa_bo': (0.0, 0.1),
     'L0_xattn_ca_bq': (0.0, 0.8),
     'L0_xattn_ca_bk': (0.0, 0.8),
     'L0_xattn_ca_bv': (0.0, 0.1),
     'L0_xattn_ca_bo': (0.0, 0.1),
     'L0_xattn_ln1_g': (1.0, 0.2),
     'L0_xattn_ln1_b': (0.0, 0.1),
     'L0_xattn_ln2_g': (1.0, 0.2),
     'L0_xattn_ln2_b': (0.0, 0.1),
     'L0_xattn_ln3_g': (1.0, 0.2),
     'L0_xattn_ln3_b': (0.0, 0.1),
     'L0_xattn_router_b': (0.0, 0.1),
     'L0_xattn_e_b1': (0.0, 0.34),
     'L0_xattn_e_b2': (0.0, 0.1)}
    factors = {'L0_xattn_sa_wq': 8.0,
     'L0_xattn_sa_wk': 8.0,
     'L0_xattn_sa_wv': 4.033,
     'L0_xattn_ca_wq': 8.0,
     'L0_xattn_ca_wk': 8.0}
    for name, (base, spread) in spreads.items():
        noise = np.random.default_rng([zlib.crc32(name.encode()), seed]).standard_normal(out[name].shape)
        drawn = base * np.exp(spread * noise) if base else spread * noise
        out[name] = jnp.asarray(drawn.astype(out[name].dtype))
    for name, factor in factors.items():
        out[name] = (out[name] * factor).astype(out[name].dtype)
    return out
```

```python
import concourse.bass as bass
from concourse import mybir
from contextlib import ExitStack

F32 = mybir.dt.float32
BF16 = mybir.dt.bfloat16
I32 = mybir.dt.int32
U32 = mybir.dt.uint32
ACT = mybir.ActivationFunctionType
ALU = mybir.AluOpType
X = mybir.AxisListType.X

P = 128
B, S, SE, D = 4, 512, 1024, 256
H, HD = 16, 16
E, FF = 8, 1024
DC, FC = D // P, FF // P
QT, ET = S // P, SE // P
TT = B * QT
TOK = B * S
G = 4
UNITS = H // G
EPS = 1e-5
NEG = -1e30
SCALE = HD ** -0.5
PARTS = 3
Q_PART = [0, 0, 0, 1, 1, 2]
K_PART = [0, 1, 2, 0, 1, 0]
NG = len(Q_PART)
KR = NG * HD
KM = KR + PARTS
SLOT_TILES = TOK * 2 // P + E
RING = 3
V_JOBS = 8 + UNITS * 17 + 6 + 2 + UNITS * 33 + 6 + 1
V_CROSS = 8 + UNITS * 17 + 6 + 2
V_PER = -(-V_JOBS // RING) * RING
A_JOBS = 2 + 4 + UNITS * 16 + UNITS * 32 + 8
A_PER = -(-A_JOBS // RING) * RING
SPLITS = 10


ROUTE_TAKEN = 2 * TT + 3 + 2 + 2 + 1


class Count:

    def __init__(self, per, credit=0):
        self.per, self.n = per, credit

    def at(self, b, k=0):
        return b * self.per + (self.n + k)

    def next(self, k=1):
        self.n += k

    def end(self, batches):
        self.n += (batches - 1) * self.per


def cross_tiles():
    return [(j, q, h) for j in range(G) for q in range(QT) for h in range(2)]


def self_tiles():
    return [(j, q, 0) for j in range(G) for q in range(QT)]


def decoder_layer(nc, a, out):
    ctx = ExitStack()
    with ctx:
        def sb(name, shape, dt=F32):
            return ctx.enter_context(nc.sbuf_tensor(name, shape, dt))

        def sem(name):
            return ctx.enter_context(nc.semaphore(name))

        parts_dram = nc.dram_tensor("parts_scratch", (SPLITS, PARTS, P, S), BF16).ap()
        max_dram = nc.dram_tensor("max_scratch", (2, PARTS, G * S), BF16).ap()
        slots_dram = nc.dram_tensor("slots_in", ((SLOT_TILES + 1) * P, D), F32).ap()
        y_dram = nc.dram_tensor("slots_out", (SLOT_TILES * P, D), F32).ap()

        x2_all = sb("x2_all", [P, TT, D])
        logits = sb("logits", [P, TT, E])
        ident = sb("ident", [P, P])
        ident_b = sb("ident_b", [P, P], BF16)
        ln_gb = sb("ln_gb", [P, 6, D])
        stats = sb("stats", [P, QT, 6])
        mv = sb("mv", [P, QT, 2])
        rstd = sb("rstd", [P, QT])
        neg_half = sb("neg_half", [P, QT])
        router_b = sb("router_b", [P, E])
        y = sb("y", [P, QT, D])

        v_bank = [ctx.enter_context(nc.psum_tensor(f"v_bank{i}", [P, 512], F32)) for i in range(RING)]
        a_bank = [ctx.enter_context(nc.psum_tensor(f"a_bank{i}", [P, 512], F32)) for i in range(RING)]
        o_bank = [ctx.enter_context(nc.psum_tensor(f"o_bank{i}", [P, 512], F32)) for i in range(2)]

        const_in = sem("const_in")
        const_made = sem("const_made")
        const_cast = sem("const_cast")
        slots_zeroed = sem("slots_zeroed")
        xt_in, ctx_in, x_in = sem("xt_in"), sem("ctx_in"), sem("x_in")
        v_full, v_free = sem("v_full"), sem("v_free")
        a_full, a_free = sem("a_full"), sem("a_free")
        high_done = sem("high_done")
        split_done = sem("split_done")
        part_out = [sem("part_out0"), sem("part_out1")]
        stack_in = [sem(f"stack_in{s}") for s in range(SPLITS)]
        maxp_ready = sem("maxp_ready")
        maxt_out = sem("maxt_out")
        max_in = [sem("max_in0"), sem("max_in1")]
        pv_done = sem("pv_done")
        o_out = sem("o_out")
        mean_ready, rstd_ready = sem("mean_ready"), sem("rstd_ready")
        y_ready = sem("y_ready")
        dve_step = sem("dve_step")
        pool_step = sem("pool_step")
        passed = sem("passed")

        att_ctx = ExitStack()

        def sba(name, shape, dt=F32):
            return att_ctx.enter_context(nc.sbuf_tensor(name, shape, dt))

        w = {n: sba("w_" + n, [P, DC, D]) for n in ("sa_wq", "sa_wk", "sa_wv", "sa_wo", "ca_wq", "ca_wk", "ca_wv", "ca_wo")}
        router_w = sba("w_router", [P, DC, E])
        bias = {n: sba("b_" + n, [P, DC]) for n in ("sa_bq", "sa_bk", "sa_bv", "ca_bq", "ca_bk", "ca_bv")}
        out_b = sba("out_b", [P, 2, D])
        mask_q = sba("mask_q", [P, P], BF16)
        mask_k = sba("mask_k", [P, P], BF16)
        xt = sba("xt", [P, DC, S])
        ctxt = sba("ctxt", [P, DC, SE])
        xres = sba("xres", [P, QT, D])
        parts = [sba(f"parts{i}", [P, PARTS, S], BF16) for i in range(2)]
        rest = [sba(f"rest{i}", [P, S]) for i in range(2)]
        q_stack = sba("q_stack", [P, H, S], BF16)
        k_stack = [sba("k_stack_self", [P, H, S], BF16), sba("k_stack_cross", [P, H, SE], BF16)]
        v_ext = [sba("v_self", [P, QT, H, 2 * HD]), sba("v_cross", [P, ET, H, 2 * HD])]
        probs = [sba(f"probs{i}", [P, G, S]) for i in range(2)]
        o_sb = sba("o_sb", [P, UNITS, S])
        o_t = sba("o_t", [P, DC, S])
        max_raw = sba("max_raw", [P, G * QT, 2])
        max_q = sba("max_q", [P, G * QT])
        max_r = sba("max_r", [P, G * QT])
        max_p = sba("max_p", [P, PARTS, G * QT], BF16)
        max_t = sba("max_t", [PARTS * G * QT, P], BF16)
        recip = sba("recip", [P, H])

        n_const = [0]

        blocks = ExitStack()
        block = blocks.enter_context(nc.Block())
        xt_d = a["xT"].rearrange("(c p) t -> p c t", p=P)
        ctx_d = a["ctxT"].rearrange("(c p) t -> p c t", p=P)
        x_d = a["x"].rearrange("(t p) d -> p t d", p=P)
        slot_view = slots_dram.rearrange("(n p) d -> p n d", p=P)
        N_LOADS = 8 + 1 + 6 + 2 + 6 + 1

        def split_target(s):
            if s in (0, 1, 8, 9):
                return q_stack, 8 * (s % 2), 0, Q_PART
            if s in (2, 3):
                return k_stack[0], 8 * (s % 2), 0, K_PART
            return k_stack[1], 8 * ((s - 4) // 2), S * (s % 2), K_PART

        @block.sync
        def _(sp):
            for n in ("sa_wq", "sa_wk", "sa_wv", "ca_wk", "ca_wv", "sa_wo", "ca_wq", "ca_wo"):
                sp.dma_start(w[n][:, :, :], a[n].rearrange("(c p) n -> p c n", p=P)).then_inc(const_in, 16)
            sp.dma_start(router_w[:, :, :], a["router_w"].rearrange("(c p) n -> p c n", p=P)).then_inc(const_in, 16)
            with nc.allow_non_contiguous_dma(reason="six columns of 256 numbers"):
                for n, t in bias.items():
                    sp.dma_start(t[:, :], a[n].rearrange("(c p) -> p c", p=P)).then_inc(const_in, 16)
            for i, n in enumerate(("sa_bo", "ca_bo")):
                sp.dma_start(out_b[:, i, :], a[n].rearrange("(o n) -> o n", o=1).to_broadcast([P, D])).then_inc(const_in, 16)
            for i, n in enumerate(("ln1_g", "ln1_b", "ln2_g", "ln2_b", "ln3_g", "ln3_b")):
                sp.dma_start(ln_gb[:, i, :], a[n].rearrange("(o n) -> o n", o=1).to_broadcast([P, D])).then_inc(const_in, 16)
            sp.dma_start(router_b[:, :], a["router_b"].rearrange("(o n) -> o n", o=1).to_broadcast([P, E])).then_inc(const_in, 16)
            sp.wait_ge(const_made, 1)
            sp.dma_start(y_dram[(SLOT_TILES - E) * P:, :].rearrange("(n p) d -> p n d", p=P),
                         y[:, 0:1, :].to_broadcast([P, E, D])).then_inc(slots_zeroed, 16)
            sp.dma_start(slot_view, y[:, 0:1, :].to_broadcast([P, SLOT_TILES + 1, D])).then_inc(slots_zeroed, 16)

            for i in range(2):
                sp.sem_inc(part_out[i], 16)
                sp.sem_inc(max_in[i], 16)
            sp.sem_inc(maxt_out, 16)
            split = Count(SPLITS)
            vring = Count(V_PER)

            def store_and_stack(b, s):
                sp.wait_ge(split_done, split.at(b, s + 1))
                sp.dma_start(parts_dram[s].rearrange("j p t -> p j t"), parts[s % 2][:, :, :]).then_inc(part_out[s % 2], 16)
                sp.wait_ge(part_out[s % 2], b * (16 * SPLITS // 2) + 16 * (s // 2 + 2))
                stack, h0, t0, which = split_target(s)
                for g in range(NG):
                    sp.dma_start(stack[HD * g:HD * (g + 1), h0:h0 + 8, t0:t0 + S],
                                 parts_dram[s, which[g]].rearrange("(h r) t -> r h t", r=HD)).then_inc(stack_in[s], 16)

            def max_rows(b, u):
                i = u % 2
                sp.wait_ge(v_free, vring.at(b, RING + (8 + 17 * (u + 1) if u < UNITS else V_CROSS + 33 * (u - UNITS + 1))))
                sp.dma_start(max_dram[i].rearrange("j (c t) -> (j c) t", t=P), max_t[:, :]).then_inc(maxt_out, 16)
                sp.wait_ge(maxt_out, b * (16 * 2 * UNITS) + 16 * (u + 2))
                h0 = G * (u % UNITS)
                sp.dma_start(q_stack[KR:KM, h0:h0 + G, :].rearrange("p h t -> p (h t)"), max_dram[i]).then_inc(max_in[i], 16)

            with sp.Fori(0, B) as b:
                for s in range(8):
                    store_and_stack(b, s)
                for u in range(UNITS):
                    max_rows(b, u)
                for s in range(8, 10):
                    store_and_stack(b, s)
                for u in range(UNITS, 2 * UNITS):
                    max_rows(b, u)

        @block.gpsimd
        def _(pool):
            nc.gpsimd.memset(y[:, 0, :], 0.0).then_inc(const_made, 1)
            nc.gpsimd.memset(neg_half[:, :], -0.5).then_inc(const_made, 1)
            nc.gpsimd.memset(ident[:, :], 0.0).then_inc(const_made, 1)
            nc.gpsimd.memset(mask_q[:, :], 0.0).then_inc(const_made, 1)
            nc.gpsimd.memset(mask_k[:, :], 0.0).then_inc(const_made, 1)
            pool.wait_ge(const_made, 5)
            nc.gpsimd.affine_select(out=ident[:, :], in_=ident[:, :], compare_op=ALU.not_equal, fill=1.0, base=0,
                                    pattern=[[-1, P]], channel_multiplier=1).then_inc(const_made, 1)
            nc.gpsimd.affine_select(out=mask_q[:, :], in_=mask_q[:, :], compare_op=ALU.is_ge, fill=NEG, base=0,
                                    pattern=[[-1, P]], channel_multiplier=1).then_inc(const_made, 1)
            nc.gpsimd.affine_select(out=mask_k[:, :], in_=mask_k[:, :], compare_op=ALU.is_ge, fill=NEG, base=0,
                                    pattern=[[1, P]], channel_multiplier=-1).then_inc(const_made, 1)

            step = Count(2)
            mean = Count(2)
            afull = Count(A_PER)

            def load(b):
                cols = bass.ds(b * S, S)
                pool.dma_start(xt[:, :, :], xt_d[:, :, cols]).then_inc(xt_in, 16)
                pool.dma_start(ctxt[:, :, :], ctx_d[:, :, bass.ds(b * SE, SE)]).then_inc(ctx_in, 16)

            def load_residual(b):
                pool.dma_start(xres[:, :, :], x_d[:, bass.ds(b * QT, QT), :]).then_inc(x_in, 16)

            def inverse_root(b, k):
                pool.wait_ge(mean_ready, mean.at(b, k + 1))
                pool.sem_inc(passed, 1)
                nc.gpsimd.tensor_scalar(rstd[:, :], mv[:, :, 1], EPS, None, ALU.add).then_inc(pool_step, 1)
                pool.wait_ge(pool_step, step.at(b, k + 1))
                nc.gpsimd.tensor_tensor(rstd[:, :], rstd[:, :], neg_half[:, :], ALU.pow).then_inc(rstd_ready, 1)

            load(0)
            load_residual(0)
            with pool.Fori(0, B - 1) as b:
                pool.wait_ge(a_full, afull.at(b, 6))
                load(b + 1)
                inverse_root(b, 0)
                inverse_root(b, 1)
                load_residual(b + 1)
            for k in range(2):
                inverse_root(B - 1, k)

        @block.tensor
        def _(pe):
            pe.wait_ge(const_in, 16 * N_LOADS)
            pe.wait_ge(const_made, 8)
            pe.wait_ge(const_cast, 8)
            pe.sem_inc(pv_done, 2)
            v = Count(V_PER)
            act = Count(A_PER)
            pv = Count(12 * UNITS)
            maxp = Count(2 * UNITS)

            def v_next(b):
                pe.wait_ge(v_free, v.at(b, 1))
                bank = v_bank[v.n % RING]
                v.next()
                return bank

            def a_next(b):
                pe.wait_ge(a_free, act.at(b, 1))
                bank = a_bank[act.n % RING]
                act.next()
                return bank

            def project(b, wname, src, t0, c):
                bank = v_next(b)
                for k in range(DC):
                    last = nc.tensor.matmul(bank[:, :], w[wname][:, k, c * P:(c + 1) * P], src[:, k, t0:t0 + S],
                                            start=(k == 0), stop=(k == DC - 1))
                last.then_inc(v_full, 1)

            def project_values(b, wname, src, pair):
                bank = a_next(b)
                for i in range(2):
                    t = 2 * pair + i
                    for k in range(DC):
                        last = nc.tensor.matmul(bank[:, i * D:(i + 1) * D], src[:, k, t * P:(t + 1) * P], w[wname][:, k, :],
                                                start=(k == 0), stop=(k == DC - 1))
                last.then_inc(a_full, 1)

            def max_tile(b, kind, u, tile):
                j, q, half = tile
                h = G * u + j
                bank = v_next(b)
                lhs = q_stack[0:KR, h, q * P:(q + 1) * P]
                if kind == 0:
                    n = (q + 1) * P
                    nc.tensor.matmul(bank[:, 0:n], lhs, k_stack[0][0:KR, h, 0:n], start=True, stop=False)
                    nc.tensor.matmul(bank[:, n - P:n], ident_b[:, :], mask_q[:, :], start=False, stop=True).then_inc(v_full, 1)
                else:
                    nc.tensor.matmul(bank[:, :], lhs, k_stack[1][0:KR, h, half * S:(half + 1) * S],
                                     start=True, stop=True).then_inc(v_full, 1)

            def max_transpose(b, kind, u):
                bank = v_next(b)
                pe.wait_ge(maxp_ready, maxp.at(b, UNITS * kind + u + 1))
                pe.sem_inc(passed, 1)
                nc.tensor.transpose(bank[0:PARTS * G * QT, 0:P // 2].bitcast(BF16), max_p[:, :, :].rearrange("p j c -> p (j c)"),
                                    ident_b[:, :]).then_inc(v_full, 1)

            def score_tile(b, kind, u, kt, j):
                h = G * u + j
                bank = a_next(b)
                lhs = k_stack[kind][0:KM, h, kt * P:(kt + 1) * P]
                if kind == 0:
                    q0 = kt * P
                    nc.tensor.matmul(bank[:, q0:S], lhs, q_stack[0:KM, h, q0:S], start=True, stop=False)
                    nc.tensor.matmul(bank[:, q0:q0 + P], ident_b[:, :], mask_k[:, :], start=False, stop=True).then_inc(a_full, 1)
                else:
                    nc.tensor.matmul(bank[:, :], lhs, q_stack[0:KM, h, :], start=True, stop=True).then_inc(a_full, 1)

            def values(b, kind, u, kt, kts, done):
                o = o_bank[u % 2]
                q0 = kt * P if kind == 0 else 0
                pe.wait_ge(a_free, done)
                for j in range(G):
                    last = nc.tensor.matmul(o[32 * j:32 * (j + 1), q0:S], v_ext[kind][:, kt, G * u + j, :], probs[kt % 2][:, j, q0:S],
                                            start=(kt == 0), stop=(kt == kts - 1))
                last.then_inc(pv_done, 1)

            def attention(b, kind):
                tiles = cross_tiles() if kind else self_tiles()
                kts = ET if kind else QT
                for t in tiles:
                    max_tile(b, kind, 0, t)
                if kind == 0:
                    for pair in range(ET // 2):
                        project_values(b, "ca_wv", ctxt, pair)
                max_transpose(b, kind, 0)
                for u in range(UNITS):
                    n_u = UNITS * kind + u
                    pe.wait_ge(max_in[n_u % 2], b * (16 * UNITS) + 16 * (n_u // 2 + 2))
                    pe.wait_ge(o_out, b * (2 * UNITS) + n_u + 1)
                    nxt = list(tiles) if u + 1 < UNITS else []
                    done = None
                    for kt in range(kts):
                        for j in range(G):
                            score_tile(b, kind, u, kt, j)
                            if nxt:
                                max_tile(b, kind, u + 1, nxt.pop(0))
                            if j == 1 and kt:
                                values(b, kind, u, kt - 1, kts, done)
                        done = act.at(b, RING)
                    if u + 1 < UNITS:
                        max_transpose(b, kind, u + 1)
                    values(b, kind, u, kts - 1, kts, done)

            def finish(b, kind):
                pe.wait_ge(o_out, b * (2 * UNITS) + UNITS * (kind + 1) + 2)
                for q in range(QT):
                    bank = v_next(b)
                    for g in range(UNITS):
                        last = nc.tensor.transpose(bank[:, g * P:(g + 1) * P], o_sb[:, g, q * P:(q + 1) * P], ident[:, :])
                    last.then_inc(v_full, 1)
                pe.wait_ge(v_free, v.at(b, RING))
                transpose_y(b)
                pe.wait_ge(a_free, act.at(b, RING))
                for pair in range(QT // 2):
                    bank = v_next(b)
                    for i in range(2):
                        t = 2 * pair + i
                        for k in range(DC):
                            last = nc.tensor.matmul(bank[:, i * D:(i + 1) * D], o_t[:, k, t * P:(t + 1) * P],
                                                    w["ca_wo" if kind else "sa_wo"][:, k, :], start=(k == 0), stop=(k == DC - 1))
                    last.then_inc(v_full, 1)
                pe.wait_ge(y_ready, b * 2 + kind + 1)
                transpose_y(b)
                pe.wait_ge(a_free, act.at(b, RING))

            def transpose_y(b):
                for c in range(DC):
                    bank = a_next(b)
                    for q in range(QT):
                        last = nc.tensor.transpose(bank[:, q * P:(q + 1) * P], y[:, q, c * P:(c + 1) * P], ident[:, :])
                    last.then_inc(a_full, 1 + (A_PER - A_JOBS if act.n == A_JOBS else 0))

            with pe.Fori(0, B) as b:
                pe.wait_ge(xt_in, b * 16 + 16)
                for c in range(DC):
                    project(b, "sa_wq", xt, 0, c)
                for c in range(DC):
                    project(b, "sa_wk", xt, 0, c)
                for pair in range(QT // 2):
                    project_values(b, "sa_wv", xt, pair)
                pe.wait_ge(ctx_in, b * 16 + 16)
                for c in range(DC):
                    for half in range(2):
                        project(b, "ca_wk", ctxt, half * S, c)
                for s in range(4):
                    pe.wait_ge(stack_in[s], b * (16 * NG) + 16 * NG)
                attention(b, 0)
                finish(b, 0)
                for c in range(DC):
                    project(b, "ca_wq", o_t, 0, c)
                for s in range(4, 10):
                    pe.wait_ge(stack_in[s], b * (16 * NG) + 16 * NG)
                attention(b, 1)
                finish(b, 1)
                bank = v_next(b)
                for q in range(QT):
                    for k in range(DC):
                        last = nc.tensor.matmul(bank[:, q * E:(q + 1) * E], o_t[:, k, q * P:(q + 1) * P], router_w[:, k, :],
                                                start=(k == 0), stop=(k == DC - 1))
                last.then_inc(v_full, 1 + V_PER - V_JOBS)
                assert v.n == V_JOBS and act.n == A_JOBS

        @block.scalar
        def _(sc):
            sc.wait_ge(const_in, 16 * N_LOADS)
            sc.sem_inc(a_free, RING)
            sc.sem_inc(o_out, 2)
            v = Count(V_PER)
            act = Count(A_PER)
            pv = Count(12 * UNITS)

            def a_job(b):
                bank = a_bank[act.n % RING]
                act.next()
                sc.wait_ge(a_full, act.at(b))
                return bank

            def high_part(b, s, vjob, bname, c):
                sc.wait_ge(part_out[s % 2], b * (16 * SPLITS // 2) + 16 * (s // 2 + 1))
                sc.wait_ge(v_full, b * V_PER + vjob + 1)
                nc.scalar.activation(parts[s % 2][:, 0, :], v_bank[vjob % RING][:, :], ACT.Identity,
                                     bias=bias[bname][:, c:c + 1]).then_inc(high_done, 1)

            def store_values(b, kind, pair):
                bank = a_job(b)
                nc.scalar.activation(v_ext[kind][:, 2 * pair:2 * pair + 2, :, 0:HD],
                                     bank[:, :].rearrange("p (t h d) -> p t h d", t=2, d=HD), ACT.Identity).then_inc(a_free, 1)

            def exponentials(b, kind):
                kts = ET if kind else QT
                for u in range(UNITS):
                    for kt in range(kts):
                        q0 = 0 if kind else kt * P
                        sc.wait_ge(pv_done, pv.at(b, 1))
                        pv.next()
                        for j in range(G):
                            bank = a_job(b)
                            nc.scalar.activation(probs[kt % 2][:, j, q0:S], bank[:, q0:S], ACT.Exp, scale=SCALE).then_inc(a_free, 1)
                    sc.wait_ge(pv_done, pv.at(b, 2))
                    nc.scalar.activation(o_sb[:, u, :], o_bank[u % 2][:, :], ACT.Identity).then_inc(o_out, 1)

            def to_o_t(b, bname=None):
                for c in range(DC):
                    bank = a_job(b)
                    kw = {"bias": bias[bname][:, c:c + 1]} if bname else {}
                    ins = nc.scalar.activation(o_t[:, c, :], bank[:, :], ACT.Identity, **kw)
                    ins.then_inc(a_free, 1 + (A_PER - A_JOBS if act.n == A_JOBS else 0))

            with sc.Fori(0, B) as b:
                for s in range(4):
                    high_part(b, s, s, "sa_bq" if s < 2 else "sa_bk", s % 2)
                for pair in range(QT // 2):
                    store_values(b, 0, pair)
                for s in range(4, 8):
                    high_part(b, s, s, "ca_bk", (s - 4) // 2)
                for pair in range(ET // 2):
                    store_values(b, 1, pair)
                exponentials(b, 0)
                to_o_t(b, "sa_bv")
                to_o_t(b)
                first = V_CROSS - 2
                for s in range(8, 10):
                    high_part(b, s, first + s - 8, "ca_bq", s - 8)
                exponentials(b, 1)
                to_o_t(b, "ca_bv")
                to_o_t(b)
                assert act.n == A_JOBS

        @block.vector
        def _(dve):
            n = 0
            nc.vector.memset(k_stack[0][96:96 + PARTS, :, :], 1.0).then_inc(const_cast, 1)
            nc.vector.memset(k_stack[1][96:96 + PARTS, :, :], 1.0).then_inc(const_cast, 1)
            for t in v_ext:
                nc.vector.memset(t[:, :, :, HD:HD + 1], 1.0).then_inc(const_cast, 1)
                nc.vector.memset(t[:, :, :, HD + 1:], 0.0).then_inc(const_cast, 1)
            dve.wait_ge(const_made, 6)
            nc.vector.tensor_copy(ident_b[:, :], ident[:, :]).then_inc(const_cast, 1)
            nc.vector.memset(max_raw[:, :, :], 0.0).then_inc(const_cast, 1)
            dve.wait_ge(const_cast, 8)
            dve.wait_ge(const_in, 16 * N_LOADS)
            dve.wait_ge(slots_zeroed, 32)
            dve.sem_inc(v_free, RING)
            v = Count(V_PER)
            STEPS = SPLITS + 2 * UNITS * 4 + 2 * (5 + 13)
            st = Count(STEPS)

            def step(b, ins):
                ins.then_inc(dve_step, 1)
                st.next()
                dve.wait_ge(dve_step, st.at(b))

            def step_all(b, instructions):
                for ins in instructions:
                    ins.then_inc(dve_step, 1)
                    st.next()
                dve.wait_ge(dve_step, st.at(b))

            def v_job(b):
                bank = v_bank[v.n % RING]
                v.next()
                dve.wait_ge(v_full, v.at(b))
                return bank

            def low_parts(b, s, bname, c):
                bank = v_bank[v.n % RING]
                v.next()
                p, r = parts[s % 2], rest[s % 2]
                dve.wait_ge(high_done, b * SPLITS + s + 1)
                nc.vector.scalar_tensor_tensor(out=r[:, :], in0=bank[:, :], scalar=bias[bname][:, c:c + 1], in1=p[:, 0, :],
                                               op0=ALU.add, op1=ALU.subtract).then_inc(v_free, 1)
                dve.wait_ge(v_free, v.at(b, RING))
                step(b, nc.vector.tensor_copy(p[:, 1, :], r[:, :]))
                nc.vector.tensor_tensor(p[:, 2, :], r[:, :], p[:, 1, :], ALU.subtract).then_inc(split_done, 1)

            def max_tile(b, kind, tile):
                j, q, half = tile
                n = (q + 1) * P if kind == 0 else S
                bank = v_job(b)
                nc.vector.reduce_max(max_raw[:, QT * j + q, half:half + 1], bank[:, 0:n], X).then_inc(v_free, 1)

            def max_parts(b, kind, u):
                dve.wait_ge(v_free, v.at(b, RING))
                if kind:
                    step(b, nc.vector.tensor_reduce(max_q[:, :], max_raw[:, :, :], X, ALU.max, negate=True))
                else:
                    step(b, nc.vector.tensor_scalar(max_q[:, :], max_raw[:, :, 0], -1.0, None, ALU.mult))
                step(b, nc.vector.tensor_copy(max_p[:, 0, :], max_q[:, :]))
                step(b, nc.vector.tensor_tensor(max_r[:, :], max_q[:, :], max_p[:, 0, :], ALU.subtract))
                step(b, nc.vector.tensor_copy(max_p[:, 1, :], max_r[:, :]))
                nc.vector.tensor_tensor(max_p[:, 2, :], max_r[:, :], max_p[:, 1, :], ALU.subtract).then_inc(maxp_ready, 1)

            def max_rows(b, kind, u):
                bank = v_job(b)
                n_u = UNITS * kind + u
                dve.wait_ge(maxt_out, b * (16 * 2 * UNITS) + 16 * (n_u + 1))
                nc.vector.tensor_copy(max_t[:, :], bank[0:PARTS * G * QT, 0:P // 2].bitcast(BF16)).then_inc(v_free, 1)

            def maxima(b, kind):
                tiles = cross_tiles() if kind else self_tiles()
                for u in range(UNITS):
                    for t in tiles:
                        max_tile(b, kind, t)
                    max_parts(b, kind, u)
                    max_rows(b, kind, u)

            def norm(b, kind, dst):
                step_all(b, [nc.vector.bn_stats(stats[:, q, :], y[:, q, :]) for q in range(QT)])
                dve.sem_inc(passed, 1)
                for q in range(QT):
                    ins = nc.vector.bn_aggr(mv[:, q, :], stats[:, q, :])
                    if q < QT - 1:
                        ins.then_inc(dve_step, 1)
                        st.next()
                    else:
                        ins.then_inc(mean_ready, 1)
                dve.wait_ge(dve_step, st.at(b))
                dve.wait_ge(mean_ready, b * 2 + kind + 1)
                dve.wait_ge(rstd_ready, b * 2 + kind + 1)
                step_all(b, [nc.vector.tensor_scalar(y[:, q, :], y[:, q, :], mv[:, q, 0:1], rstd[:, q:q + 1], ALU.subtract, ALU.mult)
                             for q in range(QT)])
                gam, bet = (ln_gb[:, 2 * kind + i:2 * kind + i + 1, :].to_broadcast([P, QT, D]) for i in range(2))
                step(b, nc.vector.tensor_tensor(y[:, :, :], y[:, :, :], gam, ALU.mult))
                nc.vector.tensor_tensor(y[:, :, :], y[:, :, :], bet, ALU.add).then_inc(y_ready, 1)
                dve.wait_ge(y_ready, b * 2 + kind + 1)
                step(b, nc.vector.tensor_copy(dst, y[:, :, :]))

            def finish(b, kind):
                for q in range(QT):
                    bank = v_job(b)
                    heads = bank[:, :].rearrange("p (h e) -> p h e", e=2 * HD)
                    step(b, nc.vector.reciprocal(recip[:, :], heads[:, :, HD]))
                    nc.vector.tensor_tensor(y[:, q, :].rearrange("p (h d) -> p h d", d=HD), heads[:, :, 0:HD],
                                            recip[:, :].unsqueeze(2).to_broadcast([P, H, HD]), ALU.mult).then_inc(v_free, 1)
                    dve.wait_ge(v_free, v.at(b, RING))
                if kind == 0:
                    dve.wait_ge(x_in, b * 16 + 16)
                step(b, nc.vector.tensor_tensor(xres[:, :, :], xres[:, :, :], out_b[:, kind:kind + 1, :].to_broadcast([P, QT, D]), ALU.add))
                for pair in range(QT // 2):
                    bank = v_job(b)
                    nc.vector.tensor_tensor(y[:, 2 * pair:2 * pair + 2, :], bank[:, :].rearrange("p (t d) -> p t d", d=D),
                                            xres[:, 2 * pair:2 * pair + 2, :], ALU.add).then_inc(v_free, 1)
                dve.wait_ge(v_free, v.at(b, RING))
                norm(b, kind, x2_all[:, bass.ds(b * QT, QT), :] if kind else xres[:, :, :])

            with dve.Fori(0, B) as b:
                for s in range(4):
                    low_parts(b, s, "sa_bq" if s < 2 else "sa_bk", s % 2)
                for s in range(4, 8):
                    low_parts(b, s, "ca_bk", (s - 4) // 2)
                maxima(b, 0)
                finish(b, 0)
                for s in range(8, 10):
                    low_parts(b, s, "ca_bq", s - 8)
                maxima(b, 1)
                finish(b, 1)
                bank = v_job(b)
                nc.vector.tensor_tensor(logits[:, bass.ds(b * QT, QT), :], bank[:, 0:QT * E].rearrange("p (q e) -> p q e", e=E),
                                        router_b[:, :].unsqueeze(1).to_broadcast([P, QT, E]), ALU.add).then_inc(v_free, 1 + V_PER - V_JOBS)
                assert v.n == V_JOBS and st.n == STEPS

        blocks.close()
        att_ctx.close()

        w1 = [sb(f"w1_{i}", [P, DC, FF]) for i in range(2)]
        w2 = [sb(f"w2_{i}", [P, FC, D]) for i in range(2)]
        b1 = sb("b1", [P, E * FC])
        b2 = sb("b2", [P, E, D])
        x_row = sb("x_row", [P, D])
        x_col = sb("x_col", [P, DC, P])
        hidden = sb("hidden", [P, FC, P])
        y_row = sb("y_row", [P, D])
        top_val = sb("top_val", [P, TT, 8])
        top_idx = sb("top_idx", [P, TT, 8], U32)
        idx_f = sb("idx_f", [P, 2, TT])
        iota_i = sb("iota_i", [P, E], I32)
        iota_f = sb("iota_f", [P, E])
        one_hot = sb("one_hot", [P, 2, TT, E])
        taken = sb("taken", [P, TT * E], BF16)
        before_b = sb("before_b", [P, P], BF16)
        ones_b = sb("ones_b", [P, P], BF16)
        total = sb("total", [P, E, TT])
        segment = sb("segment", [P, E, TT])
        running = sb("running", [P, E, TT])
        slot = sb("slot", [P, E, TT])
        picked = sb("picked", [P, 2, TT, E])
        slot_f = sb("slot_f", [P, 2, TT])
        slot_i = sb("slot_i", [P, 2, TT], U32)
        tiles_i = sb("tiles_i", [P, E], I32)
        tiles_f = sb("tiles_f", [P, E])
        ones_f = sb("ones_f", [P, E])
        tiles_run = sb("tiles_run", [P, E])
        first_f = sb("first_f", [P, E])
        first_i = sb("first_i", [P, E], I32)
        tiles_total = sb("tiles_total", [P, 1], I32)
        shifted = sb("shifted", [P, TT, E])
        exps = sb("exps", [P, TT, E])
        exp_sum = sb("exp_sum", [P, TT])
        prob_step = sb("prob_step", [P, TT])
        top_w = sb("top_w", [P, 2, TT])
        y_got = sb("y_got", [P, TT, 2, D])

        moe_const = sem("moe_const")
        moe_made = sem("moe_made")
        w_in = [sem("w_in0"), sem("w_in1")]
        route = sem("route")
        rank_full = sem("rank_full")
        shift_ready, exp_ready = sem("shift_ready"), sem("exp_ready")
        step_ready, w_ready = sem("step_ready"), sem("w_ready")
        slots_ready = sem("slots_ready")
        scattered = sem("scattered")
        xrow_in = sem("xrow_in")
        t_full, xcol_ready = sem("t_full"), sem("xcol_ready")
        h_full, gelu_done = sem("h_full"), sem("gelu_done")
        y_full, y_evac, y_stored = sem("y_full"), sem("y_evac"), sem("y_stored")
        got = [sem(f"got{t}") for t in range(TT)]
        fin_step = sem("fin_step")
        var_ready, root_ready = sem("var_ready"), sem("root_ready")
        fin_ready = sem("fin_ready")
        out_done = sem("out_done")

        HB = 4
        h_bank = [a_bank[0], a_bank[1], a_bank[2], v_bank[0]]
        t_bank, y_bank = v_bank[1], v_bank[2]
        LAST = E // 2 - 1

        def expert_tiles(eng, e, body):
            first = eng.value_load(first_i[0:1, bass.ds(e, 1)], min_val=0, max_val=SLOT_TILES)
            count = eng.value_load(tiles_i[0:1, bass.ds(e, 1)], min_val=1, max_val=TOK // P)
            with eng.Fori(0, count) as i:
                body(nc.s_assert_within(eng.snap(first + i), 0, SLOT_TILES - 1,
                                        skip_runtime_bounds_check_because="all experts' tiles together are at most SLOT_TILES"))
            return first + count

        block = ctx.enter_context(nc.Block())

        @block.sync
        def _(sp):
            def load_weights(e, i):
                sp.dma_start(w1[i][:, :, :], a["e_w1"][bass.ds(e, 1)].rearrange("o (c p) n -> p (o c) n", p=P)).then_inc(w_in[i], 16)
                sp.dma_start(w2[i][:, :, :], a["e_w2"][bass.ds(e, 1)].rearrange("o (c p) n -> p (o c) n", p=P)).then_inc(w_in[i], 16)

            def load_row(g):
                sp.dma_start(x_row[:, :], slots_dram[bass.ds(g * P, P), :]).then_inc(xrow_in, 16)

            sp.dma_start(b1[:, :], a["e_b1"]).then_inc(moe_const, 16)
            sp.dma_start(b2[:, :, :], a["e_b2"].rearrange("(o e) n -> o e n", o=1).to_broadcast([P, E, D])).then_inc(moe_const, 16)
            for i in range(2):
                load_weights(i, i)
            sp.sem_inc(y_stored, 16)
            sp.wait_ge(scattered, 16 * 2 * TT)
            load_row(0)
            sp.wait_ge(slots_ready, 2)

            def tile(g):
                sp.wait_ge(t_full, g + 1)
                load_row(g + 1)
                sp.wait_ge(y_evac, g + 2)
                sp.dma_start(y_dram[bass.ds(g * P, P), :], y_row[:, :]).then_inc(y_stored, 16)

            with sp.Fori(0, LAST) as pair:
                for i in range(2):
                    after = expert_tiles(sp, 2 * pair + i, tile)
                    sp.wait_ge(y_full, after)
                    load_weights(2 * pair + i + 2, i)
            for i in range(2):
                expert_tiles(sp, 2 * LAST + i, tile)
            out_view = out.rearrange("(t p) d -> p t d", p=P)
            for n in range(TT // QT):
                sp.wait_ge(fin_ready, n + 1)
                sp.dma_start(out_view[:, n * QT:(n + 1) * QT, :], x2_all[:, n * QT:(n + 1) * QT, :]).then_inc(out_done, 16)
            sp.wait_ge(out_done, 16 * TT // QT)

        @block.gpsimd
        def _(pool):
            nc.gpsimd.memset(before_b[:, :], 1.0).then_inc(moe_made, 1)
            nc.gpsimd.memset(ones_b[:, :], 1.0).then_inc(moe_made, 1)
            nc.gpsimd.iota(iota_i[:, :], [[1, E]], base=0, channel_multiplier=0).then_inc(moe_made, 1)
            pool.wait_ge(moe_made, 3)
            nc.gpsimd.affine_select(out=before_b[:, :], in_=before_b[:, :], compare_op=ALU.is_gt, fill=0.0, base=0,
                                    pattern=[[1, P]], channel_multiplier=-1).then_inc(moe_made, 1)
            pool.wait_ge(slots_ready, 1)
            for t in range(TT):
                for k in range(2):
                    pool.indirect_dma_start(out=slots_dram, out_offset=bass.IndirectOffsetOnAxis(ap=slot_i[:, k, t:t + 1], axis=0),
                                            in_=x2_all[:, t, :], in_offset=None).then_inc(scattered, 16)
            pool.wait_ge(slots_ready, 2)
            tiles = pool.value_load(tiles_total[0:1, 0:1], min_val=E, max_val=SLOT_TILES)
            pool.wait_ge(y_stored, tiles * 16 + 16)
            pool.sem_inc(passed, 1)
            for t in range(TT):
                for k in range(2):
                    pool.indirect_dma_start(out=y_got[:, t, k, :], out_offset=None, in_=y_dram,
                                            in_offset=bass.IndirectOffsetOnAxis(ap=slot_i[:, k, t:t + 1], axis=0)).then_inc(got[t], 16)

        @block.tensor
        def _(pe):
            pe.wait_ge(moe_made, 4)
            pe.wait_ge(route, ROUTE_TAKEN)
            nc.tensor.matmul(v_bank[0][:, 0:TT * E], before_b[:, :], taken[:, :], start=True, stop=True)
            nc.tensor.matmul(v_bank[0][:, TT * E:2 * TT * E], ones_b[:, :], taken[:, :], start=True, stop=True).then_inc(rank_full, 1)

            def transpose_row(g):
                pe.wait_ge(xrow_in, g * 16 + 16)
                for c in range(DC):
                    last = nc.tensor.transpose(t_bank[:, c * P:(c + 1) * P], x_row[:, c * P:(c + 1) * P], ident[:, :])
                last.then_inc(t_full, 1)

            pe.wait_ge(slots_ready, 2)
            transpose_row(0)

            def tile(i, g):
                pe.wait_ge(xcol_ready, g + 1)
                for f in range(FC):
                    pe.wait_ge(gelu_done, g * FC + f + 1)
                    for c in range(DC):
                        last = nc.tensor.matmul(h_bank[f % HB][:, 0:P], w1[i][:, c, f * P:(f + 1) * P], x_col[:, c, :],
                                                start=(c == 0), stop=(c == DC - 1))
                    last.then_inc(h_full, 1)
                transpose_row(g + 1)
                pe.wait_ge(y_evac, g + 1)
                for f in range(FC):
                    pe.wait_ge(gelu_done, g * FC + f + 1 + HB)
                    last = nc.tensor.matmul(y_bank[:, 0:D], hidden[:, f, :], w2[i][:, f, :], start=(f == 0), stop=(f == FC - 1))
                last.then_inc(y_full, 1)

            with pe.Fori(0, E // 2) as pair:
                for i in range(2):
                    pe.wait_ge(w_in[i], pair * 32 + 32)
                    expert_tiles(pe, 2 * pair + i, lambda g: tile(i, g))

        @block.scalar
        def _(sc):
            sc.sem_inc(gelu_done, HB)
            sc.wait_ge(shift_ready, 1)
            nc.scalar.activation(exps[:, :, :], shifted[:, :, :], ACT.Exp).then_inc(exp_ready, 1)
            sc.wait_ge(step_ready, 1)
            nc.scalar.activation(prob_step[:, :], prob_step[:, :], ACT.Exp).then_inc(w_ready, 1)
            sc.wait_ge(moe_const, 32)
            sc.wait_ge(slots_ready, 2)
            with sc.Fori(0, E // 2) as pair:
                for i in range(2):
                    e = 2 * pair + i

                    def tile(g):
                        for f in range(FC):
                            sc.wait_ge(h_full, g * FC + f + 1)
                            nc.scalar.activation(hidden[:, f, :], h_bank[f % HB][:, 0:P], ACT.Gelu,
                                                 bias=b1[:, bass.ds(e * FC + f, 1)]).then_inc(gelu_done, 1)

                    expert_tiles(sc, e, tile)
            for n in range(TT // QT):
                sc.wait_ge(var_ready, n + 1)
                nc.scalar.activation(rstd[:, :], rstd[:, :], ACT.Sqrt).then_inc(root_ready, 1)

        @block.vector
        def _(dve):
            done = [0]

            def step(*instructions):
                for ins in instructions:
                    ins.then_inc(route, 1)
                    done[0] += 1
                dve.wait_ge(route, done[0])

            dve.sem_inc(y_evac, 1)
            step(*[nc.vector.max(top_val[:, t, :], logits[:, t, :]) for t in range(TT)],
                 nc.vector.memset(segment[:, :, :], 1.0), nc.vector.memset(ones_f[:, :], 1.0))
            step(*[nc.vector.max_index(top_idx[:, t, :], top_val[:, t, :], logits[:, t, :]) for t in range(TT)],
                 nc.vector.memset(segment[:, :, 0:1], 0.0))
            dve.wait_ge(moe_made, 4)
            step(nc.vector.tensor_copy(idx_f[:, :, :], top_idx[:, :, 0:2].rearrange("p t k -> p k t")),
                 nc.vector.tensor_copy(iota_f[:, :], iota_i[:, :]))
            step(*[nc.vector.tensor_tensor(one_hot[:, k, :, :], idx_f[:, k, :].unsqueeze(2).to_broadcast([P, TT, E]),
                                           iota_f[:, :].unsqueeze(1).to_broadcast([P, TT, E]), ALU.is_equal) for k in range(2)])
            step(nc.vector.tensor_tensor(taken[:, :], one_hot[:, 0, :, :].rearrange("p t e -> p (t e)"),
                                         one_hot[:, 1, :, :].rearrange("p t e -> p (t e)"), ALU.add))
            assert done[0] == ROUTE_TAKEN
            nc.vector.tensor_tensor(shifted[:, :, :], logits[:, :, :], top_val[:, :, 0:1].to_broadcast([P, TT, E]),
                                    ALU.subtract).then_inc(shift_ready, 1)
            dve.wait_ge(rank_full, 1)
            within = v_bank[0][:, 0:TT * E].rearrange("p (t e) -> p e t", e=E)
            totals = v_bank[0][:, TT * E:2 * TT * E].rearrange("p (t e) -> p e t", e=E)
            step(nc.vector.tensor_copy(total[:, :, :], totals))
            step(nc.vector.tensor_tensor_scan(out=running[:, :, :].rearrange("p e t -> p (e t)"), data0=segment[:, :, :].rearrange("p e t -> p (e t)"),
                                              data1=total[:, :, :].rearrange("p e t -> p (e t)"), initial=0.0, op0=ALU.mult, op1=ALU.add))
            step(nc.vector.tensor_scalar(tiles_f[:, :], running[:, :, TT - 1], float(P - 1), None, ALU.add),
                 nc.vector.tensor_tensor(slot[:, :, :], running[:, :, :], total[:, :, :], ALU.subtract))
            step(nc.vector.tensor_copy(tiles_i[:, :], tiles_f[:, :]))
            step(nc.vector.tensor_scalar(tiles_i[:, :], tiles_i[:, :], 7, None, ALU.arith_shift_right))
            step(nc.vector.tensor_scalar(tiles_i[:, :], tiles_i[:, :], 1, None, ALU.max))
            step(nc.vector.tensor_copy(tiles_f[:, :], tiles_i[:, :]))
            step(nc.vector.tensor_tensor_scan(out=tiles_run[:, :], data0=ones_f[:, :], data1=tiles_f[:, :], initial=0.0,
                                              op0=ALU.mult, op1=ALU.add))
            step(nc.vector.tensor_tensor(first_f[:, :], tiles_run[:, :], tiles_f[:, :], ALU.subtract),
                 nc.vector.tensor_copy(tiles_total[:, :], tiles_run[:, E - 1:E]),
                 nc.vector.tensor_tensor(slot[:, :, :], slot[:, :, :], within, ALU.add))
            step(nc.vector.tensor_copy(first_i[:, :], first_f[:, :]),
                 nc.vector.tensor_scalar(first_f[:, :], first_f[:, :], float(P), None, ALU.mult))
            step(nc.vector.tensor_tensor(slot[:, :, :], slot[:, :, :], first_f[:, :].unsqueeze(2).to_broadcast([P, E, TT]), ALU.add))
            step(*[nc.vector.tensor_tensor(picked[:, k, :, :], one_hot[:, k, :, :], slot[:, :, :].rearrange("p e t -> p t e"), ALU.mult)
                   for k in range(2)])
            step(nc.vector.reduce_sum(slot_f[:, :, :], picked[:, :, :, :], X))
            nc.vector.tensor_copy(slot_i[:, :, :], slot_f[:, :, :]).then_inc(slots_ready, 1)
            dve.wait_ge(exp_ready, 1)
            step(nc.vector.reduce_sum(exp_sum[:, :], exps[:, :, :], X))
            step(nc.vector.reciprocal(exp_sum[:, :], exp_sum[:, :]))
            step(nc.vector.tensor_tensor(picked[:, 1, :, :], one_hot[:, 1, :, :], exps[:, :, :], ALU.mult))
            step(nc.vector.reduce_sum(prob_step[:, :], picked[:, 1, :, :], X))
            step(nc.vector.tensor_tensor(prob_step[:, :], prob_step[:, :], exp_sum[:, :], ALU.mult))
            nc.vector.tensor_tensor(prob_step[:, :], prob_step[:, :], exp_sum[:, :], ALU.subtract).then_inc(step_ready, 1)
            dve.wait_ge(w_ready, 1)
            step(nc.vector.tensor_scalar(top_w[:, 1, :], prob_step[:, :], 1.0, None, ALU.add))
            step(nc.vector.reciprocal(top_w[:, 0, :], top_w[:, 1, :]))
            nc.vector.tensor_tensor(top_w[:, 1, :], top_w[:, 0, :], prob_step[:, :], ALU.mult).then_inc(slots_ready, 1)
            dve.wait_ge(slots_ready, 2)

            def copy_column(g):
                dve.wait_ge(t_full, g + 1)
                nc.vector.tensor_copy(x_col[:, :, :], t_bank[:, 0:D].rearrange("p (c t) -> p c t", c=DC)).then_inc(xcol_ready, 1)

            copy_column(0)
            dve.wait_ge(moe_const, 32)
            with dve.Fori(0, E // 2) as pair:
                for i in range(2):
                    e = 2 * pair + i

                    def tile(g):
                        copy_column(g + 1)
                        dve.wait_ge(y_full, g + 1)
                        dve.wait_ge(y_stored, g * 16 + 16)
                        nc.vector.tensor_tensor(y_row[:, :], y_bank[:, 0:D], b2[:, bass.ds(e, 1), :].rearrange("p o d -> p (o d)"),
                                                ALU.add).then_inc(y_evac, 1)

                    expert_tiles(dve, e, tile)

            fin = [0]

            def fstep(*instructions):
                for ins in instructions:
                    ins.then_inc(fin_step, 1)
                    fin[0] += 1
                dve.wait_ge(fin_step, fin[0])

            for n in range(TT // QT):
                ts = range(n * QT, (n + 1) * QT)
                x2 = x2_all[:, n * QT:(n + 1) * QT, :]
                for t in ts:
                    dve.wait_ge(got[t], 32)
                for k in range(2):
                    fstep(*[nc.vector.scalar_tensor_tensor(out=x2_all[:, t, :], in0=y_got[:, t, k, :], scalar=top_w[:, k, t:t + 1],
                                                           in1=x2_all[:, t, :], op0=ALU.mult, op1=ALU.add) for t in ts])
                fstep(*[nc.vector.bn_stats(stats[:, t % QT, :], x2_all[:, t, :]) for t in ts])
                fstep(*[nc.vector.bn_aggr(mv[:, t % QT, :], stats[:, t % QT, :]) for t in ts])
                nc.vector.tensor_scalar(rstd[:, :], mv[:, :, 1], EPS, None, ALU.add).then_inc(var_ready, 1)
                dve.wait_ge(root_ready, n + 1)
                fstep(nc.vector.reciprocal(rstd[:, :], rstd[:, :]))
                fstep(*[nc.vector.tensor_scalar(x2_all[:, t, :], x2_all[:, t, :], mv[:, t % QT, 0:1], rstd[:, t % QT:t % QT + 1],
                                                ALU.subtract, ALU.mult) for t in ts])
                fstep(nc.vector.tensor_tensor(x2, x2, ln_gb[:, 4:5, :].to_broadcast([P, QT, D]), ALU.mult))
                nc.vector.tensor_tensor(x2, x2, ln_gb[:, 5:6, :].to_broadcast([P, QT, D]), ALU.add).then_inc(fin_ready, 1)


_INS = ["x", "xT", "ctxT"] + [f"{k}_{n}" for k in ("sa", "ca") for n in ("wq", "bq", "wk", "bk", "wv", "bv", "wo", "bo")] + [
    "ln1_g", "ln1_b", "ln2_g", "ln2_b", "ln3_g", "ln3_b", "router_w", "router_b", "e_w1", "e_b1", "e_w2", "e_b2"]


def kernel(**inputs):
    import numpy as _np
    import concourse.bacc as _bacc
    from concourse import mybir as _mybir
    from concourse.bass_utils import run_bass_kernel_spmd as _run

    given = {k.replace("L0_xattn_", ""): _np.asarray(v) for k, v in inputs.items()}
    x = given["x"].reshape(TOK, D)
    given["x"], given["xT"] = x, x.T
    given["ctxT"] = given.pop("ctx_1024").reshape(B * SE, D).T
    given["e_b1"] = given["e_b1"].reshape(E, FC, P).transpose(2, 0, 1).reshape(P, E * FC)
    nc = _bacc.Bacc("TRN2", target_bir_lowering=False, num_devices=1)
    arrays, aps = {}, {}
    for name in _INS:
        v = _np.ascontiguousarray(given[name])
        arrays[f"in_{name}"] = v
        aps[name] = nc.dram_tensor(f"in_{name}", v.shape, _mybir.dt.from_np(v.dtype), kind="ExternalInput").ap()
    out = nc.dram_tensor("out", (TOK, D), _mybir.dt.float32, kind="ExternalOutput").ap()
    decoder_layer(nc, aps, out)
    r = _run(nc, [arrays], core_ids=[0])
    return r.results[0]["out"].reshape(B, S, D)
```

```python
import concourse.bass as bass
from concourse import mybir
from contextlib import ExitStack

F32 = mybir.dt.float32
BF16 = mybir.dt.bfloat16
I32 = mybir.dt.int32
U32 = mybir.dt.uint32
ACT = mybir.ActivationFunctionType
ALU = mybir.AluOpType
X = mybir.AxisListType.X

P = 128
B, S, SE, D = 4, 512, 1024, 256
H, HD = 16, 16
E, FF = 8, 1024
DC, FC = D // P, FF // P
QT, ET = S // P, SE // P
TT = B * QT
TOK = B * S
G = 4
UNITS = H // G
EPS = 1e-5
NEG = -1e30
SCALE = HD ** -0.5
PARTS = 3
Q_PART = [0, 0, 0, 1, 1, 2]
K_PART = [0, 1, 2, 0, 1, 0]
NG = len(Q_PART)
KR = NG * HD
KM = KR + PARTS
SLOT_TILES = TOK * 2 // P + E
RING = 3
SPLITS = 10


ROUTE_TAKEN = 2 * TT + 3 + 2 + 2 + 1


class Count:

    def __init__(self, per, ring=1):
        self.n, self.per, self.pad = 0, per, -per % ring
        self.taken = 0
        self.register, self.end = None, None

    def at(self, k=0):
        return self.n + k if self.register is None else self.register * (self.per + self.pad) + (self.n + k)

    def turns(self, of, amount, k=0):
        n = amount * (self.n // of + k)
        return n if self.register is None else self.register * (self.per // of * amount) + n

    def next(self):
        self.n += 1
        self.taken += 1
        if self.n == self.end:
            self.n += self.pad
            return 1 + self.pad
        return 1

    def enter(self, register):
        self.register, self.end = register, self.n + self.per

    def leave(self, runs):
        assert self.n == self.end + self.pad, (self.n, self.end, self.pad)
        self.n += (runs - 1) * (self.per + self.pad)
        self.register, self.end = None, None


def counted(ev):
    k = ev[0]
    if k == "split":
        return ["v", "split", "step", ("stack", ev[1])]
    return {"values": ["a"], "max": ["v"], "max_parts": ["step"] * 4, "max_rows": ["v", "rows"],
            "score": ["a"] + (["tile"] if k == "score" and ev[5] else []) + (["begun"] if k == "score" and ev[3] == 0 and ev[4][0] == 0 else []), "weigh": ["pv"], "o_out": ["unit"], "o_turn": ["v", "step"],
            "att_turn": ["a"] * DC, "norm_turn": ["a"] * DC, "out": ["v"] * (QT // 2) + ["out"] + ["step"] * (2 * QT - 1),
            "norm": ["norm"] + ["step"] * (QT + 2), "route": ["v"], "add_bias": ["step"], "load_x": ["load_x"],
            "load_ctx": ["load_ctx"], "load_res": ["load_res"], "turned": []}[k]


class Counts:

    def __init__(self):
        names = ("v", "a", "split", "rows", "tile", "pv", "begun", "unit", "out", "norm", "step", "load_x", "load_ctx", "load_res") + tuple(
            ("stack", s) for s in range(SPLITS))
        per = {name: 0 for name in names}
        for ev in BODY:
            for name in counted(ev):
                per[name] += 1
        self.named = {name: Count(per[name], RING if name in ("v", "a") else 1) for name in names}
        self.v, self.a, self.step = self.named["v"], self.named["a"], self.named["step"]
        self.split, self.rows = self.named["split"], self.named["rows"]
        self.tile, self.pv = self.named["tile"], self.named["pv"]
        self.begun, self.unit = self.named["begun"], self.named["unit"]
        self.out, self.norm = self.named["out"], self.named["norm"]
        self.load_x, self.load_ctx, self.load_res = self.named["load_x"], self.named["load_ctx"], self.named["load_res"]
        self.stack = [self.named[("stack", s)] for s in range(SPLITS)]
        assert self.rows.per % AHEAD_ROWS == 0 and all(c.per % 2 == 0 for c in (self.split, self.tile, self.unit, self.pv))

    def do(self, step, ev, where):
        names = counted(ev)
        want = {name: self.named[name].taken + names.count(name) for name in names}
        step(ev, where)
        for name, n in want.items():
            while self.named[name].taken < n:
                self.named[name].next()
            assert self.named[name].taken == n, (ev, name)


class Where:
    def __init__(self, r):
        self.r = r


AHEAD_ROWS = 4
LOOPED = 2


def walk(eng, c, step):
    for ev in START:
        c.do(step, ev, Where(None))
    with eng.Fori(0, LOOPED) as r:
        for x in c.named.values():
            x.enter(r)
        for ev in BODY:
            c.do(step, ev, Where(r))
    for x in c.named.values():
        x.leave(LOOPED)
    for ev in REST:
        c.do(step, ev, Where(None))



def max_steps(kind, u):
    if kind:
        tiles = [("max", 1, u, (j,), q, half) for j in range(G) for q in range(QT) for half in range(2)]
    else:
        tiles = [("max", 0, u, tuple(range(G)), 0, 0)] + [("max", 0, u, (j, j + 1), 1, 0) for j in (0, 2)] + [
            ("max", 0, u, (j,), q, 0) for q in (2, 3) for j in range(G)]
    return tiles + [("max_parts", kind, u)]


def with_rows(items, after=2):
    out, due = [], []
    for it in items:
        out.append(it)
        due = [(n - 1, e) for n, e in due]
        while due and due[0][0] == 0:
            out.append(due.pop(0)[1])
        if it[0] == "max_parts":
            due.append((after, ("max_rows",) + it[1:]))
    return out + [e for _, e in due]


def score_steps(kind, u, kt):
    wide = 1 if kind or kt < 2 else 2 if kt == 2 else 4
    groups = [tuple(range(j, j + wide)) for j in range(0, G, wide)]
    return [("score", kind, u, kt, js, js == groups[-1]) for js in groups]


LEAD = 14
AHEAD = 4.0


def max_weight(ev):
    if ev[0] == "max_parts":
        return 2.0
    if ev[0] == "max_rows":
        return 0.5
    return 1.0 if ev[1] else 0.15 + len(ev[3]) * (ev[4] + 1) * P / 512


def attention_steps(units, pieces, maxima, held=3):
    seq = []
    weigh = None
    for n, (kind, u) in enumerate(units):
        turn = None
        for kt in range(ET if kind else QT):
            seq += [(e, 0) for e in pieces.get((n, kt), [])]
            steps = score_steps(kind, u, kt)
            weight = (1.0 if kind else 1.0 - 0.2 * kt) * (4.0 / len(steps)) 
            for i, e in enumerate(steps):
                seq.append((e, weight))
                if i == min(1, len(steps) - 1):
                    if turn and kt == 1:
                        seq.append((turn, 0))
                    if weigh:
                        seq += [(x, 0) for x in weigh]
                        if weigh[-1][0] == "o_out":
                            turn = ("o_turn",) + weigh[-1][1:]
            weigh = [("weigh", kind, u, kt)]
        weigh.append(("o_out", kind, u))
    t, starts = 0.0, []
    for e, x in seq:
        if e[0] == "score" and e[3] == 0 and e[4][0] == 0 and t > 0:
            starts.append((t, ("max_rows",) + e[1:3]))
        t += x
    cost = [max_weight(e) for e in maxima]
    upto = [sum(cost[:i + 1]) for i in range(len(cost))]
    due = [(max(s - AHEAD, 0.0), upto[maxima.index(e)]) for s, e in starts if e in maxima]
    due.append((t, upto[len(maxima) - held - 1]))
    out, now, cur, taken = [], 0.0, 0.0, 0
    for e, x in seq:
        if now > 0 and e[0] == "score" and e[3] == 0 and e[4][0] == 0 and ("max_rows",) + e[1:3] in maxima[taken:]:
            stop = taken + maxima[taken:].index(("max_rows",) + e[1:3]) + 1
            out += maxima[taken:stop]
            taken, cur = stop, max(cur, upto[stop - 1])
        out.append(e)
        rate = max((n - cur) / max(s - now, x, 1e-6) for s, n in due if n > cur or s == t)
        cur += max(rate, 0.0) * x
        now += x
        while taken < len(maxima) - held and upto[taken] <= cur + 1e-6:
            out.append(maxima[taken])
            taken += 1
    out += weigh + pieces.get("end", []) + maxima[taken:]
    return out + [("o_turn",) + weigh[-1][1:]]


SELF = [(0, u) for u in range(UNITS)]
CROSS = [(1, u) for u in range(UNITS)]


def fixed(b):
    return lambda r: b


SELF_IN = [("split", 0), ("split", 2), ("split", 1), ("split", 3), ("values", 0, 0), ("values", 0, 1)]


def make_steps():
    first_max = with_rows([e for u in range(UNITS) for e in max_steps(0, u)])
    per_batch = [e for k, u in SELF + CROSS[1:] + CROSS[:1] for e in max_steps(k, u)]
    all_max = with_rows(max_steps(1, 0) + per_batch * (B - 1) + [e for u in range(1, UNITS) for e in max_steps(1, u)])
    per = len(per_batch) + len(SELF + CROSS)
    cut = len(max_steps(1, 0)) + 1 + LEAD
    start = [("load_x", fixed(0)), ("load_ctx", fixed(0)), ("load_res", fixed(0))] + SELF_IN + [("load_x", fixed(1)), ("add_bias",)]
    early = len(max_steps(0, 0)) + 5
    start += first_max[:early]
    pieces = {(0, 1): [("split", 4)], (0, 2): [("split", 5)], (1, 0): [("values", 1, 0)], (1, 2): [("values", 1, 1)], (2, 0): [("values", 1, 2)]}
    start += attention_steps(SELF, pieces, first_max[early:])
    start += [("att_turn", 0), ("split", 0), ("out", 0), ("load_res", fixed(1)), ("split", 2), ("norm", 0, fixed(0)), ("split", 1), ("norm_turn", 0), ("split", 3), ("turned",),
              ("split", 8), ("values", 0, 0), ("values", 0, 1)] + all_max[:cut]

    def run(kinds, maxima, before, after_self, nxt, self_next, c_tile, s_tile, loads):
        units = CROSS[:1] + (SELF if kinds else []) + CROSS[1:]
        u1 = 1 + (UNITS if kinds else 0)
        p = {}

        def put(n, kt, *e):
            p.setdefault((n, kt), []).extend(e)

        put(0, 0, ("split", 9))
        put(0, 1, ("values", 1, 3), *loads["x"])
        if before:
            put(0, 1, ("att_turn", 1))
            put(0, 2, ("out", 1, c_tile))
        put(0, 3, ("split", 6))
        if before:
            put(0, 4, ("norm", 1, c_tile))
        put(0, 5, ("split", 7), *loads["ctx"])
        if before:
            put(0, 6, ("norm_turn", 1))
            put(0, 7, ("turned",), ("route", c_tile))
        if kinds:
            put(2, 0, ("add_bias",))
        if kinds:
            put(u1, 2, ("att_turn", 0))
            put(u1, 3, ("out", 0), *loads["res"])
            put(u1, 5, ("norm", 0, s_tile))
            put(u1, 7, ("norm_turn", 0))
            put(u1 + 1, 1, ("turned",), ("split", 8))
            put(u1 + 1, 2, ("split", 4))
            put(u1 + 1, 3, ("split", 5))
            if self_next:
                put(u1 + 1, 4, ("split", 0))
                put(u1 + 1, 5, ("split", 2))
                put(u1 + 1, 6, ("split", 1))
                put(u1 + 1, 7, ("split", 3))
                put(u1 + 2, 0, ("values", 0, 0))
                put(u1 + 2, 1, ("values", 0, 1))
            put(u1 + 2, 3, ("values", 1, 0))
            put(u1 + 2, 5, ("values", 1, 1))
            put(u1 + 2, 7, ("values", 1, 2))
        return attention_steps(units, p, maxima)

    body = run(True, all_max[cut:cut + per], True, True, True, True,
               lambda r: (B - 1) - r * (B - 1),
               lambda r: r + 1,
               {"x": [("load_x", lambda r: r + 2)], "ctx": [("load_ctx", lambda r: r + 1)], "res": [("load_res", lambda r: r + 2)]})
    assert all_max[cut:cut + per] == all_max[cut + per:cut + 2 * per]
    at = cut + 2 * per
    end = at + per
    rest = run(True, all_max[at:end], True, True, True, False, fixed(1), fixed(3),
               {"x": [], "ctx": [("load_ctx", fixed(3))], "res": []})
    rest += run(False, all_max[end:], True, False, False, False, fixed(2), None, {"x": [], "ctx": [], "res": []})
    rest += [("att_turn", 1), ("out", 1, fixed(3)), ("norm", 1, fixed(3)), ("norm_turn", 1), ("turned",), ("route", fixed(3))]
    return start, body, rest


START, BODY, REST = make_steps()


def decoder_layer(nc, a, out):
    ctx = ExitStack()
    with ctx:
        def sb(name, shape, dt=F32):
            return ctx.enter_context(nc.sbuf_tensor(name, shape, dt))

        def sem(name):
            return ctx.enter_context(nc.semaphore(name))

        parts_dram = nc.dram_tensor("parts_scratch", (SPLITS, PARTS, P, S), BF16).ap()
        max_dram = nc.dram_tensor("max_scratch", (2, PARTS, G * S), BF16).ap()
        slots_dram = nc.dram_tensor("slots_in", ((SLOT_TILES + 2) * P, D), F32).ap()
        y_dram = nc.dram_tensor("slots_out", (SLOT_TILES * P, D), F32).ap()

        x2_all = sb("x2_all", [P, TT, D])
        logits = sb("logits", [P, TT, E])
        ident = sb("ident", [P, P])
        ident_b = sb("ident_b", [P, P], BF16)
        ln_gb = sb("ln_gb", [P, 6, D])
        stats = sb("stats", [P, QT, 6])
        mv = sb("mv", [P, QT, 2])
        rstd = sb("rstd", [P, QT])
        neg_half = sb("neg_half", [P, QT])
        router_b = sb("router_b", [P, E])

        v_bank = [ctx.enter_context(nc.psum_tensor(f"v_bank{i}", [P, 512], F32)) for i in range(RING)]
        a_bank = [ctx.enter_context(nc.psum_tensor(f"a_bank{i}", [P, 512], F32)) for i in range(RING)]
        o_bank = [ctx.enter_context(nc.psum_tensor(f"o_bank{i}", [P, 512], F32)) for i in range(2)]

        const_in = sem("const_in")
        const_made = sem("const_made")
        const_cast = sem("const_cast")
        slots_zeroed = sem("slots_zeroed")
        xt_in, ctx_in, x_in = sem("xt_in"), sem("ctx_in"), sem("x_in")
        v_full, v_free = sem("v_full"), sem("v_free")
        a_full, a_free = sem("a_full"), sem("a_free")
        high_done = sem("high_done")
        split_done = sem("split_done")
        part_out = [sem("part_out0"), sem("part_out1")]
        stack_in = [sem(f"stack_in{s}") for s in range(SPLITS)]
        maxp_ready = sem("maxp_ready")
        maxt_out = sem("maxt_out")
        max_in = [sem(f"max_in{i}") for i in range(AHEAD_ROWS)]
        pv_done = sem("pv_done")
        o_out = sem("o_out")
        mean_ready, rstd_ready = sem("mean_ready"), sem("rstd_ready")
        y_ready = sem("y_ready")
        dve_step = sem("dve_step")
        pool_step = sem("pool_step")
        passed = sem("passed")

        att_ctx = ExitStack()

        def sba(name, shape, dt=F32):
            return att_ctx.enter_context(nc.sbuf_tensor(name, shape, dt))

        w = {n: sba("w_" + n, [P, DC, D]) for n in ("sa_wq", "sa_wk", "sa_wv", "sa_wo", "ca_wq", "ca_wk", "ca_wv", "ca_wo")}
        router_w = sba("w_router", [P, DC, E])
        bias = {n: sba("b_" + n, [P, DC]) for n in ("sa_bq", "sa_bk", "sa_bv", "ca_bq", "ca_bk", "ca_bv")}
        out_b = sba("out_b", [P, 2, D])
        mask_q = sba("mask_q", [P, P], BF16)
        mask_k = sba("mask_k", [P, P], BF16)
        xt = sba("xt", [P, DC, S])
        ctxt = sba("ctxt", [P, DC, SE])
        xres = sba("xres", [P, QT, D])
        parts = [sba(f"parts{i}", [P, PARTS, S], BF16) for i in range(2)]
        rest = [sba(f"rest{i}", [P, S]) for i in range(2)]
        q_stack = [sba("q_stack_self", [P, H, S], BF16), sba("q_stack_cross", [P, H, S], BF16)]
        k_stack = [sba("k_stack_self", [P, H, S], BF16), sba("k_stack_cross", [P, H, SE], BF16)]
        v_ext = [sba("v_self", [P, QT, H, 2 * HD]), sba("v_cross", [P, ET, H, 2 * HD])]
        probs = [sba(f"probs{i}", [P, G, S]) for i in range(2)]
        o_sb = [sba(f"o_sb{i}", [P, S]) for i in range(2)]
        y = [sba("y_self", [P, QT, D]), sba("y_cross", [P, QT, D])]
        o_t = sba("o_t", [P, DC, S])
        max_raw = sba("max_raw", [P, G, QT, 2])
        max_q = sba("max_q", [P, G * QT])
        max_r = sba("max_r", [P, G * QT])
        max_p = sba("max_p", [P, PARTS, G * QT], BF16)
        max_t = sba("max_t", [PARTS * G * QT, P], BF16)
        recip = sba("recip", [P, QT, G])

        blocks = ExitStack()
        block = blocks.enter_context(nc.Block())
        xt_d = a["xT"].rearrange("(c p) t -> p c t", p=P)
        ctx_d = a["ctxT"].rearrange("(c p) t -> p c t", p=P)
        x_d = a["x"].rearrange("(t p) d -> p t d", p=P)
        slot_view = slots_dram.rearrange("(n p) d -> p n d", p=P)
        N_LOADS = 8 + 1 + 6 + 2 + 6 + 1

        def split_target(s):
            if s in (0, 1, 8, 9):
                return q_stack[s // 8], 8 * (s % 2), 0, Q_PART
            if s in (2, 3):
                return k_stack[0], 8 * (s % 2), 0, K_PART
            return k_stack[1], 8 * ((s - 4) // 2), S * (s % 2), K_PART

        def projection(s):
            if s < 2:
                return "sa_wq", xt, "sa_bq", s, 0
            if s < 4:
                return "sa_wk", xt, "sa_bk", s - 2, 0
            if s < 8:
                return "ca_wk", ctxt, "ca_bk", (s - 4) // 2, S * (s % 2)
            return "ca_wq", o_t, "ca_bq", s - 8, 0

        CASTS = 8

        @block.sync
        def _(sp):
            for n in ("sa_wq", "sa_wk", "sa_wv", "ca_wk", "ca_wv", "sa_wo", "ca_wq", "ca_wo"):
                sp.dma_start(w[n][:, :, :], a[n].rearrange("(c p) n -> p c n", p=P)).then_inc(const_in, 16)
            sp.dma_start(router_w[:, :, :], a["router_w"].rearrange("(c p) n -> p c n", p=P)).then_inc(const_in, 16)
            with nc.allow_non_contiguous_dma(reason="six columns of 256 numbers"):
                for n, t in bias.items():
                    sp.dma_start(t[:, :], a[n].rearrange("(c p) -> p c", p=P)).then_inc(const_in, 16)
            for i, n in enumerate(("sa_bo", "ca_bo")):
                sp.dma_start(out_b[:, i, :], a[n].rearrange("(o n) -> o n", o=1).to_broadcast([P, D])).then_inc(const_in, 16)
            for i, n in enumerate(("ln1_g", "ln1_b", "ln2_g", "ln2_b", "ln3_g", "ln3_b")):
                sp.dma_start(ln_gb[:, i, :], a[n].rearrange("(o n) -> o n", o=1).to_broadcast([P, D])).then_inc(const_in, 16)
            sp.dma_start(router_b[:, :], a["router_b"].rearrange("(o n) -> o n", o=1).to_broadcast([P, E])).then_inc(const_in, 16)
            sp.wait_ge(const_made, 1)
            sp.dma_start(y_dram[(SLOT_TILES - E) * P:, :].rearrange("(n p) d -> p n d", p=P),
                         y[1][:, 0:1, :].to_broadcast([P, E, D])).then_inc(slots_zeroed, 16)
            sp.dma_start(slot_view, y[1][:, 0:1, :].to_broadcast([P, SLOT_TILES + 2, D])).then_inc(slots_zeroed, 16)

            for i in range(2):
                sp.sem_inc(part_out[i], 16)
            sp.sem_inc(maxt_out, 16)
            c = Counts()

            def step(ev, where):
                k, args = ev[0], ev[1:]
                if k == "split":
                    s = args[0]
                    i, stored = c.split.n % 2, c.split.turns(2, 16, 1) + 16
                    c.split.next()
                    sp.wait_ge(split_done, c.split.at())
                    sp.dma_start(parts_dram[s].rearrange("j p t -> p j t"), parts[i][:, :, :]).then_inc(part_out[i], 16)
                    sp.wait_ge(part_out[i], stored)
                    sp.sem_inc(passed, 1)
                    if c.pv.n:
                        sp.wait_ge(pv_done, c.pv.at(2))
                    stack, h0, t0, which = split_target(s)
                    for g in range(NG):
                        sp.dma_start(stack[HD * g:HD * (g + 1), h0:h0 + 8, t0:t0 + S],
                                     parts_dram[s, which[g]].rearrange("(h r) t -> r h t", r=HD)).then_inc(stack_in[s], 16)
                elif k == "max_rows":
                    kind, u = args
                    c.v.next()
                    i, n = c.rows.n % 2, c.rows.n % AHEAD_ROWS
                    c.rows.next()
                    sp.wait_ge(v_free, c.v.at(RING))
                    sp.dma_start(max_dram[i].rearrange("j (c t) -> (j c) t", t=P), max_t[:, :]).then_inc(maxt_out, 16)
                    sp.wait_ge(maxt_out, c.rows.at() * 16 + 16)
                    sp.dma_start(q_stack[kind][KR:KM, G * u:G * (u + 1), :].rearrange("p h t -> p (h t)"), max_dram[i]).then_inc(max_in[n], 16)
            walk(sp, c, step)

        @block.gpsimd
        def _(pool):
            nc.gpsimd.memset(y[1][:, :, :], 0.0).then_inc(const_made, 1)
            nc.gpsimd.memset(neg_half[:, :], -0.5).then_inc(const_made, 1)
            nc.gpsimd.memset(ident[:, :], 0.0).then_inc(const_made, 1)
            nc.gpsimd.memset(mask_q[:, :], 0.0).then_inc(const_made, 1)
            nc.gpsimd.memset(mask_k[:, :], 0.0).then_inc(const_made, 1)
            pool.wait_ge(const_made, 5)
            nc.gpsimd.affine_select(out=ident[:, :], in_=ident[:, :], compare_op=ALU.not_equal, fill=1.0, base=0,
                                    pattern=[[-1, P]], channel_multiplier=1).then_inc(const_made, 1)
            nc.gpsimd.affine_select(out=mask_q[:, :], in_=mask_q[:, :], compare_op=ALU.is_ge, fill=NEG, base=0,
                                    pattern=[[-1, P]], channel_multiplier=1).then_inc(const_made, 1)
            nc.gpsimd.affine_select(out=mask_k[:, :], in_=mask_k[:, :], compare_op=ALU.is_ge, fill=NEG, base=0,
                                    pattern=[[1, P]], channel_multiplier=-1).then_inc(const_made, 1)
            c = Counts()

            def step(ev, where):
                k, args = ev[0], ev[1:]
                if k == "out":
                    c.out.next()
                if k == "load_x":
                    if c.v.n:
                        pool.wait_ge(v_full, c.v.at())
                        pool.wait_ge(a_full, c.a.at())
                    pool.dma_start(xt[:, :, :], xt_d[:, :, bass.ds(args[0](where.r) * S, S)]).then_inc(xt_in, 16)
                elif k == "load_ctx":
                    if c.v.n:
                        pool.wait_ge(v_full, c.v.at())
                        pool.wait_ge(a_full, c.a.at())
                    pool.dma_start(ctxt[:, :, :], ctx_d[:, :, bass.ds(args[0](where.r) * SE, SE)]).then_inc(ctx_in, 16)
                elif k == "load_res":
                    pool.dma_start(xres[:, :, :], x_d[:, bass.ds(args[0](where.r) * QT, QT), :]).then_inc(x_in, 16)
                elif k == "out":
                    pool.wait_ge(mean_ready, c.out.at())
                    pool.sem_inc(passed, 1)
                    nc.gpsimd.tensor_scalar(rstd[:, :], mv[:, :, 1], EPS, None, ALU.add).then_inc(pool_step, 1)
                    pool.wait_ge(pool_step, c.out.at())
                    nc.gpsimd.tensor_tensor(rstd[:, :], rstd[:, :], neg_half[:, :], ALU.pow).then_inc(rstd_ready, 1)

            walk(pool, c, step)

        @block.tensor
        def _(pe):
            pe.wait_ge(const_in, 16 * N_LOADS)
            pe.wait_ge(const_made, 8)
            pe.wait_ge(const_cast, CASTS)
            pe.sem_inc(pv_done, 2)
            c = Counts()
            probs_ready = []

            def v_next():
                pe.wait_ge(v_free, c.v.at(1))
                bank = v_bank[c.v.n % RING]
                return bank, c.v.next()

            def a_next():
                pe.wait_ge(a_free, c.a.at(1))
                bank = a_bank[c.a.n % RING]
                return bank, c.a.next()

            def transpose_y(kind):
                for ch in range(DC):
                    bank, n = a_next()
                    for q in range(QT):
                        last = nc.tensor.transpose(bank[:, q * P:(q + 1) * P], y[kind][:, q, ch * P:(ch + 1) * P], ident[:, :])
                    last.then_inc(a_full, n)

            def stacks_ready(kind, u):
                for s in ((u // 2, 2 + u // 2) if kind == 0 else (4 + 2 * (u // 2), 5 + 2 * (u // 2), 8 + u // 2)):
                    pe.wait_ge(stack_in[s], c.stack[s].at() * (16 * NG))

            def step(ev, where):
                k, args = ev[0], ev[1:]
                if k == "split":
                    s = args[0]
                    wname, src, _, ch, t0 = projection(s)
                    if s == 0:
                        pe.wait_ge(xt_in, c.load_x.at() * 16)
                    elif s == 4:
                        pe.wait_ge(ctx_in, c.load_ctx.at() * 16)
                    bank, n = v_next()
                    for kk in range(DC):
                        last = nc.tensor.matmul(bank[:, :], w[wname][:, kk, ch * P:(ch + 1) * P], src[:, kk, t0:t0 + S],
                                                start=(kk == 0), stop=(kk == DC - 1))
                    last.then_inc(v_full, n)
                    c.stack[s].next()
                elif k == "values":
                    kind, pair = args
                    src, wname = (ctxt, "ca_wv") if kind else (xt, "sa_wv")
                    bank, n = a_next()
                    for i in range(2):
                        t = 2 * pair + i
                        for kk in range(DC):
                            last = nc.tensor.matmul(bank[:, i * D:(i + 1) * D], src[:, kk, t * P:(t + 1) * P], w[wname][:, kk, :],
                                                    start=(kk == 0), stop=(kk == DC - 1))
                    last.then_inc(a_full, n)
                elif k == "max":
                    kind, u, js, q, half = args
                    if js[0] == 0 and q == 0:
                        stacks_ready(kind, u)
                    bank, inc = v_next()
                    for i, j in enumerate(js):
                        lhs = q_stack[kind][0:KR, G * u + j, q * P:(q + 1) * P]
                        if kind:
                            last = nc.tensor.matmul(bank[:, :], lhs, k_stack[1][0:KR, G * u + j, half * S:(half + 1) * S], start=True, stop=True)
                        else:
                            n = (q + 1) * P
                            nc.tensor.matmul(bank[:, i * n:(i + 1) * n], lhs, k_stack[0][0:KR, G * u + j, 0:n], start=True, stop=False)
                            last = nc.tensor.matmul(bank[:, (i + 1) * n - P:(i + 1) * n], ident_b[:, :], mask_q[:, :], start=False, stop=True)
                    last.then_inc(v_full, inc)
                elif k == "max_rows":
                    bank, n = v_next()
                    c.rows.next()
                    pe.wait_ge(maxp_ready, c.rows.at())
                    pe.sem_inc(passed, 1)
                    nc.tensor.transpose(bank[0:PARTS * G * QT, 0:P // 2].bitcast(BF16), max_p[:, :, :].rearrange("p j c -> p (j c)"),
                                        ident_b[:, :]).then_inc(v_full, n)
                elif k == "score":
                    kind, u, kt, js, last_of_tile = args
                    if kt == 0 and js[0] == 0:
                        pe.wait_ge(max_in[c.begun.n % AHEAD_ROWS], c.begun.turns(AHEAD_ROWS, 16, 1))
                    bank, inc = a_next()
                    q0 = 0 if kind else kt * P
                    n = S - q0
                    for i, j in enumerate(js):
                        lhs = k_stack[kind][0:KM, G * u + j, kt * P:(kt + 1) * P]
                        last = nc.tensor.matmul(bank[:, i * n:(i + 1) * n], lhs, q_stack[kind][0:KM, G * u + j, q0:S],
                                                start=True, stop=bool(kind))
                        if kind == 0:
                            last = nc.tensor.matmul(bank[:, i * n:i * n + P], ident_b[:, :], mask_k[:, :], start=False, stop=True)
                    last.then_inc(a_full, inc)
                    if last_of_tile:
                        probs_ready.append(c.a.at(RING))
                elif k == "weigh":
                    kind, u, kt = args
                    o = o_bank[c.unit.n % 2]
                    q0 = 0 if kind else kt * P
                    if kt == 0:
                        pe.wait_ge(o_out, c.unit.at(1))
                    pe.wait_ge(a_free, probs_ready.pop(0))
                    for j in range(G):
                        last = nc.tensor.matmul(o[32 * j:32 * (j + 1), q0:S], v_ext[kind][:, kt, G * u + j, :], probs[c.pv.n % 2][:, j, q0:S],
                                                start=(kt == 0), stop=(kt == (ET if kind else QT) - 1))
                    last.then_inc(pv_done, 1)
                    c.pv.next()
                elif k == "o_turn":
                    bank, n = v_next()
                    pe.wait_ge(o_out, c.unit.at(2))
                    for q in range(QT):
                        last = nc.tensor.transpose(bank[:, q * P:(q + 1) * P], o_sb[(c.unit.n - 1) % 2][:, q * P:(q + 1) * P], ident[:, :])
                    last.then_inc(v_full, n)
                elif k == "att_turn":
                    pe.wait_ge(v_free, c.v.at(RING))
                    transpose_y(args[0])
                elif k == "out":
                    kind = args[0]
                    pe.wait_ge(a_free, c.a.at(RING))
                    for pair in range(QT // 2):
                        bank, n = v_next()
                        for i in range(2):
                            t = 2 * pair + i
                            for kk in range(DC):
                                last = nc.tensor.matmul(bank[:, i * D:(i + 1) * D], o_t[:, kk, t * P:(t + 1) * P],
                                                        w["ca_wo" if kind else "sa_wo"][:, kk, :], start=(kk == 0), stop=(kk == DC - 1))
                        last.then_inc(v_full, n)
                elif k == "norm_turn":
                    pe.wait_ge(y_ready, c.norm.at())
                    transpose_y(args[0])
                    norm_in_o_t = c.a.at(RING)
                    follow_up.append(norm_in_o_t)
                elif k == "turned":
                    pe.wait_ge(a_free, follow_up.pop())
                elif k == "route":
                    bank, n = v_next()
                    for q in range(QT):
                        for kk in range(DC):
                            last = nc.tensor.matmul(bank[:, q * E:(q + 1) * E], o_t[:, kk, q * P:(q + 1) * P], router_w[:, kk, :],
                                                    start=(kk == 0), stop=(kk == DC - 1))
                    last.then_inc(v_full, n)

            follow_up = []
            walk(pe, c, step)

        @block.scalar
        def _(sc):
            sc.wait_ge(const_in, 16 * N_LOADS)
            sc.sem_inc(a_free, RING)
            sc.sem_inc(o_out, 2)
            c = Counts()

            def a_job():
                bank = a_bank[c.a.n % RING]
                n = c.a.next()
                sc.wait_ge(a_full, c.a.at())
                return bank, n

            def to_o_t(bname=None):
                for ch in range(DC):
                    bank, n = a_job()
                    kw = {"bias": bias[bname][:, ch:ch + 1]} if bname else {}
                    nc.scalar.activation(o_t[:, ch, :], bank[:, :], ACT.Identity, **kw).then_inc(a_free, n)

            def step(ev, where):
                k, args = ev[0], ev[1:]
                if k == "split":
                    _, _, bname, ch, _ = projection(args[0])
                    i = c.split.n % 2
                    sc.wait_ge(part_out[i], c.split.turns(2, 16) + 16)
                    c.split.next()
                    bank = v_bank[c.v.n % RING]
                    c.v.next()
                    sc.wait_ge(v_full, c.v.at())
                    nc.scalar.activation(parts[i][:, 0, :], bank[:, :], ACT.Identity, bias=bias[bname][:, ch:ch + 1]).then_inc(high_done, 1)
                elif k == "values":
                    kind, pair = args
                    bank, n = a_job()
                    nc.scalar.activation(v_ext[kind][:, 2 * pair:2 * pair + 2, :, 0:HD],
                                         bank[:, :].rearrange("p (t h d) -> p t h d", t=2, d=HD), ACT.Identity).then_inc(a_free, n)
                elif k == "score":
                    kind, u, kt, js, last_of_tile = args
                    q0 = 0 if kind else kt * P
                    if js[0] == 0:
                        sc.wait_ge(pv_done, c.tile.at(1))
                    bank, n = a_job()
                    nc.scalar.activation(probs[c.tile.n % 2][:, js[0]:js[-1] + 1, q0:S],
                                         bank[:, 0:len(js) * (S - q0)].rearrange("p (j t) -> p j t", j=len(js)), ACT.Exp,
                                         scale=SCALE).then_inc(a_free, n)
                    if last_of_tile:
                        c.tile.next()
                elif k == "o_out":
                    sc.wait_ge(pv_done, c.pv.at(2))
                    nc.scalar.activation(o_sb[c.unit.n % 2][:, :], o_bank[c.unit.n % 2][:, :], ACT.Identity).then_inc(o_out, 1)
                    c.unit.next()
                elif k == "att_turn":
                    to_o_t("ca_bv" if args[0] else "sa_bv")
                elif k == "norm_turn":
                    to_o_t()

            walk(sc, c, step)

        @block.vector
        def _(dve):
            nc.vector.memset(k_stack[0][96:96 + PARTS, :, :], 1.0).then_inc(const_cast, 1)
            nc.vector.memset(k_stack[1][96:96 + PARTS, :, :], 1.0).then_inc(const_cast, 1)
            for t in v_ext:
                nc.vector.memset(t[:, :, :, HD:HD + 1], 1.0).then_inc(const_cast, 1)
                nc.vector.memset(t[:, :, :, HD + 1:], 0.0).then_inc(const_cast, 1)
            dve.wait_ge(const_made, 6)
            nc.vector.tensor_copy(ident_b[:, :], ident[:, :]).then_inc(const_cast, 1)
            nc.vector.memset(x2_all[:, TT - QT:TT, :], 0.0).then_inc(const_cast, 1)
            dve.wait_ge(const_cast, CASTS)
            dve.wait_ge(const_in, 16 * N_LOADS)
            dve.wait_ge(slots_zeroed, 32)
            dve.sem_inc(v_free, RING)
            c = Counts()

            def own(*instructions):
                for ins in instructions:
                    ins.then_inc(dve_step, 1)
                    c.step.next()
                dve.wait_ge(dve_step, c.step.at())

            def v_job():
                bank = v_bank[c.v.n % RING]
                n = c.v.next()
                dve.wait_ge(v_full, c.v.at())
                return bank, n

            def step(ev, where):
                k, args = ev[0], ev[1:]
                if k == "split":
                    _, _, bname, ch, _ = projection(args[0])
                    bank = v_bank[c.v.n % RING]
                    n = c.v.next()
                    p, r = parts[c.split.n % 2], rest[c.split.n % 2]
                    c.split.next()
                    dve.wait_ge(high_done, c.split.at())
                    nc.vector.scalar_tensor_tensor(out=r[:, :], in0=bank[:, :], scalar=bias[bname][:, ch:ch + 1], in1=p[:, 0, :],
                                                   op0=ALU.add, op1=ALU.subtract).then_inc(v_free, n)
                    dve.wait_ge(v_free, c.v.at(RING))
                    own(nc.vector.tensor_copy(p[:, 1, :], r[:, :]))
                    nc.vector.tensor_tensor(p[:, 2, :], r[:, :], p[:, 1, :], ALU.subtract).then_inc(split_done, 1)
                elif k == "max":
                    kind, u, js, q, half = args
                    n = S if kind else (q + 1) * P
                    bank, inc = v_job()
                    nc.vector.reduce_max(max_raw[:, js[0]:js[-1] + 1, q, half], bank[:, 0:len(js) * n].rearrange("p (j t) -> p j t", j=len(js)),
                                         X).then_inc(v_free, inc)
                elif k == "max_parts":
                    dve.wait_ge(v_free, c.v.at(RING))
                    raw = max_raw[:, :, :, :].rearrange("p j q h -> p (j q) h")
                    if args[0]:
                        own(nc.vector.tensor_reduce(max_q[:, :], raw, X, ALU.max, negate=True))
                    else:
                        own(nc.vector.tensor_scalar(max_q[:, :], raw[:, :, 0], -1.0, None, ALU.mult))
                    own(nc.vector.tensor_copy(max_p[:, 0, :], max_q[:, :]))
                    own(nc.vector.tensor_tensor(max_r[:, :], max_q[:, :], max_p[:, 0, :], ALU.subtract))
                    own(nc.vector.tensor_copy(max_p[:, 1, :], max_r[:, :]))
                    nc.vector.tensor_tensor(max_p[:, 2, :], max_r[:, :], max_p[:, 1, :], ALU.subtract).then_inc(maxp_ready, 1)
                elif k == "max_rows":
                    bank, n = v_job()
                    c.rows.next()
                    dve.wait_ge(maxt_out, c.rows.at() * 16)
                    nc.vector.tensor_copy(max_t[:, :], bank[0:PARTS * G * QT, 0:P // 2].bitcast(BF16)).then_inc(v_free, n)
                elif k == "o_turn":
                    kind, u = args
                    dve.wait_ge(v_free, c.v.at(RING))
                    bank, n = v_job()
                    heads = bank[:, :].rearrange("p (q h e) -> p q h e", q=QT, e=2 * HD)
                    own(nc.vector.reciprocal(recip[:, :, :], heads[:, :, :, HD]))
                    nc.vector.tensor_tensor(y[kind][:, :, G * HD * u:G * HD * (u + 1)].rearrange("p q (h d) -> p q h d", d=HD),
                                            heads[:, :, :, 0:HD], recip[:, :, :].unsqueeze(3).to_broadcast([P, QT, G, HD]),
                                            ALU.mult).then_inc(v_free, n)
                elif k == "add_bias":
                    dve.wait_ge(x_in, c.load_res.at() * 16)
                    own(nc.vector.tensor_tensor(xres[:, :, :], xres[:, :, :], out_b[:, 0:1, :].to_broadcast([P, QT, D]), ALU.add))
                elif k == "out":
                    kind = args[0]
                    for pair in range(QT // 2):
                        bank, n = v_job()
                        old = x2_all[:, bass.ds(args[1](where.r) * QT + 2 * pair, 2), :] if kind else xres[:, 2 * pair:2 * pair + 2, :]
                        nc.vector.tensor_tensor(y[kind][:, 2 * pair:2 * pair + 2, :], bank[:, :].rearrange("p (t d) -> p t d", d=D),
                                                old, ALU.add).then_inc(v_free, n)
                    dve.wait_ge(v_free, c.v.at(RING))
                    own(*[nc.vector.bn_stats(stats[:, q, :], y[kind][:, q, :]) for q in range(QT)])
                    dve.sem_inc(passed, 1)
                    c.out.next()
                    for q in range(QT):
                        ins = nc.vector.bn_aggr(mv[:, q, :], stats[:, q, :])
                        if q < QT - 1:
                            ins.then_inc(dve_step, 1)
                            c.step.next()
                        else:
                            ins.then_inc(mean_ready, 1)
                    dve.wait_ge(dve_step, c.step.at())
                    dve.wait_ge(mean_ready, c.out.at())
                elif k == "norm":
                    kind, tile = args[0], args[1](where.r)
                    yk = y[kind]
                    c.norm.next()
                    dve.wait_ge(rstd_ready, c.norm.at())
                    own(*[nc.vector.tensor_scalar(yk[:, q, :], yk[:, q, :], mv[:, q, 0:1], rstd[:, q:q + 1], ALU.subtract, ALU.mult)
                          for q in range(QT)])
                    gam, bet = (ln_gb[:, 2 * kind + i:2 * kind + i + 1, :].to_broadcast([P, QT, D]) for i in range(2))
                    own(nc.vector.tensor_tensor(yk[:, :, :], yk[:, :, :], gam, ALU.mult))
                    nc.vector.tensor_tensor(yk[:, :, :], yk[:, :, :], bet, ALU.add).then_inc(y_ready, 1)
                    dve.wait_ge(y_ready, c.norm.at())
                    dst = x2_all[:, bass.ds(tile * QT, QT), :]
                    if kind:
                        dve.sem_inc(passed, 1)
                        own(nc.vector.tensor_copy(dst, yk[:, :, :]))
                    else:
                        own(nc.vector.tensor_tensor(dst, yk[:, :, :], out_b[:, 1:2, :].to_broadcast([P, QT, D]), ALU.add))
                elif k == "route":
                    bank, n = v_job()
                    nc.vector.tensor_tensor(logits[:, bass.ds(args[0](where.r) * QT, QT), :], bank[:, 0:QT * E].rearrange("p (q e) -> p q e", e=E),
                                            router_b[:, :].unsqueeze(1).to_broadcast([P, QT, E]), ALU.add).then_inc(v_free, n)

            walk(dve, c, step)

        blocks.close()
        att_ctx.close()

        w1 = [sb(f"w1_{i}", [P, DC, FF]) for i in range(2)]
        w2 = [sb(f"w2_{i}", [P, FC, D]) for i in range(2)]
        b1 = sb("b1", [P, E * FC])
        b2 = sb("b2", [P, E, D])
        x_row = sb("x_row", [P, D])
        x_col = sb("x_col", [P, DC, P])
        hidden = sb("hidden", [P, FC, P])
        x_slots = sb("x_slots", [P, SLOT_TILES + 2, D])
        y_slots = sb("y_slots", [P, SLOT_TILES, D])
        top_val = sb("top_val", [P, TT, 8])
        top_idx = sb("top_idx", [P, TT, 8], U32)
        idx_f = sb("idx_f", [P, 2, TT])
        iota_i = sb("iota_i", [P, E], I32)
        iota_f = sb("iota_f", [P, E])
        one_hot = sb("one_hot", [P, 2, TT, E])
        taken = sb("taken", [P, TT * E], BF16)
        before_b = sb("before_b", [P, P], BF16)
        ones_b = sb("ones_b", [P, P], BF16)
        total = sb("total", [P, E, TT])
        segment = sb("segment", [P, E, TT])
        running = sb("running", [P, E, TT])
        slot = sb("slot", [P, E, TT])
        picked = sb("picked", [P, 2, TT, E])
        slot_f = sb("slot_f", [P, 2, TT])
        slot_i = sb("slot_i", [P, 2, TT], U32)
        tiles_i = sb("tiles_i", [P, E], I32)
        tiles_f = sb("tiles_f", [P, E])
        ones_f = sb("ones_f", [P, E])
        tiles_run = sb("tiles_run", [P, E])
        first_f = sb("first_f", [P, E])
        first_i = sb("first_i", [P, E], I32)
        tiles_total = sb("tiles_total", [P, 1], I32)
        shifted = sb("shifted", [P, TT, E])
        exps = sb("exps", [P, TT, E])
        exp_sum = sb("exp_sum", [P, TT])
        prob_step = sb("prob_step", [P, TT])
        gelu_warm = sb("gelu_warm", [P, 1])
        top_w = sb("top_w", [P, 2, TT])
        y_got = sb("y_got", [P, TT, 2, D])

        moe_const = sem("moe_const")
        moe_made = sem("moe_made")
        w_in = [sem("w_in0"), sem("w_in1")]
        warmed = sem("warmed")
        route = sem("route")
        rank_full = sem("rank_full")
        shift_ready, exp_ready = sem("shift_ready"), sem("exp_ready")
        step_ready, w_ready = sem("step_ready"), sem("w_ready")
        slots_ready = sem("slots_ready")
        scattered = sem("scattered")
        x_in_slots = sem("x_in_slots")
        row_ready = sem("row_ready")
        t_full, xcol_ready = sem("t_full"), sem("xcol_ready")
        h_full, gelu_done = sem("h_full"), sem("gelu_done")
        y_full, y_evac, y_stored = sem("y_full"), sem("y_evac"), sem("y_stored")
        got = [sem(f"got{t}") for t in range(TT)]
        fin_step = sem("fin_step")
        var_ready, root_ready = sem("var_ready"), sem("root_ready")
        fin_ready = sem("fin_ready")
        out_done = sem("out_done")

        HB = 4
        h_bank = [a_bank[0], a_bank[1], a_bank[2], v_bank[0]]
        t_bank, y_bank = v_bank[1], v_bank[2]
        LAST = E // 2 - 1

        def expert_tiles(eng, e, body):
            first = eng.value_load(first_i[0:1, bass.ds(e, 1)], min_val=0, max_val=SLOT_TILES)
            count = eng.value_load(tiles_i[0:1, bass.ds(e, 1)], min_val=1, max_val=TOK // P)
            with eng.Fori(0, count) as i:
                body(nc.s_assert_within(eng.snap(first + i), 0, SLOT_TILES - 1,
                                        skip_runtime_bounds_check_because="all experts' tiles together are at most SLOT_TILES"))
            return first + count

        block = ctx.enter_context(nc.Block())

        @block.sync
        def _(sp):
            def load_weights(e, i):
                sp.dma_start(w1[i][:, :, :], a["e_w1"][bass.ds(e, 1)].rearrange("o (c p) n -> p (o c) n", p=P)).then_inc(w_in[i], 16)
                sp.dma_start(w2[i][:, :, :], a["e_w2"][bass.ds(e, 1)].rearrange("o (c p) n -> p (o c) n", p=P)).then_inc(w_in[i], 16)

            sp.dma_start(b1[:, :], a["e_b1"]).then_inc(moe_const, 16)
            sp.dma_start(b2[:, :, :], a["e_b2"].rearrange("(o e) n -> o e n", o=1).to_broadcast([P, E, D])).then_inc(moe_const, 16)
            for i in range(2):
                load_weights(i, i)
            sp.sem_inc(y_stored, 16)
            sp.wait_ge(slots_ready, 2)

            def tile(g):
                sp.wait_ge(y_evac, g + 2)
                sp.dma_start(y_dram[bass.ds(g * P, P), :], y_slots[:, bass.ds(g, 1), :].rearrange("p o d -> p (o d)")).then_inc(y_stored, 16)

            with sp.Fori(0, LAST) as pair:
                for i in range(2):
                    after = expert_tiles(sp, 2 * pair + i, tile)
                    sp.wait_ge(y_full, after)
                    load_weights(2 * pair + i + 2, i)
            for i in range(2):
                expert_tiles(sp, 2 * LAST + i, tile)
            out_view = out.rearrange("(t p) d -> p t d", p=P)
            for n in range(TT // QT):
                sp.wait_ge(fin_ready, n + 1)
                sp.dma_start(out_view[:, n * QT:(n + 1) * QT, :], x2_all[:, n * QT:(n + 1) * QT, :]).then_inc(out_done, 16)
            sp.wait_ge(out_done, 16 * TT // QT)

        @block.gpsimd
        def _(pool):
            nc.gpsimd.memset(before_b[:, :], 1.0).then_inc(moe_made, 1)
            nc.gpsimd.memset(ones_b[:, :], 1.0).then_inc(moe_made, 1)
            nc.gpsimd.iota(iota_i[:, :], [[1, E]], base=0, channel_multiplier=0).then_inc(moe_made, 1)
            pool.wait_ge(moe_made, 3)
            nc.gpsimd.affine_select(out=before_b[:, :], in_=before_b[:, :], compare_op=ALU.is_gt, fill=0.0, base=0,
                                    pattern=[[1, P]], channel_multiplier=-1).then_inc(moe_made, 1)
            pool.wait_ge(slots_ready, 1)
            for t in range(TT):
                for k in range(2):
                    pool.indirect_dma_start(out=slots_dram, out_offset=bass.IndirectOffsetOnAxis(ap=slot_i[:, k, t:t + 1], axis=0),
                                            in_=x2_all[:, t, :], in_offset=None).then_inc(scattered, 16)
            pool.wait_ge(slots_ready, 2)
            pool.wait_ge(scattered, 16 * 2 * TT)
            with pool.Fori(0, SLOT_TILES + 2) as g:
                pool.dma_start(x_slots[:, bass.ds(g, 1), :].rearrange("p o d -> p (o d)"), slots_dram[bass.ds(g * P, P), :]).then_inc(x_in_slots, 16)
                pool.wait_ge(x_in_slots, g * 16 + 16)
            tiles = pool.value_load(tiles_total[0:1, 0:1], min_val=E, max_val=SLOT_TILES)
            pool.wait_ge(y_stored, tiles * 16 + 16)
            pool.sem_inc(passed, 1)
            for t in range(TT):
                for k in range(2):
                    pool.indirect_dma_start(out=y_got[:, t, k, :], out_offset=None, in_=y_dram,
                                            in_offset=bass.IndirectOffsetOnAxis(ap=slot_i[:, k, t:t + 1], axis=0)).then_inc(got[t], 16)

        @block.tensor
        def _(pe):
            pe.wait_ge(moe_made, 4)
            pe.wait_ge(route, ROUTE_TAKEN)
            nc.tensor.matmul(v_bank[0][:, 0:TT * E], before_b[:, :], taken[:, :], start=True, stop=True)
            nc.tensor.matmul(v_bank[0][:, TT * E:2 * TT * E], ones_b[:, :], taken[:, :], start=True, stop=True).then_inc(rank_full, 1)

            def transpose_row(g):
                pe.wait_ge(row_ready, g + 1)
                for c in range(DC):
                    last = nc.tensor.transpose(t_bank[:, c * P:(c + 1) * P], x_row[:, c * P:(c + 1) * P], ident[:, :])
                last.then_inc(t_full, 1)

            pe.wait_ge(slots_ready, 2)
            transpose_row(0)

            def tile(i, g):
                pe.wait_ge(xcol_ready, g + 1)
                for f in range(FC):
                    pe.wait_ge(gelu_done, g * FC + f + 1)
                    for c in range(DC):
                        last = nc.tensor.matmul(h_bank[f % HB][:, 0:P], w1[i][:, c, f * P:(f + 1) * P], x_col[:, c, :],
                                                start=(c == 0), stop=(c == DC - 1))
                    last.then_inc(h_full, 1)
                transpose_row(g + 1)
                pe.wait_ge(y_evac, g + 1)
                for f in range(FC):
                    pe.wait_ge(gelu_done, g * FC + f + 1 + HB)
                    last = nc.tensor.matmul(y_bank[:, 0:D], hidden[:, f, :], w2[i][:, f, :], start=(f == 0), stop=(f == FC - 1))
                last.then_inc(y_full, 1)

            with pe.Fori(0, E // 2) as pair:
                for i in range(2):
                    pe.wait_ge(w_in[i], pair * 32 + 32)
                    expert_tiles(pe, 2 * pair + i, lambda g: tile(i, g))

        @block.scalar
        def _(sc):
            sc.sem_inc(gelu_done, HB)
            sc.wait_ge(shift_ready, 1)
            nc.scalar.activation(exps[:, :, :], shifted[:, :, :], ACT.Exp).then_inc(exp_ready, 1)
            sc.wait_ge(step_ready, 1)
            nc.scalar.activation(prob_step[:, :], prob_step[:, :], ACT.Exp).then_inc(w_ready, 1)
            sc.wait_ge(moe_const, 32)
            nc.scalar.activation(gelu_warm[:, :], b1[:, 0:1], ACT.Gelu).then_inc(warmed, 1)
            sc.wait_ge(slots_ready, 2)
            with sc.Fori(0, E // 2) as pair:
                for i in range(2):
                    e = 2 * pair + i

                    def tile(g):
                        for f in range(FC):
                            sc.wait_ge(h_full, g * FC + f + 1)
                            nc.scalar.activation(hidden[:, f, :], h_bank[f % HB][:, 0:P], ACT.Gelu,
                                                 bias=b1[:, bass.ds(e * FC + f, 1)]).then_inc(gelu_done, 1)

                    expert_tiles(sc, e, tile)
            for n in range(TT // QT):
                sc.wait_ge(var_ready, n + 1)
                nc.scalar.activation(rstd[:, :], rstd[:, :], ACT.Sqrt).then_inc(root_ready, 1)

        @block.vector
        def _(dve):
            done = [0]

            def step(*instructions):
                for ins in instructions:
                    ins.then_inc(route, 1)
                    done[0] += 1
                dve.wait_ge(route, done[0])

            dve.sem_inc(y_evac, 1)
            step(*[nc.vector.max(top_val[:, t, :], logits[:, t, :]) for t in range(TT)],
                 nc.vector.memset(segment[:, :, :], 1.0), nc.vector.memset(ones_f[:, :], 1.0))
            step(*[nc.vector.max_index(top_idx[:, t, :], top_val[:, t, :], logits[:, t, :]) for t in range(TT)],
                 nc.vector.memset(segment[:, :, 0:1], 0.0))
            dve.wait_ge(moe_made, 4)
            step(nc.vector.tensor_copy(idx_f[:, :, :], top_idx[:, :, 0:2].rearrange("p t k -> p k t")),
                 nc.vector.tensor_copy(iota_f[:, :], iota_i[:, :]))
            step(*[nc.vector.tensor_tensor(one_hot[:, k, :, :], idx_f[:, k, :].unsqueeze(2).to_broadcast([P, TT, E]),
                                           iota_f[:, :].unsqueeze(1).to_broadcast([P, TT, E]), ALU.is_equal) for k in range(2)])
            step(nc.vector.tensor_tensor(taken[:, :], one_hot[:, 0, :, :].rearrange("p t e -> p (t e)"),
                                         one_hot[:, 1, :, :].rearrange("p t e -> p (t e)"), ALU.add))
            assert done[0] == ROUTE_TAKEN
            nc.vector.tensor_tensor(shifted[:, :, :], logits[:, :, :], top_val[:, :, 0:1].to_broadcast([P, TT, E]),
                                    ALU.subtract).then_inc(shift_ready, 1)
            dve.wait_ge(rank_full, 1)
            within = v_bank[0][:, 0:TT * E].rearrange("p (t e) -> p e t", e=E)
            totals = v_bank[0][:, TT * E:2 * TT * E].rearrange("p (t e) -> p e t", e=E)
            step(nc.vector.tensor_copy(total[:, :, :], totals))
            step(nc.vector.tensor_tensor_scan(out=running[:, :, :].rearrange("p e t -> p (e t)"), data0=segment[:, :, :].rearrange("p e t -> p (e t)"),
                                              data1=total[:, :, :].rearrange("p e t -> p (e t)"), initial=0.0, op0=ALU.mult, op1=ALU.add))
            step(nc.vector.tensor_scalar(tiles_f[:, :], running[:, :, TT - 1], float(P - 1), None, ALU.add),
                 nc.vector.tensor_tensor(slot[:, :, :], running[:, :, :], total[:, :, :], ALU.subtract))
            step(nc.vector.tensor_copy(tiles_i[:, :], tiles_f[:, :]))
            step(nc.vector.tensor_scalar(tiles_i[:, :], tiles_i[:, :], 7, None, ALU.arith_shift_right))
            step(nc.vector.tensor_scalar(tiles_i[:, :], tiles_i[:, :], 1, None, ALU.max))
            step(nc.vector.tensor_copy(tiles_f[:, :], tiles_i[:, :]))
            step(nc.vector.tensor_tensor_scan(out=tiles_run[:, :], data0=ones_f[:, :], data1=tiles_f[:, :], initial=0.0,
                                              op0=ALU.mult, op1=ALU.add))
            step(nc.vector.tensor_tensor(first_f[:, :], tiles_run[:, :], tiles_f[:, :], ALU.subtract),
                 nc.vector.tensor_copy(tiles_total[:, :], tiles_run[:, E - 1:E]),
                 nc.vector.tensor_tensor(slot[:, :, :], slot[:, :, :], within, ALU.add))
            step(nc.vector.tensor_copy(first_i[:, :], first_f[:, :]),
                 nc.vector.tensor_scalar(first_f[:, :], first_f[:, :], float(P), None, ALU.mult))
            step(nc.vector.tensor_tensor(slot[:, :, :], slot[:, :, :], first_f[:, :].unsqueeze(2).to_broadcast([P, E, TT]), ALU.add))
            step(*[nc.vector.tensor_tensor(picked[:, k, :, :], one_hot[:, k, :, :], slot[:, :, :].rearrange("p e t -> p t e"), ALU.mult)
                   for k in range(2)])
            step(nc.vector.reduce_sum(slot_f[:, :, :], picked[:, :, :, :], X))
            nc.vector.tensor_copy(slot_i[:, :, :], slot_f[:, :, :]).then_inc(slots_ready, 1)
            dve.wait_ge(exp_ready, 1)
            step(nc.vector.reduce_sum(exp_sum[:, :], exps[:, :, :], X))
            step(nc.vector.reciprocal(exp_sum[:, :], exp_sum[:, :]))
            step(nc.vector.tensor_tensor(picked[:, 1, :, :], one_hot[:, 1, :, :], exps[:, :, :], ALU.mult))
            step(nc.vector.reduce_sum(prob_step[:, :], picked[:, 1, :, :], X))
            step(nc.vector.tensor_tensor(prob_step[:, :], prob_step[:, :], exp_sum[:, :], ALU.mult))
            nc.vector.tensor_tensor(prob_step[:, :], prob_step[:, :], exp_sum[:, :], ALU.subtract).then_inc(step_ready, 1)
            dve.wait_ge(w_ready, 1)
            step(nc.vector.tensor_scalar(top_w[:, 1, :], prob_step[:, :], 1.0, None, ALU.add))
            step(nc.vector.reciprocal(top_w[:, 0, :], top_w[:, 1, :]))
            nc.vector.tensor_tensor(top_w[:, 1, :], top_w[:, 0, :], prob_step[:, :], ALU.mult).then_inc(slots_ready, 1)
            dve.wait_ge(slots_ready, 2)

            def copy_column(g):
                dve.wait_ge(t_full, g + 1)
                nc.vector.tensor_copy(x_col[:, :, :], t_bank[:, 0:D].rearrange("p (c t) -> p c t", c=DC)).then_inc(xcol_ready, 1)

            def copy_row(g):
                dve.wait_ge(x_in_slots, g * 16 + 16)
                dve.sem_inc(passed, 1)
                nc.vector.tensor_copy(x_row[:, :], x_slots[:, bass.ds(g, 1), :].rearrange("p o d -> p (o d)")).then_inc(row_ready, 1)

            copy_row(0)
            copy_column(0)
            copy_row(1)
            dve.wait_ge(moe_const, 32)
            with dve.Fori(0, E // 2) as pair:
                for i in range(2):
                    e = 2 * pair + i

                    def tile(g):
                        copy_column(g + 1)
                        copy_row(g + 2)
                        dve.wait_ge(y_full, g + 1)
                        nc.vector.tensor_tensor(y_slots[:, bass.ds(g, 1), :].rearrange("p o d -> p (o d)"), y_bank[:, 0:D], b2[:, bass.ds(e, 1), :].rearrange("p o d -> p (o d)"),
                                                ALU.add).then_inc(y_evac, 1)

                    expert_tiles(dve, e, tile)

            fin = [0]

            def fstep(*instructions):
                for ins in instructions:
                    ins.then_inc(fin_step, 1)
                    fin[0] += 1
                dve.wait_ge(fin_step, fin[0])

            for n in range(TT // QT):
                ts = range(n * QT, (n + 1) * QT)
                x2 = x2_all[:, n * QT:(n + 1) * QT, :]
                for t in ts:
                    dve.wait_ge(got[t], 32)
                for k in range(2):
                    fstep(*[nc.vector.scalar_tensor_tensor(out=x2_all[:, t, :], in0=y_got[:, t, k, :], scalar=top_w[:, k, t:t + 1],
                                                           in1=x2_all[:, t, :], op0=ALU.mult, op1=ALU.add) for t in ts])
                fstep(*[nc.vector.bn_stats(stats[:, t % QT, :], x2_all[:, t, :]) for t in ts])
                fstep(*[nc.vector.bn_aggr(mv[:, t % QT, :], stats[:, t % QT, :]) for t in ts])
                nc.vector.tensor_scalar(rstd[:, :], mv[:, :, 1], EPS, None, ALU.add).then_inc(var_ready, 1)
                dve.wait_ge(root_ready, n + 1)
                fstep(nc.vector.reciprocal(rstd[:, :], rstd[:, :]))
                fstep(*[nc.vector.tensor_scalar(x2_all[:, t, :], x2_all[:, t, :], mv[:, t % QT, 0:1], rstd[:, t % QT:t % QT + 1],
                                                ALU.subtract, ALU.mult) for t in ts])
                fstep(nc.vector.tensor_tensor(x2, x2, ln_gb[:, 4:5, :].to_broadcast([P, QT, D]), ALU.mult))
                nc.vector.tensor_tensor(x2, x2, ln_gb[:, 5:6, :].to_broadcast([P, QT, D]), ALU.add).then_inc(fin_ready, 1)


_INS = ["x", "xT", "ctxT"] + [f"{k}_{n}" for k in ("sa", "ca") for n in ("wq", "bq", "wk", "bk", "wv", "bv", "wo", "bo")] + [
    "ln1_g", "ln1_b", "ln2_g", "ln2_b", "ln3_g", "ln3_b", "router_w", "router_b", "e_w1", "e_b1", "e_w2", "e_b2"]


def kernel(**inputs):
    import numpy as _np
    import concourse.bacc as _bacc
    from concourse import mybir as _mybir
    from concourse.bass_utils import run_bass_kernel_spmd as _run

    given = {k.replace("L0_xattn_", ""): _np.asarray(v) for k, v in inputs.items()}
    x = given["x"].reshape(TOK, D)
    given["x"], given["xT"] = x, x.T
    given["ctxT"] = given.pop("ctx_1024").reshape(B * SE, D).T
    given["e_b1"] = given["e_b1"].reshape(E, FC, P).transpose(2, 0, 1).reshape(P, E * FC)
    nc = _bacc.Bacc("TRN2", target_bir_lowering=False, num_devices=1)
    arrays, aps = {}, {}
    for name in _INS:
        v = _np.ascontiguousarray(given[name])
        arrays[f"in_{name}"] = v
        aps[name] = nc.dram_tensor(f"in_{name}", v.shape, _mybir.dt.from_np(v.dtype), kind="ExternalInput").ap()
    out = nc.dram_tensor("out", (TOK, D), _mybir.dt.float32, kind="ExternalOutput").ap()
    decoder_layer(nc, aps, out)
    r = _run(nc, [arrays], core_ids=[0])
    return r.results[0]["out"].reshape(B, S, D)
```

```python
import concourse.bass as bass
from concourse import mybir
from contextlib import ExitStack

F32 = mybir.dt.float32
BF16 = mybir.dt.bfloat16
I32 = mybir.dt.int32
U32 = mybir.dt.uint32
ACT = mybir.ActivationFunctionType
ALU = mybir.AluOpType
X = mybir.AxisListType.X

P = 128
B, S, SE, D = 4, 512, 1024, 256
H, HD = 16, 16
E, FF = 8, 1024
DC, FC = D // P, FF // P
QT, ET = S // P, SE // P
TT = B * QT
TOK = B * S
G = 4
UNITS = H // G
EPS = 1e-5
NEG = -1e30
SCALE = HD ** -0.5
PARTS = 3
Q_PART = [0, 0, 0, 1, 1, 2]
K_PART = [0, 1, 2, 0, 1, 0]
NG = len(Q_PART)
KR = NG * HD
KM = KR + PARTS
SLOT_TILES = TOK * 2 // P + E
RING = 3
SPLITS = 10
CAP = TOK + P
ROW = D + 2
LAST_BATCH = TT - QT


def chosen(part):
    early = 2 * LAST_BATCH + 4
    return early if part == 1 else chosen(1) + placed(1) + 1 + 2 * QT + 4


def placed(part):
    return 9


class Count:

    def __init__(self, per, ring=1):
        self.n, self.per, self.pad = 0, per, -per % ring
        self.taken = 0
        self.register, self.end = None, None

    def at(self, k=0):
        return self.n + k if self.register is None else self.register * (self.per + self.pad) + (self.n + k)

    def turns(self, of, amount, k=0):
        n = amount * (self.n // of + k)
        return n if self.register is None else self.register * (self.per // of * amount) + n

    def next(self):
        self.n += 1
        self.taken += 1
        if self.n == self.end:
            self.n += self.pad
            return 1 + self.pad
        return 1

    def enter(self, register):
        self.register, self.end = register, self.n + self.per

    def leave(self, runs):
        assert self.n == self.end + self.pad, (self.n, self.end, self.pad)
        self.n += (runs - 1) * (self.per + self.pad)
        self.register, self.end = None, None


def counted(ev):
    k = ev[0]
    if k == "split":
        return ["v", "split", ("stack", ev[1])]
    if k == "score":
        kt, heads, last_of_tile = ev[3:]
        return ["a"] + (["tile"] if last_of_tile else []) + (["begun"] if kt == 0 and heads[0] == 0 else [])
    if k in ("turned", "add_bias", "experts_in", "constants", "rest_in", "cross_made", "choose"):
        return []
    return {"values": ["a"], "max": ["v"], "max_parts": ["step"] * 4, "max_rows": ["v", "rows"], "weigh": ["pv"],
            "o_out": ["unit"], "o_turn": ["v", "step"], "att_turn": ["a"] * DC, "norm_turn": ["a"] * DC,
            "out": ["v"] * (QT // 2), "stats": ["out"] + ["step"] * (2 * QT - 1), "norm": ["norm"], "route": ["v"], "place": ["v"],
            "load_x": ["load_x"], "load_ctx": ["load_ctx"], "load_res": ["load_res"]}[k]


class Counts:

    def __init__(self):
        names = ("v", "a", "split", "rows", "tile", "pv", "begun", "unit", "out", "norm", "step", "load_x", "load_ctx", "load_res") + tuple(
            ("stack", s) for s in range(SPLITS))
        per = {name: 0 for name in names}
        for ev in BODY:
            for name in counted(ev):
                per[name] += 1
        self.named = {name: Count(per[name], RING if name in ("v", "a") else 1) for name in names}
        self.v, self.a, self.step = self.named["v"], self.named["a"], self.named["step"]
        self.split, self.rows = self.named["split"], self.named["rows"]
        self.tile, self.pv = self.named["tile"], self.named["pv"]
        self.begun, self.unit = self.named["begun"], self.named["unit"]
        self.out, self.norm = self.named["out"], self.named["norm"]
        self.load_x, self.load_ctx, self.load_res = self.named["load_x"], self.named["load_ctx"], self.named["load_res"]
        self.stack = [self.named[("stack", s)] for s in range(SPLITS)]
        assert self.rows.per % AHEAD_ROWS == 0 and all(c.per % 2 == 0 for c in (self.split, self.tile, self.unit, self.pv))

    def do(self, step, ev, where):
        names = counted(ev)
        want = {name: self.named[name].taken + names.count(name) for name in names}
        step(ev, where)
        for name, n in want.items():
            while self.named[name].taken < n:
                self.named[name].next()
            assert self.named[name].taken == n, (ev, name)


class Where:

    def __init__(self, r):
        self.r = r


AHEAD_ROWS = 4
LOOPED = 2


def walk(eng, c, step):
    for ev in START:
        c.do(step, ev, Where(None))
    with eng.Fori(0, LOOPED) as r:
        for x in c.named.values():
            x.enter(r)
        for ev in BODY:
            c.do(step, ev, Where(r))
    for x in c.named.values():
        x.leave(LOOPED)
    for ev in REST:
        c.do(step, ev, Where(None))



def max_steps(kind, u):
    if kind:
        tiles = [("max", 1, u, (j,), q, half) for j in range(G) for q in range(QT) for half in range(2)]
    else:
        tiles = [("max", 0, u, tuple(range(G)), 0, 0)] + [("max", 0, u, (j, j + 1), 1, 0) for j in (0, 2)] + [
            ("max", 0, u, (j,), q, 0) for q in (2, 3) for j in range(G)]
    return tiles + [("max_parts", kind, u)]


def with_rows(items, after=2):
    out, due = [], []
    for it in items:
        out.append(it)
        due = [(n - 1, e) for n, e in due]
        while due and due[0][0] == 0:
            out.append(due.pop(0)[1])
        if it[0] == "max_parts":
            due.append((after, ("max_rows",) + it[1:]))
    return out + [e for _, e in due]


def score_steps(kind, u, kt):
    wide = 1 if kind or kt < 2 else 2 if kt == 2 else 4
    groups = [tuple(range(j, j + wide)) for j in range(0, G, wide)]
    return [("score", kind, u, kt, js, js == groups[-1]) for js in groups]


LEAD = 16
AHEAD = 6.0


def max_weight(ev):
    if ev[0] == "max_parts":
        return 2.0
    if ev[0] == "max_rows":
        return 0.5
    return 1.0 if ev[1] else 0.15 + len(ev[3]) * (ev[4] + 1) * P / 512


def attention_steps(units, pieces, maxima, held=3):
    seq = []
    weigh = None
    for n, (kind, u) in enumerate(units):
        turn = None
        for kt in range(ET if kind else QT):
            steps = score_steps(kind, u, kt)
            weight = (1.0 if kind else 1.0 - 0.2 * kt) * (4.0 / len(steps)) 
            for i, e in enumerate(steps):
                seq += [(x, 0) for x in pieces.get((n, kt, i), [])]
                seq.append((e, weight))
                if i == min(1, len(steps) - 1):
                    if turn and kt == 1:
                        seq.append((turn, 0))
                    if weigh:
                        seq += [(x, 0) for x in weigh]
                        if weigh[-1][0] == "o_out":
                            turn = ("o_turn",) + weigh[-1][1:]
            weigh = [("weigh", kind, u, kt)]
        weigh.append(("o_out", kind, u))
    own = maxima[:maxima.index(("max_rows", 1, 0))] if ("max_rows", 1, 0) in maxima else maxima
    t, starts = 0.0, []
    for e, x in seq:
        if e[0] == "score" and e[3] == 0 and e[4][0] == 0 and t > 0:
            starts.append((t, ("max_rows",) + e[1:3]))
        t += x
    cost = [max_weight(e) for e in maxima]
    upto = [sum(cost[:i + 1]) for i in range(len(cost))]
    due = [(max(s - AHEAD, 0.0), upto[maxima.index(e)]) for s, e in starts if e in own]
    due.append((t, upto[len(maxima) - held - 1]))
    out, now, cur, taken = [], 0.0, 0.0, 0
    for e, x in seq:
        if now > 0 and e[0] == "score" and e[3] == 0 and e[4][0] == 0 and ("max_rows",) + e[1:3] in own[taken:]:
            stop = taken + maxima[taken:].index(("max_rows",) + e[1:3]) + 1
            out += maxima[taken:stop]
            taken, cur = stop, max(cur, upto[stop - 1])
        out.append(e)
        rate = max((n - cur) / max(s - now, x, 1e-6) for s, n in due if n > cur or s == t)
        cur += max(rate, 0.0) * x
        now += x
        while taken < len(maxima) - held and upto[taken] <= cur + 1e-6:
            out.append(maxima[taken])
            taken += 1
    out += weigh + pieces.get("end", []) + maxima[taken:]
    return out + [("o_turn",) + weigh[-1][1:]]


SELF = [(0, u) for u in range(UNITS)]
CROSS = [(1, u) for u in range(UNITS)]


def fixed(b):
    return lambda r: b


SELF_IN = [("split", 0), ("split", 2), ("split", 1), ("split", 3), ("values", 0, 0), ("values", 0, 1)]


POS = {"q1": (0, 0, 3), "v3": (0, 1, 0), "att1": (0, 1, 0), "out1": (0, 2, 0), "stats1": (0, 3, 0),
       "k2": (0, 3, 0), "norm1": (0, 4, 0), "k3": (0, 5, 0), "turn1": (0, 5, 2), "route": (0, 7, 0),
       "bias": (2, 0, 0), "att0": (0, 2, 0), "out0": (0, 3, 0), "stats0": (0, 3, 0), "norm0": (0, 5, 0),
       "turn0": (0, 7, 0), "q0": (1, 0, 0), "k0": (1, 1, 0), "k1": (1, 1, 0), "s0": (1, 4, 0), "s2": (1, 5, 0),
       "s1": (1, 6, 0), "s3": (1, 7, 0), "sv0": (2, 0, 0), "sv1": (2, 1, 0), "v0": (2, 3, 0), "v1": (2, 5, 0),
       "v2": (2, 6, 2)}
AFTER_SELF = ("att0", "out0", "stats0", "norm0", "turn0", "q0", "k0", "k1", "s0", "s1", "s2", "s3", "sv0", "sv1", "v0", "v1", "v2")


def make_steps():
    first_max = with_rows([e for u in range(UNITS) for e in max_steps(0, u)])
    per_batch = [e for k, u in SELF + CROSS[1:] + CROSS[:1] for e in max_steps(k, u)]
    all_max = with_rows(max_steps(1, 0) + per_batch * (B - 1) + [e for u in range(1, UNITS) for e in max_steps(1, u)])
    per = len(per_batch) + len(SELF + CROSS)
    cut = len(max_steps(1, 0)) + 1 + LEAD
    start = [("load_x", fixed(0)), ("load_ctx", fixed(0)), ("load_res", fixed(0))] + SELF_IN + [("constants",), ("load_x", fixed(1))]
    early = len(max_steps(0, 0)) + 5
    start += first_max[:early] + [("rest_in",), ("add_bias",)]
    pieces = {(0, 1, 0): [("split", 4)], (0, 2, 0): [("split", 5)], (1, 0, 0): [("values", 1, 0)], (1, 2, 0): [("values", 1, 1)],
              (2, 0, 0): [("values", 1, 2)]}
    start += attention_steps(SELF, pieces, first_max[early:], held=0)
    start += [("cross_made",), ("att_turn", 0), ("split", 0), ("out", 0), ("stats", 0), ("load_res", fixed(1)), ("split", 2), ("norm", 0, fixed(0), True), ("norm_turn", 0), ("turned",),
              ("split", 8), ("split", 1), ("split", 3), ("values", 0, 0), ("values", 0, 1)] + all_max[:cut]

    def run(with_self, maxima, self_next, c_tile, s_tile, loads):
        units = CROSS[:1] + (SELF if with_self else []) + CROSS[1:]
        u1 = 1 + (UNITS if with_self else 0)
        p = {}

        def put(n, kt, i, *e):
            p.setdefault((n, kt, i), []).extend(e)

        def at(name):
            n, *rest = POS[name]
            return (n + (u1 if name in AFTER_SELF else 0), *rest)

        put(*at("q1"), ("split", 9))
        put(*at("v3"), ("values", 1, 3))
        put(*at("att1"), *loads["x"])
        put(*at("att1"), ("att_turn", 1))
        put(*at("out1"), ("out", 1, c_tile))
        put(*at("stats1"), ("stats", 1))
        put(*at("norm1"), ("norm", 1, c_tile, False))
        put(*at("turn1"), ("norm_turn", 1))
        put(*at("route"), ("turned",), ("route", c_tile))
        if with_self:
            put(*at("k2"), ("split", 6))
            put(*at("k3"), ("split", 7), *loads["ctx"])
            put(*at("bias"), ("add_bias",))
            put(*at("att0"), ("att_turn", 0))
            put(*at("out0"), ("out", 0))
            put(*at("stats0"), ("stats", 0), *loads["res"])
            put(*at("norm0"), ("norm", 0, s_tile, False))
            put(*at("turn0"), ("norm_turn", 0))
            put(*at("q0"), ("turned",), ("split", 8))
            put(*at("k0"), ("split", 4))
            put(*at("k1"), ("split", 5))
            if self_next:
                for name, e in (("s0", ("split", 0)), ("s2", ("split", 2)), ("s1", ("split", 1)), ("s3", ("split", 3)),
                                ("sv0", ("values", 0, 0)), ("sv1", ("values", 0, 1))):
                    put(*at(name), e)
            put(*at("v0"), ("values", 1, 0))
            put(*at("v1"), ("values", 1, 1))
            put(*at("v2"), ("values", 1, 2))
        else:
            put(0, 1, 2, ("split", 6))
            put(0, 2, 0, ("split", 7))
            put(0, 2, 2, ("experts_in",))
            put(1, 1, 0, ("choose",))
            put(1, 3, 0, ("place",))
        return attention_steps(units, p, maxima, held=3 if with_self else 0)

    body = run(True, all_max[cut:cut + per], True,
               lambda r: (B - 1) - r * (B - 1),
               lambda r: r + 1,
               {"x": [("load_x", lambda r: r + 2)], "ctx": [("load_ctx", lambda r: r + 1)], "res": [("load_res", lambda r: r + 2)]})
    assert all_max[cut:cut + per] == all_max[cut + per:cut + 2 * per]
    at = cut + 2 * per
    end = at + per
    rest = run(True, all_max[at:end], False, fixed(1), fixed(3),
               {"x": [], "ctx": [("load_ctx", fixed(3))], "res": []})
    rest += run(False, all_max[end:], False, fixed(2), None, {"x": [], "ctx": [], "res": []})
    rest += [("att_turn", 1), ("out", 1, fixed(3)), ("stats", 1), ("norm", 1, fixed(3), True), ("norm_turn", 1), ("turned",), ("route", fixed(3))]
    return start, body, rest


START, BODY, REST = make_steps()


def decoder_layer(nc, a, out):
    ctx = ExitStack()
    with ctx:
        def sb(name, shape, dt=F32):
            return ctx.enter_context(nc.sbuf_tensor(name, shape, dt))

        def sem(name):
            return ctx.enter_context(nc.semaphore(name))

        parts_dram = nc.dram_tensor("parts_scratch", (SPLITS, PARTS, P, S), BF16).ap()
        max_dram = nc.dram_tensor("max_scratch", (2, PARTS, G * S), BF16).ap()
        slots_dram = nc.dram_tensor("slots_in", (E * CAP, ROW), F32).ap()
        y_dram = nc.dram_tensor("token_out", (3 * TOK + P, D), F32).ap()

        x2_all = sb("x2_all", [P, TT, ROW])
        top_val = sb("top_val", [P, TT, 8])
        expert_no = sb("expert_no", [P, E])
        expert_row = sb("expert_row", [P, E])
        expert_end = sb("expert_end", [P, E])
        expert_i = sb("expert_i", [P, E], I32)
        token_i = sb("token_i", [P, TT], I32)
        big = [sb(f"stack_or_weights{i}", [P, 2, DC * FF]) for i in range(2)]
        w1 = [t[:, 0, :].rearrange("p (c n) -> p c n", c=DC) for t in big]
        w2 = [t[:, 1, :].rearrange("p (c n) -> p c n", c=FC) for t in big]
        before_b = sb("before_b", [P, P], BF16)
        ones_b = sb("ones_b", [P, P], BF16)
        logits = sb("logits", [P, TT, E])
        ident = sb("ident", [P, P])
        ident_b = sb("ident_b", [P, P], BF16)
        ln_gb = sb("ln_gb", [P, 6, D])
        stats = sb("stats", [P, QT, 6])
        mv = sb("mv", [P, QT, 2])
        rstd = sb("rstd", [P, QT])
        neg_half = sb("neg_half", [P, QT])
        router_b = sb("router_b", [P, E])

        v_bank = [ctx.enter_context(nc.psum_tensor(f"v_bank{i}", [P, 512], F32)) for i in range(RING)]
        a_bank = [ctx.enter_context(nc.psum_tensor(f"a_bank{i}", [P, 512], F32)) for i in range(RING)]
        o_bank = [ctx.enter_context(nc.psum_tensor(f"o_bank{i}", [P, 512], F32)) for i in range(2)]

        first_in = sem("first_in")
        const_in = sem("const_in")
        const_made = sem("const_made")
        const_cast = sem("const_cast")
        w_in = [sem("w_in0"), sem("w_in1")]
        route = sem("route")
        rank_full = sem("rank_full")
        slots_ready = sem("slots_ready")
        scattered = sem("scattered")
        xt_in, ctx_in, x_in = sem("xt_in"), sem("ctx_in"), sem("x_in")
        v_full, v_free = sem("v_full"), sem("v_free")
        a_full, a_free = sem("a_full"), sem("a_free")
        high_done = sem("high_done")
        split_done = sem("split_done")
        part_out = [sem("part_out0"), sem("part_out1")]
        stack_in = [sem(f"stack_in{s}") for s in range(SPLITS)]
        maxp_ready = sem("maxp_ready")
        maxt_out = sem("maxt_out")
        max_in = [sem(f"max_in{i}") for i in range(AHEAD_ROWS)]
        pv_done = sem("pv_done")
        o_out = sem("o_out")
        mean_ready, rstd_ready = sem("mean_ready"), sem("rstd_ready")
        y_ready = sem("y_ready")
        middle_done = sem("middle_done")
        bias_added = sem("bias_added")
        centred, scaled = sem("centred"), sem("scaled")
        kept = sem("kept")
        dve_step = sem("dve_step")
        pool_step = sem("pool_step")
        passed = sem("passed")

        att_ctx = ExitStack()

        def sba(name, shape, dt=F32):
            return att_ctx.enter_context(nc.sbuf_tensor(name, shape, dt))

        w = {n: sba("w_" + n, [P, DC, D]) for n in ("sa_wq", "sa_wk", "sa_wv", "sa_wo", "ca_wq", "ca_wk", "ca_wv", "ca_wo")}
        router_w = sba("w_router", [P, DC, E])
        bias = {n: sba("b_" + n, [P, DC]) for n in ("sa_bq", "sa_bk", "sa_bv", "ca_bq", "ca_bk", "ca_bv")}
        out_b = sba("out_b", [P, 2, D])
        mask_q = sba("mask_q", [P, P], BF16)
        mask_k = sba("mask_k", [P, P], BF16)
        xt = sba("xt", [P, DC, S])
        ctxt = sba("ctxt", [P, DC, SE])
        xres = sba("xres", [P, QT, D])
        parts = [sba(f"parts{i}", [P, PARTS, S], BF16) for i in range(2)]
        rest = [sba(f"rest{i}", [P, S]) for i in range(2)]
        self_stacks = [t[:, :, :].rearrange("p o n -> p (o n)").bitcast(BF16).rearrange("p (h t) -> p h t", h=H) for t in big]
        q_stack = [self_stacks[0], sba("q_stack_cross", [P, H, S], BF16)]
        k_stack = [self_stacks[1], sba("k_stack_cross", [P, H, SE], BF16)]
        v_ext = [sba("v_self", [P, QT, H, 2 * HD]), sba("v_cross", [P, ET, H, 2 * HD])]
        probs = [sba(f"probs{i}", [P, G, S]) for i in range(2)]
        o_sb = [sba(f"o_sb{i}", [P, S]) for i in range(2)]
        y = [sba("y_self", [P, QT, D]), sba("y_cross", [P, QT, D])]
        o_t = sba("o_t", [P, DC, S])
        max_raw = sba("max_raw", [P, G, QT, 2])
        max_q = sba("max_q", [P, G * QT])
        max_r = sba("max_r", [P, G * QT])
        max_p = sba("max_p", [P, PARTS, G * QT], BF16)
        max_t = sba("max_t", [PARTS * G * QT, P], BF16)
        recip = sba("recip", [P, QT, G])

        blocks = ExitStack()
        block = blocks.enter_context(nc.Block())
        xt_d = a["xT"].rearrange("(c p) t -> p c t", p=P)
        ctx_d = a["ctxT"].rearrange("(c p) t -> p c t", p=P)
        x_d = a["x"].rearrange("(t p) d -> p t d", p=P)
        FIRST_LOADS = 3 + 6
        N_LOADS = 5 + 1 + 2 + 6 + 1

        def split_target(s):
            if s in (0, 1, 8, 9):
                return q_stack[s // 8], 8 * (s % 2), 0, Q_PART
            if s in (2, 3):
                return k_stack[0], 8 * (s % 2), 0, K_PART
            return k_stack[1], 8 * ((s - 4) // 2), S * (s % 2), K_PART

        def projection(s):
            if s < 2:
                return "sa_wq", xt, "sa_bq", s, 0
            if s < 4:
                return "sa_wk", xt, "sa_bk", s - 2, 0
            if s < 8:
                return "ca_wk", ctxt, "ca_bk", (s - 4) // 2, S * (s % 2)
            return "ca_wq", o_t, "ca_bq", s - 8, 0

        def load_weights(sp, e, i):
            sp.dma_start(w1[i][:, :, :], a["e_w1"][bass.ds(e, 1)].rearrange("o (c p) n -> p (o c) n", p=P)).then_inc(w_in[i], 16)
            sp.dma_start(w2[i][:, :, :], a["e_w2"][bass.ds(e, 1)].rearrange("o (c p) n -> p (o c) n", p=P)).then_inc(w_in[i], 16)

        ONE_PAIR = float.fromhex("0x1.007f000000000p+0")

        def ones_rows(stack):
            return stack[KR:KM, :, :].rearrange("p h t -> p (h t)").bitcast(F32)

        class Routing:

            def __init__(self, space, t0, t1):
                n = t1 - t0
                self.t0, self.n, self.used, self.space = t0, n, 0, space
                self.top_idx = self.take(n * 8).bitcast(U32).rearrange("p (t e) -> p t e", e=8)
                self.idx_f = self.take(2 * n).rearrange("p (k t) -> p k t", k=2)
                self.one_hot = self.take(2 * n * E).rearrange("p (k t e) -> p k t e", k=2, e=E)
                self.taken = self.take(n * E // 2).bitcast(BF16)
                self.segment, self.total, self.running, self.slot = (self.take(n * E).rearrange("p (e t) -> p e t", e=E) for _ in range(4))
                self.picked = self.take(2 * n * E).rearrange("p (k t e) -> p k t e", k=2, e=E)
                self.slot_f = self.take(2 * n).rearrange("p (k t) -> p k t", k=2)
                self.slot_i = self.take(2 * n).bitcast(U32).rearrange("p (k t) -> p k t", k=2)

            def take(self, n):
                self.used += n
                return self.space[:, self.used - n:self.used]

            def choose(self, step):
                t0, n, vec = self.t0, self.n, nc.vector
                step(*[vec.max(top_val[:, t0 + t, :], logits[:, t0 + t, :]) for t in range(n)], vec.memset(self.segment, 1.0))
                step(*[vec.max_index(self.top_idx[:, t, :], top_val[:, t0 + t, :], logits[:, t0 + t, :]) for t in range(n)])
                step(vec.tensor_copy(self.idx_f, self.top_idx[:, :, 0:2].rearrange("p t k -> p k t")))
                step(vec.tensor_tensor(self.one_hot, self.idx_f.unsqueeze(3).to_broadcast([P, 2, n, E]),
                                       expert_no[:, :].unsqueeze(1).unsqueeze(1).to_broadcast([P, 2, n, E]), ALU.is_equal))
                step(vec.tensor_tensor(self.taken, self.one_hot[:, 0].rearrange("p t e -> p (t e)"),
                                       self.one_hot[:, 1].rearrange("p t e -> p (t e)"), ALU.add))

            def rank(self, bank):
                m = self.n * E
                nc.tensor.matmul(bank[:, 0:m], before_b[:, :], self.taken, start=True, stop=True)
                return nc.tensor.matmul(bank[:, m:2 * m], ones_b[:, :], self.taken, start=True, stop=True)

            def place(self, step, bank):
                n, m, vec = self.n, self.n * E, nc.vector
                within, totals = (bank[:, i * m:(i + 1) * m].rearrange("p (t e) -> p e t", e=E) for i in range(2))
                step(vec.tensor_copy(self.total, totals), vec.memset(self.segment[:, :, 0:1], 0.0))
                step(vec.tensor_tensor_scan(out=self.running.rearrange("p e t -> p (e t)"), data0=self.segment.rearrange("p e t -> p (e t)"),
                                            data1=self.total.rearrange("p e t -> p (e t)"), initial=0.0, op0=ALU.mult, op1=ALU.add))
                step(vec.tensor_tensor(self.slot, self.running, self.total, ALU.subtract))
                step(vec.tensor_tensor(self.slot, self.slot, within, ALU.add))
                step(vec.tensor_tensor(self.slot, self.slot, expert_end[:, :].unsqueeze(2).to_broadcast([P, E, n]), ALU.add))
                step(vec.tensor_tensor(self.picked, self.one_hot, self.slot.rearrange("p e t -> p t e").unsqueeze(1).to_broadcast([P, 2, n, E]),
                                       ALU.mult),
                     vec.tensor_tensor(expert_end[:, :], expert_end[:, :], self.running[:, :, n - 1], ALU.add))
                step(vec.reduce_sum(self.slot_f, self.picked, X))
                vec.tensor_copy(x2_all[:, self.t0:self.t0 + n, D + 1], self.idx_f[:, 0, :]).then_inc(slots_ready, 1)
                return vec.tensor_copy(self.slot_i, self.slot_f)

        early = Routing(xres[:, :, :].rearrange("p q d -> p (q d)"), 0, LAST_BATCH)

        CASTS = 8

        @block.sync
        def _(sp):
            for n in ("sa_wq", "sa_wk", "sa_wv"):
                sp.dma_start(w[n][:, :, :], a[n].rearrange("(c p) n -> p c n", p=P)).then_inc(first_in, 16)
            with nc.allow_non_contiguous_dma(reason="six columns of 256 numbers"):
                for n, t in bias.items():
                    sp.dma_start(t[:, :], a[n].rearrange("(c p) -> p c", p=P)).then_inc(first_in, 16)
            for n in ("ca_wk", "ca_wv", "sa_wo", "ca_wq", "ca_wo"):
                sp.dma_start(w[n][:, :, :], a[n].rearrange("(c p) n -> p c n", p=P)).then_inc(const_in, 16)
            sp.dma_start(router_w[:, :, :], a["router_w"].rearrange("(c p) n -> p c n", p=P)).then_inc(const_in, 16)
            for i, n in enumerate(("sa_bo", "ca_bo")):
                sp.dma_start(out_b[:, i, :], a[n].rearrange("(o n) -> o n", o=1).to_broadcast([P, D])).then_inc(const_in, 16)
            for i, n in enumerate(("ln1_g", "ln1_b", "ln2_g", "ln2_b", "ln3_g", "ln3_b")):
                sp.dma_start(ln_gb[:, i, :], a[n].rearrange("(o n) -> o n", o=1).to_broadcast([P, D])).then_inc(const_in, 16)
            sp.dma_start(router_b[:, :], a["router_b"].rearrange("(o n) -> o n", o=1).to_broadcast([P, E])).then_inc(const_in, 16)
            for i in range(2):
                sp.sem_inc(part_out[i], 16)
            sp.sem_inc(maxt_out, 16)
            c = Counts()

            def step(ev, where):
                k, args = ev[0], ev[1:]
                if k == "split":
                    s = args[0]
                    i, stored = c.split.n % 2, c.split.turns(2, 16, 1) + 16
                    c.split.next()
                    sp.wait_ge(split_done, c.split.at())
                    sp.dma_start(parts_dram[s].rearrange("j p t -> p j t"), parts[i][:, :, :]).then_inc(part_out[i], 16)
                    sp.wait_ge(part_out[i], stored)
                    sp.sem_inc(passed, 1)
                    if c.pv.n:
                        sp.wait_ge(pv_done, c.pv.at(2))
                    stack, h0, t0, which = split_target(s)
                    for g in range(NG):
                        sp.dma_start(stack[HD * g:HD * (g + 1), h0:h0 + 8, t0:t0 + S],
                                     parts_dram[s, which[g]].rearrange("(h r) t -> r h t", r=HD)).then_inc(stack_in[s], 16)
                elif k == "experts_in":
                    sp.wait_ge(pv_done, c.pv.at(2))
                    for i in range(2):
                        load_weights(sp, i, i)
                elif k == "max_rows":
                    kind, u = args
                    c.v.next()
                    i, n = c.rows.n % 2, c.rows.n % AHEAD_ROWS
                    c.rows.next()
                    sp.wait_ge(v_free, c.v.at(RING))
                    sp.dma_start(max_dram[i].rearrange("j (c t) -> (j c) t", t=P), max_t[:, :]).then_inc(maxt_out, 16)
                    sp.wait_ge(maxt_out, c.rows.at() * 16 + 16)
                    sp.dma_start(q_stack[kind][KR:KM, G * u:G * (u + 1), :].rearrange("p h t -> p (h t)"), max_dram[i]).then_inc(max_in[n], 16)
            walk(sp, c, step)

        @block.gpsimd
        def _(pool):
            c = Counts()

            def step(ev, where):
                k, args = ev[0], ev[1:]
                if k == "stats":
                    c.out.next()
                if k == "load_x":
                    if c.v.n:
                        pool.wait_ge(v_full, c.v.at())
                        pool.wait_ge(a_full, c.a.at())
                    pool.dma_start(xt[:, :, :], xt_d[:, :, bass.ds(args[0](where.r) * S, S)]).then_inc(xt_in, 16)
                elif k == "load_ctx":
                    if c.v.n:
                        pool.wait_ge(v_full, c.v.at())
                        pool.wait_ge(a_full, c.a.at())
                    pool.dma_start(ctxt[:, :, :], ctx_d[:, :, bass.ds(args[0](where.r) * SE, SE)]).then_inc(ctx_in, 16)
                elif k == "constants":
                    nc.gpsimd.memset(y[1][:, :, :], 0.0).then_inc(const_made, 1)
                    nc.gpsimd.memset(neg_half[:, :], -0.5).then_inc(const_made, 1)
                    nc.gpsimd.memset(ident[:, :], 0.0).then_inc(const_made, 1)
                    nc.gpsimd.memset(mask_q[:, :], 0.0).then_inc(const_made, 1)
                    nc.gpsimd.memset(mask_k[:, :], 0.0).then_inc(const_made, 1)
                    nc.gpsimd.memset(before_b[:, :], 1.0).then_inc(const_made, 1)
                    nc.gpsimd.memset(ones_b[:, :], 1.0).then_inc(const_made, 1)
                    nc.gpsimd.iota(expert_i[:, :], [[1, E]], base=0, channel_multiplier=0).then_inc(const_made, 1)
                    nc.gpsimd.iota(token_i[:, :], [[P, TT]], base=0, channel_multiplier=1).then_inc(const_made, 1)
                    pool.wait_ge(const_made, 9)
                    nc.gpsimd.affine_select(out=ident[:, :], in_=ident[:, :], compare_op=ALU.not_equal, fill=1.0, base=0,
                                            pattern=[[-1, P]], channel_multiplier=1).then_inc(const_made, 1)
                    nc.gpsimd.affine_select(out=mask_q[:, :], in_=mask_q[:, :], compare_op=ALU.is_ge, fill=NEG, base=0,
                                            pattern=[[-1, P]], channel_multiplier=1).then_inc(const_made, 1)
                    nc.gpsimd.affine_select(out=mask_k[:, :], in_=mask_k[:, :], compare_op=ALU.is_ge, fill=NEG, base=0,
                                            pattern=[[1, P]], channel_multiplier=-1).then_inc(const_made, 1)
                    nc.gpsimd.affine_select(out=before_b[:, :], in_=before_b[:, :], compare_op=ALU.is_gt, fill=0.0, base=0,
                                            pattern=[[1, P]], channel_multiplier=-1).then_inc(const_made, 1)
                    pool.wait_ge(const_made, 13)
                    nc.gpsimd.memset(ones_rows(k_stack[1]), ONE_PAIR).then_inc(const_made, 1)
                    pool.wait_ge(const_made, 14)
                    nc.gpsimd.memset(v_ext[1][:, :, :, HD:HD + 1], 1.0).then_inc(const_made, 1)
                    nc.gpsimd.memset(v_ext[1][:, :, :, HD + 1:], 0.0).then_inc(const_made, 1)
                    nc.gpsimd.memset(x2_all[:, TT - QT:TT, 0:D], 0.0).then_inc(const_made, 1)
                elif k == "place":
                    pool.wait_ge(slots_ready, 2)
                    pool.wait_ge(kept, c.norm.at())
                    for t in range(LAST_BATCH):
                        for kk in range(2):
                            pool.indirect_dma_start(out=slots_dram, out_offset=bass.IndirectOffsetOnAxis(ap=early.slot_i[:, kk, t:t + 1], axis=0),
                                                    in_=x2_all[:, t, :], in_offset=None).then_inc(scattered, 16)
                    pool.wait_ge(scattered, 16 * 2 * LAST_BATCH)
                elif k == "split":
                    i = c.split.n % 2
                    c.split.next()
                    pool.wait_ge(middle_done, c.split.at())
                    nc.gpsimd.tensor_tensor(parts[i][:, 2, :], rest[i][:, :], parts[i][:, 1, :], ALU.subtract).then_inc(split_done, 1)
                elif k == "rest_in":
                    pool.wait_ge(const_in, 16 * N_LOADS)
                elif k == "add_bias":
                    pool.wait_ge(x_in, c.load_res.at() * 16)
                    nc.gpsimd.tensor_tensor(xres[:, :, :], xres[:, :, :], out_b[:, 0:1, :].to_broadcast([P, QT, D]), ALU.add).then_inc(bias_added, 1)
                elif k == "norm" and not args[2]:
                    kind, tile = args[0], args[1](where.r)
                    yk = y[kind]
                    c.norm.next()
                    gam, bet = (ln_gb[:, 2 * kind + i:2 * kind + i + 1, :].to_broadcast([P, QT, D]) for i in range(2))
                    pool.wait_ge(centred, c.norm.at() * QT)
                    nc.gpsimd.tensor_tensor(yk[:, :, :], yk[:, :, :], gam, ALU.mult).then_inc(scaled, 1)
                    pool.wait_ge(scaled, c.norm.at())
                    nc.gpsimd.tensor_tensor(yk[:, :, :], yk[:, :, :], bet, ALU.add).then_inc(y_ready, 1)
                    pool.wait_ge(y_ready, c.norm.at())
                    pool.sem_inc(passed, 1)
                    dst = x2_all[:, bass.ds(tile * QT, QT), 0:D]
                    if kind:
                        nc.gpsimd.tensor_copy(dst, yk[:, :, :]).then_inc(kept, 1)
                    else:
                        nc.gpsimd.tensor_tensor(dst, yk[:, :, :], out_b[:, 1:2, :].to_broadcast([P, QT, D]), ALU.add).then_inc(kept, 1)
                elif k == "load_res":
                    pool.dma_start(xres[:, :, :], x_d[:, bass.ds(args[0](where.r) * QT, QT), :]).then_inc(x_in, 16)
                elif k == "stats":
                    pool.wait_ge(mean_ready, c.out.at())
                    pool.sem_inc(passed, 1)
                    nc.gpsimd.tensor_scalar(rstd[:, :], mv[:, :, 1], EPS, None, ALU.add).then_inc(pool_step, 1)
                    pool.wait_ge(pool_step, c.out.at())
                    nc.gpsimd.tensor_tensor(rstd[:, :], rstd[:, :], neg_half[:, :], ALU.pow).then_inc(rstd_ready, 1)

            walk(pool, c, step)

        @block.tensor
        def _(pe):
            pe.wait_ge(first_in, 16 * FIRST_LOADS)
            pe.sem_inc(pv_done, 2)
            c = Counts()
            probs_ready = []

            def v_next():
                pe.wait_ge(v_free, c.v.at(1))
                bank = v_bank[c.v.n % RING]
                return bank, c.v.next()

            def a_next():
                pe.wait_ge(a_free, c.a.at(1))
                bank = a_bank[c.a.n % RING]
                return bank, c.a.next()

            def transpose_y(kind):
                for ch in range(DC):
                    bank, n = a_next()
                    for q in range(QT):
                        last = nc.tensor.transpose(bank[:, q * P:(q + 1) * P], y[kind][:, q, ch * P:(ch + 1) * P], ident[:, :])
                    last.then_inc(a_full, n)

            def stacks_ready(kind, u):
                for s in ((u // 2, 2 + u // 2) if kind == 0 else (4 + 2 * (u // 2), 5 + 2 * (u // 2), 8 + u // 2)):
                    pe.wait_ge(stack_in[s], c.stack[s].at() * (16 * NG))

            def step(ev, where):
                k, args = ev[0], ev[1:]
                if k == "split":
                    s = args[0]
                    wname, src, _, ch, t0 = projection(s)
                    if s == 0:
                        pe.wait_ge(xt_in, c.load_x.at() * 16)
                    elif s == 4:
                        pe.wait_ge(ctx_in, c.load_ctx.at() * 16)
                    bank, n = v_next()
                    for kk in range(DC):
                        last = nc.tensor.matmul(bank[:, :], w[wname][:, kk, ch * P:(ch + 1) * P], src[:, kk, t0:t0 + S],
                                                start=(kk == 0), stop=(kk == DC - 1))
                    last.then_inc(v_full, n)
                    c.stack[s].next()
                elif k == "values":
                    kind, pair = args
                    src, wname = (ctxt, "ca_wv") if kind else (xt, "sa_wv")
                    bank, n = a_next()
                    for i in range(2):
                        t = 2 * pair + i
                        for kk in range(DC):
                            last = nc.tensor.matmul(bank[:, i * D:(i + 1) * D], src[:, kk, t * P:(t + 1) * P], w[wname][:, kk, :],
                                                    start=(kk == 0), stop=(kk == DC - 1))
                    last.then_inc(a_full, n)
                elif k == "max":
                    kind, u, js, q, half = args
                    if js[0] == 0 and q == 0:
                        stacks_ready(kind, u)
                    bank, inc = v_next()
                    for i, j in enumerate(js):
                        lhs = q_stack[kind][0:KR, G * u + j, q * P:(q + 1) * P]
                        if kind:
                            last = nc.tensor.matmul(bank[:, :], lhs, k_stack[1][0:KR, G * u + j, half * S:(half + 1) * S], start=True, stop=True)
                        else:
                            n = (q + 1) * P
                            nc.tensor.matmul(bank[:, i * n:(i + 1) * n], lhs, k_stack[0][0:KR, G * u + j, 0:n], start=True, stop=False)
                            last = nc.tensor.matmul(bank[:, (i + 1) * n - P:(i + 1) * n], ident_b[:, :], mask_q[:, :], start=False, stop=True)
                    last.then_inc(v_full, inc)
                elif k == "max_rows":
                    bank, n = v_next()
                    c.rows.next()
                    pe.wait_ge(maxp_ready, c.rows.at())
                    pe.sem_inc(passed, 1)
                    nc.tensor.transpose(bank[0:PARTS * G * QT, 0:P // 2].bitcast(BF16), max_p[:, :, :].rearrange("p j c -> p (j c)"),
                                        ident_b[:, :]).then_inc(v_full, n)
                elif k == "score":
                    kind, u, kt, js, last_of_tile = args
                    if kt == 0 and js[0] == 0:
                        pe.wait_ge(max_in[c.begun.n % AHEAD_ROWS], c.begun.turns(AHEAD_ROWS, 16, 1))
                    bank, inc = a_next()
                    q0 = 0 if kind else kt * P
                    n = S - q0
                    for i, j in enumerate(js):
                        lhs = k_stack[kind][0:KM, G * u + j, kt * P:(kt + 1) * P]
                        last = nc.tensor.matmul(bank[:, i * n:(i + 1) * n], lhs, q_stack[kind][0:KM, G * u + j, q0:S],
                                                start=True, stop=bool(kind))
                        if kind == 0:
                            last = nc.tensor.matmul(bank[:, i * n:i * n + P], ident_b[:, :], mask_k[:, :], start=False, stop=True)
                    last.then_inc(a_full, inc)
                    if last_of_tile:
                        probs_ready.append(c.a.at(RING))
                elif k == "weigh":
                    kind, u, kt = args
                    o = o_bank[c.unit.n % 2]
                    q0 = 0 if kind else kt * P
                    if kt == 0:
                        pe.wait_ge(o_out, c.unit.at(1))
                    pe.wait_ge(a_free, probs_ready.pop(0))
                    for j in range(G):
                        last = nc.tensor.matmul(o[32 * j:32 * (j + 1), q0:S], v_ext[kind][:, kt, G * u + j, :], probs[c.pv.n % 2][:, j, q0:S],
                                                start=(kt == 0), stop=(kt == (ET if kind else QT) - 1))
                    last.then_inc(pv_done, 1)
                    c.pv.next()
                elif k == "o_turn":
                    bank, n = v_next()
                    pe.wait_ge(o_out, c.unit.at(2))
                    for q in range(QT):
                        last = nc.tensor.transpose(bank[:, q * P:(q + 1) * P], o_sb[(c.unit.n - 1) % 2][:, q * P:(q + 1) * P], ident[:, :])
                    last.then_inc(v_full, n)
                elif k == "att_turn":
                    pe.wait_ge(v_free, c.v.at(RING))
                    transpose_y(args[0])
                elif k == "out":
                    kind = args[0]
                    pe.wait_ge(a_free, c.a.at(RING))
                    for pair in range(QT // 2):
                        bank, n = v_next()
                        for i in range(2):
                            t = 2 * pair + i
                            for kk in range(DC):
                                last = nc.tensor.matmul(bank[:, i * D:(i + 1) * D], o_t[:, kk, t * P:(t + 1) * P],
                                                        w["ca_wo" if kind else "sa_wo"][:, kk, :], start=(kk == 0), stop=(kk == DC - 1))
                        last.then_inc(v_full, n)
                elif k == "norm_turn":
                    pe.wait_ge(y_ready, c.norm.at())
                    transpose_y(args[0])
                    norm_in_o_t = c.a.at(RING)
                    follow_up.append(norm_in_o_t)
                elif k == "turned":
                    pe.wait_ge(a_free, follow_up.pop())
                elif k == "constants":
                    pe.wait_ge(const_made, 13)
                    pe.wait_ge(const_cast, 1)
                elif k == "rest_in":
                    pe.wait_ge(const_in, 16 * N_LOADS)
                    pe.wait_ge(const_cast, CASTS)
                elif k == "cross_made":
                    pe.wait_ge(const_made, 17)
                elif k == "place":
                    bank, n = v_next()
                    pe.wait_ge(route, chosen(1))
                    early.rank(bank).then_inc(v_full, n)
                elif k == "route":
                    bank, n = v_next()
                    for q in range(QT):
                        for kk in range(DC):
                            last = nc.tensor.matmul(bank[:, q * E:(q + 1) * E], o_t[:, kk, q * P:(q + 1) * P], router_w[:, kk, :],
                                                    start=(kk == 0), stop=(kk == DC - 1))
                    last.then_inc(v_full, n)

            follow_up = []
            walk(pe, c, step)

        @block.scalar
        def _(sc):
            sc.wait_ge(first_in, 16 * FIRST_LOADS)
            sc.sem_inc(a_free, RING)
            sc.sem_inc(o_out, 2)
            c = Counts()

            def a_job():
                bank = a_bank[c.a.n % RING]
                n = c.a.next()
                sc.wait_ge(a_full, c.a.at())
                return bank, n

            def to_o_t(bname=None):
                for ch in range(DC):
                    bank, n = a_job()
                    kw = {"bias": bias[bname][:, ch:ch + 1]} if bname else {}
                    nc.scalar.activation(o_t[:, ch, :], bank[:, :], ACT.Identity, **kw).then_inc(a_free, n)

            def step(ev, where):
                k, args = ev[0], ev[1:]
                if k == "split":
                    _, _, bname, ch, _ = projection(args[0])
                    i = c.split.n % 2
                    sc.wait_ge(part_out[i], c.split.turns(2, 16) + 16)
                    c.split.next()
                    bank = v_bank[c.v.n % RING]
                    c.v.next()
                    sc.wait_ge(v_full, c.v.at())
                    nc.scalar.activation(parts[i][:, 0, :], bank[:, :], ACT.Identity, bias=bias[bname][:, ch:ch + 1]).then_inc(high_done, 1)
                elif k == "values":
                    kind, pair = args
                    bank, n = a_job()
                    nc.scalar.activation(v_ext[kind][:, 2 * pair:2 * pair + 2, :, 0:HD],
                                         bank[:, :].rearrange("p (t h d) -> p t h d", t=2, d=HD), ACT.Identity).then_inc(a_free, n)
                elif k == "score":
                    kind, u, kt, js, last_of_tile = args
                    q0 = 0 if kind else kt * P
                    if js[0] == 0:
                        sc.wait_ge(pv_done, c.tile.at(1))
                    bank, n = a_job()
                    nc.scalar.activation(probs[c.tile.n % 2][:, js[0]:js[-1] + 1, q0:S],
                                         bank[:, 0:len(js) * (S - q0)].rearrange("p (j t) -> p j t", j=len(js)), ACT.Exp,
                                         scale=SCALE).then_inc(a_free, n)
                    if last_of_tile:
                        c.tile.next()
                elif k == "o_out":
                    sc.wait_ge(pv_done, c.pv.at(2))
                    nc.scalar.activation(o_sb[c.unit.n % 2][:, :], o_bank[c.unit.n % 2][:, :], ACT.Identity).then_inc(o_out, 1)
                    c.unit.next()
                elif k == "att_turn":
                    to_o_t("ca_bv" if args[0] else "sa_bv")
                elif k == "norm_turn":
                    to_o_t()

            walk(sc, c, step)

        @block.vector
        def _(dve):
            dve.wait_ge(first_in, 16 * FIRST_LOADS)
            dve.sem_inc(v_free, RING)
            c = Counts()

            def own(*instructions):
                for ins in instructions:
                    ins.then_inc(dve_step, 1)
                    c.step.next()
                dve.wait_ge(dve_step, c.step.at())

            def v_job():
                bank = v_bank[c.v.n % RING]
                n = c.v.next()
                dve.wait_ge(v_full, c.v.at())
                return bank, n

            routed = [0]

            def route_step(*instructions):
                for ins in instructions:
                    ins.then_inc(route, 1)
                    routed[0] += 1
                dve.wait_ge(route, routed[0])

            def step(ev, where):
                k, args = ev[0], ev[1:]
                if k == "split":
                    _, _, bname, ch, _ = projection(args[0])
                    bank = v_bank[c.v.n % RING]
                    n = c.v.next()
                    p, r = parts[c.split.n % 2], rest[c.split.n % 2]
                    c.split.next()
                    dve.wait_ge(high_done, c.split.at())
                    nc.vector.scalar_tensor_tensor(out=r[:, :], in0=bank[:, :], scalar=bias[bname][:, ch:ch + 1], in1=p[:, 0, :],
                                                   op0=ALU.add, op1=ALU.subtract).then_inc(v_free, n)
                    dve.wait_ge(v_free, c.v.at(RING))
                    nc.vector.tensor_copy(p[:, 1, :], r[:, :]).then_inc(middle_done, 1)
                elif k == "max":
                    kind, u, js, q, half = args
                    n = S if kind else (q + 1) * P
                    bank, inc = v_job()
                    nc.vector.reduce_max(max_raw[:, js[0]:js[-1] + 1, q, half], bank[:, 0:len(js) * n].rearrange("p (j t) -> p j t", j=len(js)),
                                         X).then_inc(v_free, inc)
                elif k == "max_parts":
                    dve.wait_ge(v_free, c.v.at(RING))
                    raw = max_raw[:, :, :, :].rearrange("p j q h -> p (j q) h")
                    if args[0]:
                        own(nc.vector.tensor_reduce(max_q[:, :], raw, X, ALU.max, negate=True))
                    else:
                        own(nc.vector.tensor_scalar(max_q[:, :], raw[:, :, 0], -1.0, None, ALU.mult))
                    own(nc.vector.tensor_copy(max_p[:, 0, :], max_q[:, :]))
                    own(nc.vector.tensor_tensor(max_r[:, :], max_q[:, :], max_p[:, 0, :], ALU.subtract))
                    own(nc.vector.tensor_copy(max_p[:, 1, :], max_r[:, :]))
                    nc.vector.tensor_tensor(max_p[:, 2, :], max_r[:, :], max_p[:, 1, :], ALU.subtract).then_inc(maxp_ready, 1)
                elif k == "max_rows":
                    bank, n = v_job()
                    c.rows.next()
                    dve.wait_ge(maxt_out, c.rows.at() * 16)
                    nc.vector.tensor_copy(max_t[:, :], bank[0:PARTS * G * QT, 0:P // 2].bitcast(BF16)).then_inc(v_free, n)
                elif k == "o_turn":
                    kind, u = args
                    if u == 0 and c.norm.n:
                        dve.wait_ge(kept, c.norm.at())
                    dve.wait_ge(v_free, c.v.at(RING))
                    bank, n = v_job()
                    heads = bank[:, :].rearrange("p (q h e) -> p q h e", q=QT, e=2 * HD)
                    own(nc.vector.reciprocal(recip[:, :, :], heads[:, :, :, HD]))
                    nc.vector.tensor_tensor(y[kind][:, :, G * HD * u:G * HD * (u + 1)].rearrange("p q (h d) -> p q h d", d=HD),
                                            heads[:, :, :, 0:HD], recip[:, :, :].unsqueeze(3).to_broadcast([P, QT, G, HD]),
                                            ALU.mult).then_inc(v_free, n)
                elif k == "out":
                    kind = args[0]
                    dve.wait_ge(*((kept, c.norm.at()) if kind else (bias_added, c.load_res.at())))
                    for pair in range(QT // 2):
                        bank, n = v_job()
                        old = x2_all[:, bass.ds(args[1](where.r) * QT + 2 * pair, 2), 0:D] if kind else xres[:, 2 * pair:2 * pair + 2, :]
                        nc.vector.tensor_tensor(y[kind][:, 2 * pair:2 * pair + 2, :], bank[:, :].rearrange("p (t d) -> p t d", d=D),
                                                old, ALU.add).then_inc(v_free, n)
                elif k == "stats":
                    kind = args[0]
                    dve.wait_ge(v_free, c.v.at(RING))
                    own(*[nc.vector.bn_stats(stats[:, q, :], y[kind][:, q, :]) for q in range(QT)])
                    dve.sem_inc(passed, 1)
                    c.out.next()
                    for q in range(QT):
                        ins = nc.vector.bn_aggr(mv[:, q, :], stats[:, q, :])
                        if q < QT - 1:
                            ins.then_inc(dve_step, 1)
                            c.step.next()
                        else:
                            ins.then_inc(mean_ready, 1)
                    dve.wait_ge(dve_step, c.step.at())
                    dve.wait_ge(mean_ready, c.out.at())
                elif k == "norm":
                    kind = args[0]
                    c.norm.next()
                    dve.wait_ge(rstd_ready, c.norm.at())
                    for q in range(QT):
                        nc.vector.tensor_scalar(y[kind][:, q, :], y[kind][:, q, :], mv[:, q, 0:1], rstd[:, q:q + 1], ALU.subtract,
                                                ALU.mult).then_inc(centred, 1)
                    if args[2]:
                        yk, dst = y[kind], x2_all[:, args[1](None) * QT:(args[1](None) + 1) * QT, 0:D]
                        gam, bet = (ln_gb[:, 2 * kind + i:2 * kind + i + 1, :].to_broadcast([P, QT, D]) for i in range(2))
                        dve.wait_ge(centred, c.norm.at() * QT)
                        nc.vector.tensor_tensor(yk[:, :, :], yk[:, :, :], gam, ALU.mult).then_inc(scaled, 1)
                        dve.wait_ge(scaled, c.norm.at())
                        nc.vector.tensor_tensor(yk[:, :, :], yk[:, :, :], bet, ALU.add).then_inc(y_ready, 1)
                        dve.wait_ge(y_ready, c.norm.at())
                        if kind:
                            nc.vector.tensor_copy(dst, yk[:, :, :]).then_inc(kept, 1)
                        else:
                            nc.vector.tensor_tensor(dst, yk[:, :, :], out_b[:, 1:2, :].to_broadcast([P, QT, D]), ALU.add).then_inc(kept, 1)
                elif k == "constants":
                    dve.wait_ge(const_made, 10)
                    nc.vector.tensor_copy(ident_b[:, :], ident[:, :]).then_inc(const_cast, 1)
                    nc.vector.memset(ones_rows(k_stack[0]), ONE_PAIR).then_inc(const_cast, 1)
                    nc.vector.memset(v_ext[0][:, :, :, HD:HD + 1], 1.0).then_inc(const_cast, 1)
                    nc.vector.memset(v_ext[0][:, :, :, HD + 1:], 0.0).then_inc(const_cast, 1)
                elif k == "rest_in":
                    dve.wait_ge(const_in, 16 * N_LOADS)
                    nc.vector.tensor_copy(expert_no[:, :], expert_i[:, :]).then_inc(const_cast, 1)
                    nc.vector.tensor_copy(x2_all[:, :, D], token_i[:, :]).then_inc(const_cast, 1)
                    dve.wait_ge(const_cast, 6)
                    nc.vector.tensor_scalar(expert_row[:, :], expert_no[:, :], float(CAP), None, ALU.mult).then_inc(const_cast, 1)
                    nc.vector.tensor_scalar(expert_end[:, :], expert_no[:, :], float(CAP), None, ALU.mult).then_inc(const_cast, 1)
                    dve.wait_ge(const_cast, CASTS)
                elif k == "cross_made":
                    dve.wait_ge(const_made, 17)
                elif k == "choose":
                    dve.wait_ge(v_free, c.v.at(RING))
                    early.choose(route_step)
                    assert routed[0] == chosen(1)
                elif k == "place":
                    bank, n = v_job()
                    last = early.place(route_step, bank)
                    last.then_inc(v_free, n)
                    dve.wait_ge(v_free, c.v.at(RING))
                    dve.sem_inc(slots_ready, 1)
                elif k == "route":
                    bank, n = v_job()
                    nc.vector.tensor_tensor(logits[:, bass.ds(args[0](where.r) * QT, QT), :], bank[:, 0:QT * E].rearrange("p (q e) -> p q e", e=E),
                                            router_b[:, :].unsqueeze(1).to_broadcast([P, QT, E]), ALU.add).then_inc(v_free, n)

            walk(dve, c, step)

        blocks.close()
        att_ctx.close()

        b1 = sb("b1", [P, E * FC])
        b2 = sb("b2", [P, E, D])
        x_row = sb("x_row", [P, D])
        x_slots = sb("x_slots", [P, SLOT_TILES + 2, ROW])
        x_col = sb("x_col", [P, DC, P])
        hidden = sb("hidden", [P, FC, P])
        y_row = sb("y_row", [P, D])
        to_f = sb("to_f", [P, 1])
        to_i = sb("to_i", [P, 1], U32)
        pad_rows = sb("pad_rows", [P, ROW])
        pad_i = sb("pad_i", [P, 1], I32)
        late = Routing(sb("route_late", [P, QT * D]), TT - QT, TT)
        tiles_i = sb("tiles_i", [P, E], I32)
        tiles_f = sb("tiles_f", [P, E])
        ones_f = sb("ones_f", [P, E])
        tiles_run = sb("tiles_run", [P, E])
        first_f = sb("first_f", [P, E])
        first_i = sb("first_i", [P, E], I32)
        end_i = sb("end_i", [P, E], I32)
        shifted = sb("shifted", [P, TT, E])
        exps = sb("exps", [P, TT, E])
        second = sb("second", [P, TT])
        exp_sum = sb("exp_sum", [P, TT])
        prob_step = sb("prob_step", [P, TT])
        gelu_warm = sb("gelu_warm", [P, 1])
        top_w = sb("top_w", [P, 2, TT])
        y_got = sb("y_got", [P, TT, 2, D])
        shift_m = sb("shift_m", [P, QT])

        moe_const = sem("moe_const")
        moe_made = sem("moe_made")
        pads_ready = sem("pads_ready")
        pads_out = sem("pads_out")
        weigh_step = sem("weigh_step")
        warmed = sem("warmed")
        shift_ready, exp_ready = sem("shift_ready"), sem("exp_ready")
        step_ready, w_ready = sem("step_ready"), sem("w_ready")
        counts_ready = sem("counts_ready")
        scattered_late = sem("scattered_late")
        x_in_slots = sem("x_in_slots")
        row_ready = sem("row_ready")
        t_full, xcol_ready = sem("t_full"), sem("xcol_ready")
        h_full, gelu_done = sem("h_full"), sem("gelu_done")
        y_full, y_evac, y_stored = sem("y_full"), sem("y_evac"), sem("y_stored")
        to_half, to_ready = sem("to_half"), sem("to_ready")
        got = [sem(f"got{n}") for n in range(TT // QT)]
        fin_step = sem("fin_step")
        var_ready, root_ready = sem("var_ready"), sem("root_ready")
        move_ready, normed = sem("move_ready"), sem("normed")
        stretched = sem("stretched")
        fin_ready, last_ready = sem("fin_ready"), sem("last_ready")
        out_done = sem("out_done")

        HB = 4
        h_bank = [a_bank[0], a_bank[1], a_bank[2], v_bank[0]]
        t_bank, y_bank = v_bank[1], v_bank[2]
        LAST = E // 2 - 1

        def expert_tiles(eng, e, body, row=None):
            first = eng.value_load(first_i[0:1, bass.ds(e, 1)], min_val=0, max_val=SLOT_TILES)
            count = eng.value_load(tiles_i[0:1, bass.ds(e, 1)], min_val=1, max_val=TOK // P)
            with eng.Fori(0, count) as i:
                g = nc.s_assert_within(eng.snap(first + i), 0, SLOT_TILES - 1,
                                       skip_runtime_bounds_check_because="all experts' tiles together are at most SLOT_TILES")
                if row is None:
                    body(g)
                else:
                    body(g, e * CAP + i * P)
            return first + count

        block = ctx.enter_context(nc.Block())

        @block.sync
        def _(sp):
            sp.dma_start(b1[:, :], a["e_b1"]).then_inc(moe_const, 16)
            sp.dma_start(b2[:, :, :], a["e_b2"].rearrange("(o e) n -> o e n", o=1).to_broadcast([P, E, D])).then_inc(moe_const, 16)
            sp.wait_ge(pads_ready, 1)
            sp.wait_ge(counts_ready, 1)
            for e in range(E):
                end = sp.value_load(end_i[0:1, e:e + 1], min_val=e * CAP, max_val=e * CAP + TOK)
                sp.dma_start(slots_dram[bass.ds(end, P), :], pad_rows[:, :]).then_inc(pads_out, 16)
            sp.wait_ge(pads_out, 16 * E)
            sp.wait_ge(counts_ready, 2)

            def load_tile(g, row):
                sp.dma_start(x_slots[:, bass.ds(g, 1), :].rearrange("p o d -> p (o d)"), slots_dram[bass.ds(row, P), :]).then_inc(x_in_slots, 16)
                sp.wait_ge(x_in_slots, g * 16 + 16)
                sp.sem_inc(passed, 1)

            for e in range(2):
                expert_tiles(sp, e, load_tile, row=True)
            with sp.Fori(0, LAST) as pair:
                for i in range(2):
                    sp.wait_ge(y_full, sp.value_load(first_i[0:1, bass.ds(2 * pair + i + 1, 1)], min_val=0, max_val=SLOT_TILES))
                    sp.sem_inc(passed, 1)
                    load_weights(sp, 2 * pair + i + 2, i)
                    after = expert_tiles(sp, 2 * pair + i + 2, load_tile, row=True)
            first = sp.value_load(first_i[0:1, E - 1:E], min_val=0, max_val=SLOT_TILES)
            count = sp.value_load(tiles_i[0:1, E - 1:E], min_val=1, max_val=TOK // P)
            for k in range(2):
                g = nc.s_assert_within(sp.snap(first + count + k), 0, SLOT_TILES + 1,
                                       skip_runtime_bounds_check_because="all experts' tiles together are at most SLOT_TILES")
                load_tile(g, 0)
            sp.wait_ge(y_stored, (first + count) * 16)
            sp.sem_inc(passed, 1)
            y_view = y_dram.rearrange("(t p) d -> p t d", p=P)
            for n in range(TT // QT):
                for k in range(2):
                    sp.dma_start(y_got[:, n * QT:(n + 1) * QT, k, :], y_view[:, k * TT + n * QT:k * TT + (n + 1) * QT, :]).then_inc(got[n], 16)
            out_view = out.rearrange("(t p) d -> p t d", p=P)
            for n in range(TT // QT):
                if n < TT // QT - 1:
                    sp.wait_ge(fin_ready, n + 1)
                else:
                    sp.wait_ge(last_ready, 1)
                sp.dma_start(out_view[:, n * QT:(n + 1) * QT, :], x2_all[:, n * QT:(n + 1) * QT, 0:D]).then_inc(out_done, 16)
            sp.wait_ge(out_done, 16 * TT // QT)

        @block.gpsimd
        def _(pool):
            nc.gpsimd.memset(pad_rows[:, :], 0.0).then_inc(moe_made, 1)
            nc.gpsimd.iota(pad_i[:, :], [[0, 1]], base=2 * TOK, channel_multiplier=1).then_inc(moe_made, 1)
            pool.wait_ge(moe_made, 2)
            nc.gpsimd.tensor_copy(pad_rows[:, D:D + 1], pad_i[:, :]).then_inc(pads_ready, 1)
            pool.wait_ge(slots_ready, 4)
            for t in range(TT - QT, TT):
                for k in range(2):
                    pool.indirect_dma_start(out=slots_dram, out_offset=bass.IndirectOffsetOnAxis(ap=late.slot_i[:, k, t - late.t0:t - late.t0 + 1], axis=0),
                                            in_=x2_all[:, t, :], in_offset=None).then_inc(scattered_late, 16)
            pool.wait_ge(scattered_late, 16 * 2 * QT)
            pool.wait_ge(counts_ready, 1)
            pool.sem_inc(counts_ready, 1)

            def tile(g):
                pool.wait_ge(to_ready, g + 1)
                pool.wait_ge(y_evac, g + 2)
                pool.sem_inc(passed, 1)
                pool.indirect_dma_start(out=y_dram, out_offset=bass.IndirectOffsetOnAxis(ap=to_i[:, 0:1], axis=0),
                                        in_=y_row[:, :], in_offset=None).then_inc(y_stored, 16)

            with pool.Fori(0, E) as e:
                expert_tiles(pool, e, tile)
            for n in range(TT // QT - 1):
                x2 = x2_all[:, n * QT:(n + 1) * QT, 0:D]
                pool.wait_ge(normed, (n + 1) * QT)
                nc.gpsimd.tensor_tensor(x2, x2, ln_gb[:, 4:5, :].to_broadcast([P, QT, D]), ALU.mult).then_inc(stretched, 1)
                pool.wait_ge(stretched, n + 1)
                nc.gpsimd.tensor_tensor(x2, x2, ln_gb[:, 5:6, :].to_broadcast([P, QT, D]), ALU.add).then_inc(fin_ready, 1)

        @block.tensor
        def _(pe):
            pe.wait_ge(route, chosen(2))
            late.rank(v_bank[0]).then_inc(rank_full, 1)

            def transpose_row(g):
                pe.wait_ge(row_ready, g + 1)
                for c in range(DC):
                    last = nc.tensor.transpose(t_bank[:, c * P:(c + 1) * P], x_row[:, c * P:(c + 1) * P], ident[:, :])
                last.then_inc(t_full, 1)

            pe.wait_ge(counts_ready, 2)
            transpose_row(0)

            def tile(i, g):
                pe.wait_ge(xcol_ready, g + 1)
                for f in range(FC):
                    pe.wait_ge(gelu_done, g * FC + f + 1)
                    for c in range(DC):
                        last = nc.tensor.matmul(h_bank[f % HB][:, 0:P], w1[i][:, c, f * P:(f + 1) * P], x_col[:, c, :],
                                                start=(c == 0), stop=(c == DC - 1))
                    last.then_inc(h_full, 1)
                transpose_row(g + 1)
                pe.wait_ge(y_evac, g + 1)
                for f in range(FC):
                    pe.wait_ge(gelu_done, g * FC + f + 1 + HB)
                    last = nc.tensor.matmul(y_bank[:, 0:D], hidden[:, f, :], w2[i][:, f, :], start=(f == 0), stop=(f == FC - 1))
                last.then_inc(y_full, 1)

            with pe.Fori(0, E // 2) as pair:
                for i in range(2):
                    pe.wait_ge(w_in[i], pair * 32 + 32)
                    expert_tiles(pe, 2 * pair + i, lambda g: tile(i, g))

        @block.scalar
        def _(sc):
            sc.sem_inc(gelu_done, HB)
            sc.wait_ge(shift_ready, 1)
            nc.scalar.activation(exps[:, :, :], shifted[:, :, :], ACT.Exp).then_inc(exp_ready, 1)
            nc.scalar.activation(second[:, :], second[:, :], ACT.Exp).then_inc(exp_ready, 1)
            sc.wait_ge(step_ready, 1)
            nc.scalar.activation(prob_step[:, :], prob_step[:, :], ACT.Exp).then_inc(w_ready, 1)
            sc.wait_ge(moe_const, 32)
            nc.scalar.activation(gelu_warm[:, :], b1[:, 0:1], ACT.Gelu).then_inc(warmed, 1)
            sc.wait_ge(counts_ready, 2)
            with sc.Fori(0, E // 2) as pair:
                for i in range(2):
                    e = 2 * pair + i

                    def tile(g):
                        for f in range(FC):
                            sc.wait_ge(h_full, g * FC + f + 1)
                            nc.scalar.activation(hidden[:, f, :], h_bank[f % HB][:, 0:P], ACT.Gelu,
                                                 bias=b1[:, bass.ds(e * FC + f, 1)]).then_inc(gelu_done, 1)

                    expert_tiles(sc, e, tile)
            for n in range(TT // QT):
                sc.wait_ge(var_ready, n + 1)
                nc.scalar.activation(rstd[:, :], rstd[:, :], ACT.Sqrt).then_inc(root_ready, 1)
                sc.wait_ge(move_ready, n + 1)
                for q in range(QT):
                    t = n * QT + q
                    nc.scalar.activation(x2_all[:, t, 0:D], x2_all[:, t, 0:D], ACT.Identity, bias=shift_m[:, q:q + 1],
                                         scale=rstd[:, q:q + 1]).then_inc(normed, 1)

        @block.vector
        def _(dve):
            dve.sem_inc(y_evac, 1)
            nc.vector.memset(ones_f[:, :], 1.0).then_inc(route, 1)
            done = [chosen(1) + placed(1) + 1]

            def step(*instructions):
                for ins in instructions:
                    ins.then_inc(route, 1)
                    done[0] += 1
                dve.wait_ge(route, done[0])

            late.choose(step)
            assert done[0] == chosen(2)
            dve.wait_ge(rank_full, 1)
            late.place(step, v_bank[0]).then_inc(slots_ready, 1)
            step(nc.vector.tensor_tensor(tiles_f[:, :], expert_end[:, :], expert_row[:, :], ALU.subtract),
                 nc.vector.tensor_copy(end_i[:, :], expert_end[:, :]))
            step(nc.vector.tensor_scalar(tiles_f[:, :], tiles_f[:, :], float(P - 1), None, ALU.add))
            step(nc.vector.tensor_copy(tiles_i[:, :], tiles_f[:, :]))
            step(nc.vector.tensor_scalar(tiles_i[:, :], tiles_i[:, :], 7, None, ALU.arith_shift_right))
            step(nc.vector.tensor_scalar(tiles_i[:, :], tiles_i[:, :], 1, None, ALU.max))
            step(nc.vector.tensor_copy(tiles_f[:, :], tiles_i[:, :]))
            step(nc.vector.tensor_tensor_scan(out=tiles_run[:, :], data0=ones_f[:, :], data1=tiles_f[:, :], initial=0.0,
                                              op0=ALU.mult, op1=ALU.add))
            step(nc.vector.tensor_tensor(first_f[:, :], tiles_run[:, :], tiles_f[:, :], ALU.subtract))
            nc.vector.tensor_copy(first_i[:, :], first_f[:, :]).then_inc(counts_ready, 1)
            step(nc.vector.tensor_tensor(shifted[:, :, :], logits[:, :, :], top_val[:, :, 0:1].to_broadcast([P, TT, E]), ALU.subtract))
            nc.vector.tensor_tensor(second[:, :], top_val[:, :, 1], top_val[:, :, 0], ALU.subtract).then_inc(shift_ready, 1)
            dve.wait_ge(exp_ready, 2)
            step(nc.vector.reduce_sum(exp_sum[:, :], exps[:, :, :], X))
            step(nc.vector.reciprocal(exp_sum[:, :], exp_sum[:, :]))
            step(nc.vector.tensor_tensor(prob_step[:, :], second[:, :], exp_sum[:, :], ALU.mult))
            nc.vector.tensor_tensor(prob_step[:, :], prob_step[:, :], exp_sum[:, :], ALU.subtract).then_inc(step_ready, 1)
            dve.wait_ge(w_ready, 1)
            step(nc.vector.tensor_scalar(top_w[:, 1, :], prob_step[:, :], 1.0, None, ALU.add))
            step(nc.vector.reciprocal(top_w[:, 0, :], top_w[:, 1, :]))
            step(nc.vector.tensor_tensor(top_w[:, 1, :], top_w[:, 0, :], prob_step[:, :], ALU.mult))
            dve.wait_ge(counts_ready, 2)

            def copy_column(g):
                dve.wait_ge(t_full, g + 1)
                nc.vector.tensor_copy(x_col[:, :, :], t_bank[:, 0:D].rearrange("p (c t) -> p c t", c=DC)).then_inc(xcol_ready, 1)

            def copy_row(g):
                dve.wait_ge(x_in_slots, g * 16 + 16)
                dve.sem_inc(passed, 1)
                nc.vector.tensor_copy(x_row[:, :], x_slots[:, bass.ds(g, 1), 0:D].rearrange("p o d -> p (o d)")).then_inc(row_ready, 1)

            copy_row(0)
            copy_column(0)
            copy_row(1)
            dve.wait_ge(moe_const, 32)
            with dve.Fori(0, E // 2) as pair:
                for i in range(2):
                    e = 2 * pair + i

                    def tile(g):
                        copy_column(g + 1)
                        copy_row(g + 2)
                        if_second, token = (x_slots[:, bass.ds(g, 1), c:c + 1].rearrange("p o d -> p (o d)") for c in (D + 1, D))
                        dve.wait_ge(y_stored, g * 16)
                        dve.sem_inc(passed, 1)
                        nc.vector.tensor_scalar(to_f[:, :], if_second, expert_no[:, bass.ds(e, 1)], float(TOK), ALU.not_equal, ALU.mult).then_inc(to_half, 1)
                        dve.wait_ge(to_half, g + 1)
                        dve.sem_inc(passed, 1)
                        nc.vector.tensor_tensor(to_i[:, :], to_f[:, :], token, ALU.add).then_inc(to_ready, 1)
                        dve.wait_ge(y_full, g + 1)
                        nc.vector.tensor_tensor(y_row[:, :], y_bank[:, 0:D], b2[:, bass.ds(e, 1), :].rearrange("p o d -> p (o d)"),
                                                ALU.add).then_inc(y_evac, 1)

                    expert_tiles(dve, e, tile)

            fin = [0]

            def fstep(*instructions):
                for ins in instructions:
                    ins.then_inc(fin_step, 1)
                    fin[0] += 1
                dve.wait_ge(fin_step, fin[0])

            def combine(n):
                ts = range(n * QT, (n + 1) * QT)
                dve.wait_ge(got[n], 32)
                for k in range(2):
                    fstep(*[nc.vector.scalar_tensor_tensor(out=x2_all[:, t, 0:D], in0=y_got[:, t, k, :], scalar=top_w[:, k, t:t + 1],
                                                           in1=x2_all[:, t, 0:D], op0=ALU.mult, op1=ALU.add) for t in ts])
                fstep(*[nc.vector.bn_stats(stats[:, t % QT, :], x2_all[:, t, 0:D]) for t in ts])
                if n:
                    dve.wait_ge(normed, n * QT)
                fstep(*[nc.vector.bn_aggr(mv[:, t % QT, :], stats[:, t % QT, :]) for t in ts])
                nc.vector.tensor_scalar(rstd[:, :], mv[:, :, 1], EPS, None, ALU.add).then_inc(var_ready, 1)

            def invert(n):
                dve.wait_ge(root_ready, n + 1)
                fstep(nc.vector.reciprocal(rstd[:, :], rstd[:, :]))
                nc.vector.scalar_tensor_tensor(out=shift_m[:, :], in0=mv[:, :, 0], scalar=-1.0, in1=rstd[:, :], op0=ALU.mult,
                                               op1=ALU.mult).then_inc(move_ready, 1)
                dve.wait_ge(move_ready, n + 1)

            def stretch(n):
                x2 = x2_all[:, n * QT:(n + 1) * QT, 0:D]
                dve.wait_ge(normed, (n + 1) * QT)
                fstep(nc.vector.tensor_tensor(x2, x2, ln_gb[:, 4:5, :].to_broadcast([P, QT, D]), ALU.mult))
                nc.vector.tensor_tensor(x2, x2, ln_gb[:, 5:6, :].to_broadcast([P, QT, D]), ALU.add).then_inc(last_ready, 1)

            for n in range(TT // QT):
                combine(n)
                invert(n)
            stretch(TT // QT - 1)


_INS = ["x", "xT", "ctxT"] + [f"{k}_{n}" for k in ("sa", "ca") for n in ("wq", "bq", "wk", "bk", "wv", "bv", "wo", "bo")] + [
    "ln1_g", "ln1_b", "ln2_g", "ln2_b", "ln3_g", "ln3_b", "router_w", "router_b", "e_w1", "e_b1", "e_w2", "e_b2"]


def kernel(**inputs):
    import numpy as _np
    import concourse.bacc as _bacc
    from concourse import mybir as _mybir
    from concourse.bass_utils import run_bass_kernel_spmd as _run

    given = {k.replace("L0_xattn_", ""): _np.asarray(v) for k, v in inputs.items()}
    x = given["x"].reshape(TOK, D)
    given["x"], given["xT"] = x, x.T
    given["ctxT"] = given.pop("ctx_1024").reshape(B * SE, D).T
    given["e_b1"] = given["e_b1"].reshape(E, FC, P).transpose(2, 0, 1).reshape(P, E * FC)
    nc = _bacc.Bacc("TRN2", target_bir_lowering=False, num_devices=1)
    arrays, aps = {}, {}
    for name in _INS:
        v = _np.ascontiguousarray(given[name])
        arrays[f"in_{name}"] = v
        aps[name] = nc.dram_tensor(f"in_{name}", v.shape, _mybir.dt.from_np(v.dtype), kind="ExternalInput").ap()
    out = nc.dram_tensor("out", (TOK, D), _mybir.dt.float32, kind="ExternalOutput").ap()
    decoder_layer(nc, aps, out)
    r = _run(nc, [arrays], core_ids=[0])
    return r.results[0]["out"].reshape(B, S, D)
```
